# Optimizing a Trainium2 kernel written in Bass

```python
import numpy as np
import jax
import jax.numpy as jnp

def _softmax(x, axis=-1):
    return jax.nn.softmax(x, axis=axis)

def _gelu(x):
    return jax.nn.gelu(x, approximate=True)

def _silu(x):
    return jax.nn.silu(x)

def _sigmoid(x):
    return jax.nn.sigmoid(x)

def _layernorm(x, axis=-1, eps=1e-05):
    m = jnp.mean(x, axis=axis, keepdims=True)
    v = jnp.var(x, axis=axis, keepdims=True)
    return (x - m) / jnp.sqrt(v + eps)

def _scatter_add(tgt, idx, src, axis=0):
    return tgt.at[idx].add(src)

def _segment_sum(src, seg, n):
    return jax.ops.segment_sum(src, seg, n)
kernel_name = 'mk_gnn_resnorm_d2_gnn_r64_87073d'

def setup_inputs(seed: int=0):
    np.random.seed(seed)
    _w = jnp.asarray

    def _rec_inputs():
        import jax
        import jax.numpy as jnp
        _gk = jax.random.key(seed)
        x = -0.0002117 + 1 * jax.random.normal(jax.random.fold_in(_gk, 1), (100000, 256), jnp.float32)
        src = jax.random.randint(jax.random.fold_in(_gk, 2), (25000,), 0, 100000, jnp.int32)
        dst = jnp.minimum((100000 * jax.random.uniform(jax.random.fold_in(_gk, 3), (25000,)) ** 2.0).astype(jnp.int32), 99999)
        _o = jnp.argsort(dst, stable=True)
        src = src[_o]
        dst = dst[_o]
        edge_weight = jax.random.uniform(jax.random.fold_in(_gk, 13), (25000,), jnp.float32, 0.0, 1)
        return (x, src, dst, edge_weight)
    x, src, dst, edge_weight = _rec_inputs()

    def _L0_gnn_setup():
        import jax, jax.numpy as jnp
        import numpy as np
        N = 100000
        D = 256
        E = 300000
        BN_EPS = 1e-05

        def _batchnorm(x, gamma, beta):
            mean = jnp.mean(x, axis=0)
            var = jnp.var(x, axis=0)
            return (x - mean) * jax.lax.rsqrt(var + BN_EPS) * gamma + beta
        key = jax.random.key(seed)
        ks = jax.random.split(key, 8)
        h = jax.random.normal(ks[0], (N, D), dtype=jnp.float32)
        edge_index = jax.random.randint(ks[1], (2, E), 0, N, dtype=jnp.int64)
        W1 = jax.random.normal(ks[2], (D, 2 * D), dtype=jnp.float32) / np.sqrt(D)
        b1 = jnp.zeros((2 * D,), dtype=jnp.float32)
        g1 = jnp.ones((2 * D,), dtype=jnp.float32)
        bt1 = jnp.zeros((2 * D,), dtype=jnp.float32)
        W2 = jax.random.normal(ks[3], (2 * D, D), dtype=jnp.float32) / np.sqrt(2 * D)
        b2 = jnp.zeros((D,), dtype=jnp.float32)
        g2 = jnp.ones((D,), dtype=jnp.float32)
        bt2 = jnp.zeros((D,), dtype=jnp.float32)
        eps_gin = jnp.zeros((), dtype=jnp.float32)
        return {'h': h, 'edge_index': edge_index, 'W1': W1, 'b1': b1, 'g1': g1, 'bt1': bt1, 'W2': W2, 'b2': b2, 'g2': g2, 'bt2': bt2, 'eps_gin': eps_gin}
    _L0_gnn_all = _L0_gnn_setup()
    _L0_gnn_in = {k: v for k, v in _L0_gnn_all.items() if k in ('W1', 'b1', 'g1', 'bt1', 'W2', 'b2', 'g2', 'bt2', 'eps_gin')}
    del _L0_gnn_all

    def _L1_gnn_setup():
        import jax, jax.numpy as jnp
        import numpy as np
        N = 100000
        E = 50000
        D_IN = 256
        D_OUT = 256
        key = jax.random.key(seed)
        k_x, k_w, k_r, k_c, k_v = jax.random.split(key, 5)
        x = jax.random.normal(k_x, (N, D_IN), dtype=jnp.float32)
        W = jax.random.normal(k_w, (D_OUT, D_IN), dtype=jnp.float32) / np.sqrt(D_IN)
        edge_row = jax.random.randint(k_r, (E,), 0, N, dtype=jnp.int32)
        edge_col = jax.random.randint(k_c, (E,), 0, N, dtype=jnp.int32)
        edge_val = jax.random.uniform(k_v, (E,), dtype=jnp.float32)
        return {'x': x, 'W': W, 'edge_row': edge_row, 'edge_col': edge_col, 'edge_val': edge_val}
    _L1_gnn_all = _L1_gnn_setup()
    _L1_gnn_in = {k: v for k, v in _L1_gnn_all.items() if k in ('W',)}
    del _L1_gnn_all
    return {'x': x, 'src': src, 'dst': dst, 'edge_weight': edge_weight, 'L0_gnn_W1': _L0_gnn_in['W1'], 'L0_gnn_b1': _L0_gnn_in['b1'], 'L0_gnn_g1': _L0_gnn_in['g1'], 'L0_gnn_bt1': _L0_gnn_in['bt1'], 'L0_gnn_W2': _L0_gnn_in['W2'], 'L0_gnn_b2': _L0_gnn_in['b2'], 'L0_gnn_g2': _L0_gnn_in['g2'], 'L0_gnn_bt2': _L0_gnn_in['bt2'], 'L0_gnn_eps_gin': _L0_gnn_in['eps_gin'], 'L1_gnn_W': _L1_gnn_in['W']}

def reference(x, src, dst, edge_weight, L0_gnn_W1, L0_gnn_b1, L0_gnn_g1, L0_gnn_bt1, L0_gnn_W2, L0_gnn_b2, L0_gnn_g2, L0_gnn_bt2, L0_gnn_eps_gin, L1_gnn_W):
    import jax
    import jax.numpy as jnp

    def _L0_gnn_ref(h, edge_index, W1, b1, g1, bt1, W2, b2, g2, bt2, eps_gin):
        import jax, jax.numpy as jnp
        import numpy as np
        N = 100000
        D = 256
        E = 300000
        BN_EPS = 1e-05

        def _batchnorm(x, gamma, beta):
            mean = jnp.mean(x, axis=0)
            var = jnp.var(x, axis=0)
            return (x - mean) * jax.lax.rsqrt(var + BN_EPS) * gamma + beta
        src, dst = (edge_index[0], edge_index[1])
        agg = jax.ops.segment_sum(h[src], dst, num_segments=N)
        z = (1.0 + eps_gin) * h + agg
        t = jnp.dot(z, W1) + b1
        t = jax.nn.relu(_batchnorm(t, g1, bt1))
        conv_out = jnp.dot(t, W2) + b2
        out = jax.nn.relu(_batchnorm(conv_out + h, g2, bt2))
        return out

    def _L1_gnn_ref(x, W, edge_row, edge_col, edge_val):
        import jax, jax.numpy as jnp
        import numpy as np
        N = 100000
        E = 50000
        D_IN = 256
        D_OUT = 256
        support = jnp.einsum('nd,od->no', x.astype(jnp.float32), W.astype(jnp.float32))
        gathered = edge_val.astype(jnp.float32)[:, None] * support[edge_col]
        out = jax.ops.segment_sum(gathered, edge_row, num_segments=N)
        return out
    edge_index = jnp.stack([src, dst])
    x = _layernorm(x + _L0_gnn_ref(x, edge_index, L0_gnn_W1, L0_gnn_b1, L0_gnn_g1, L0_gnn_bt1, L0_gnn_W2, L0_gnn_b2, L0_gnn_g2, L0_gnn_bt2, L0_gnn_eps_gin), axis=-1)
    x = _layernorm(x + _L1_gnn_ref(x, L1_gnn_W, src, dst, edge_weight), axis=-1)
    return x

_drawn_inputs = setup_inputs


def setup_inputs(seed=0):
    import zlib

    import numpy as np

    out = dict(_drawn_inputs(seed))
    spreads = {'L0_gnn_b1': (0.0, 0.8),
     'L0_gnn_g1': (1.0, 0.2),
     'L0_gnn_bt1': (0.0, 0.383),
     'L0_gnn_b2': (0.0, 0.8),
     'L0_gnn_g2': (1.0, 0.2),
     'L0_gnn_bt2': (0.0, 0.1)}
    factors = {}
    for name, (base, spread) in spreads.items():
        noise = np.random.default_rng([zlib.crc32(name.encode()), seed]).standard_normal(out[name].shape)
        drawn = base * np.exp(spread * noise) if base else spread * noise
        out[name] = jnp.asarray(drawn.astype(out[name].dtype))
    for name, factor in factors.items():
        out[name] = (out[name] * factor).astype(out[name].dtype)
    return out
```

```python
import concourse.bass as bass
from concourse import mybir
from contextlib import ExitStack

f32 = mybir.dt.float32
f16 = mybir.dt.float16
i32 = mybir.dt.int32
ALU = mybir.AluOpType
ACT = mybir.ActivationFunctionType
IOA = bass.IndirectOffsetOnAxis

EPS = 1e-5
WS = 64.0
K = 4
G = 4
RING = 4


class Shapes:

    def __init__(s, n, d, h, e):
        s.N, s.D, s.H, s.E = n, d, h, e
        s.KD, s.KH = d // 128, h // 128
        s.BR = 128 * G
        s.NB = n // s.BR
        s.TP = (n - s.NB * s.BR) // G
        assert s.NB * s.BR + s.TP * G == n and 0 < s.TP < 128
        s.C = -(-e // (128 * K)) * K
        s.NG = s.C // K
        s.ZR = 8
        s.NZ = -(-(n + 1 + K * 128) // (128 * s.ZR))
        s.T = s.NZ * 128 * s.ZR


def over(eng, lo, hi, unroll, step):
    first = max(lo, 2 * unroll)
    n = (hi - first) // unroll
    if n < 2:
        first, n = hi, 0
    for b in range(lo, first):
        step(b, b % unroll, b // unroll)
    if n:
        with eng.Fori(0, n) as i:
            for s in range(unroll):
                b = first + s
                step(i * unroll + b, b % unroll, i + b // unroll)
    for b in range(first + n * unroll, hi):
        step(b, b % unroll, b // unroll)


def after(eng, sem, value):
    if not isinstance(value, int) or value > 0:
        eng.wait_ge(sem, value)


def row_blocks(ap, sh):
    full = ap[0:sh.NB * sh.BR, :].rearrange("(b p g) d -> b p (g d)", p=128, g=G)
    tail = ap[sh.NB * sh.BR:sh.N, :].rearrange("(p g) d -> p (g d)", g=G)
    return full, tail


def block_of(views, b, P):
    full, tail = views
    return full[bass.ds(b, 1)].rearrange("a p d -> (a p) d") if P == 128 else tail


def gnn(nc, x, src, dst, ew, W1, b1, g1, bt1, W2, b2, g2, bt2, eps_gin, LW, out):
    sh = Shapes(x.shape[0], x.shape[1], W1.shape[1], src.shape[0])
    N, D, H, E, C, NG, NB, TP = sh.N, sh.D, sh.H, sh.E, sh.C, sh.NG, sh.NB, sh.TP
    KD, KH = sh.KD, sh.KH
    agg = nc.dram_tensor("agg", (sh.T, D), f32).ap()
    agg2 = nc.dram_tensor("agg2", (sh.T, D), f32).ap()
    ubuf = nc.dram_tensor("ubuf", (N, D), f32).ap()
    agg_z = agg.rearrange("(z p r) d -> z p (r d)", p=128, r=sh.ZR)
    agg2_z = agg2.rearrange("(z p r) d -> z p (r d)", p=128, r=sh.ZR)
    xv, aggv, agg2v, uv, outv = (row_blocks(t, sh) for t in (x, agg, agg2, ubuf, out))
    whole = ExitStack()
    with whole:
        def sb(name, shape, dt, scope=whole):
            return scope.enter_context(nc.sbuf_tensor(name, shape, dt))

        def ps(name, cols, scope):
            return scope.enter_context(nc.psum_tensor(name, [128, cols], f32))

        def sem(name):
            return whole.enter_context(nc.semaphore(name))

        ident = sb("ident", [128, 128], f32)
        ones = sb("ones", [128, 128], f32)
        ones16 = sb("ones16", [128, 1], f16)
        zeros16 = sb("zeros16", [128, 512], f16)
        zrows = sb("zrows", [128, sh.ZR * D], f32)
        w1f = sb("w1f", [128, KD, H], f32)
        w1h = sb("w1h", [128, KD, H], f16)
        w1l = sb("w1l", [128, KD, H], f16)
        w2h = sb("w2h", [128, KH, D], f16)
        w2l = sb("w2l", [128, KH, D], f16)
        lwt = sb("lwt", [128, KD, D], f32)
        cc = sb("cc", [128, 1], f32)
        b1c = sb("b1c", [128, 3, KH], f32)
        scale1 = sb("scale1", [128, KH], f32)
        bias1 = sb("bias1", [128, KH], f32)
        rows2 = sb("rows2", [128, 3, D], f32)
        scale2 = sb("scale2", [128, D], f32)
        bias2 = sb("bias2", [128, D], f32)
        gsrc = sb("gsrc", [128, C], i32)
        gdst = sb("gdst", [128, C], i32)
        key_i = sb("key_i", [128, 2, C], i32)
        kdst = sb("kdst", [128, C], f32)
        ksrc = sb("ksrc", [128, C], f32)
        wgt = sb("wgt", [128, C], f32)
        picked = [sb(f"picked{s}", [128, K], i32) for s in range(2)]
        halves = sb("halves", [128, K], f32)
        before = sb("before", [128, K, K * 128], f32)
        spare = sb("spare", [128, K], f32)
        spare_i = sb("spare_i", [128, K], i32)

        ph = ExitStack()
        w2f = sb("w2f", [128, KH, D], f32, ph)
        lwf = sb("lwf", [128, KD, D], f32, ph)
        rows_x = [sb(f"rows_x{s}", [128, K, D], f32, ph) for s in range(2)]
        sums = [sb(f"sums{s}", [128, K, D], f32, ph) for s in range(2)]
        sel = [sb(f"sel{s}", [128, K, K * 128], f32, ph) for s in range(2)]
        diag = sb("diag", [128, K, 128], f32, ph)
        junk = sb("junk", [128, K, K * 128], f16, ph)
        cnt = sb("cnt", [128, 3, K], f32, ph)
        target = [sb(f"target{s}", [128, K], i32, ph) for s in range(2)]
        keyrow = ps("keyrow", K * 128, ph)
        comb = ps("comb", K * D, ph)
        lwp = ps("lwp", 512, ph)

        pool_passed, dve_passed = sem("pool_passed"), sem("dve_passed")
        const_loaded = sem("const_loaded")
        idx_cleared = sem("idx_cleared")
        idx_loaded = sem("idx_loaded")
        consts_made = sem("consts_made")
        pool_consts = sem("pool_consts")
        dve_c = sem("dve_c")
        lw_turned = sem("lw_turned")
        table_zeroed = sem("table_zeroed")
        x_gathered = [sem(f"x_gathered{s}") for s in range(2)]
        x_picked = sem("x_picked")
        keys_spread = sem("keys_spread")
        keyrow_ready = sem("keyrow_ready")
        sel_ready = sem("sel_ready")
        cnt_ready = sem("cnt_ready")
        target_ready = sem("target_ready")
        comb_ready = sem("comb_ready")
        sums_ready = sem("sums_ready")
        sums_added = [sem(f"sums_added{s}") for s in range(2)]

        full_p, rest = E // C, E % C

        def load_edges(eng, to, ap):
            eng.dma_start(to[0:full_p, :], ap[0:full_p * C].rearrange("(p c) -> p c", c=C)).then_inc(idx_loaded, 16)
            n = 1
            if rest:
                eng.dma_start(to[full_p:full_p + 1, 0:rest],
                              ap[full_p * C:E].rearrange("(a c) -> a c", a=1)).then_inc(idx_loaded, 16)
                n = 2
            return n

        IDX_LOADS = 5 * (2 if rest else 1)

        def select_edges(dve, g, slot, keys, ready):
            spread, row_ready, sel_sem, cnt_sem, target_sem, sel_t, key_row, target_t, tmp, jnk, dg = ready
            kcols = keys[:, bass.ds(g * K, K)]
            dve.wait_ge(row_ready, g + 1)
            for k in range(K):
                last = nc.vector.tensor_scalar(sel_t[slot][:, k, :], key_row[:, :], keys[:, bass.ds(g * K + k, 1)], None,
                                               ALU.is_equal)
            for k in range(K):
                last = nc.vector.scalar_tensor_tensor(out=jnk[:, k, :], in0=key_row[:, :], scalar=keys[:, bass.ds(g * K + k, 1)],
                                                      in1=before[:, k, :], op0=ALU.is_equal, op1=ALU.mult,
                                                      accum_out=tmp[:, 0, k:k + 1])
            last = nc.vector.tensor_tensor(tmp[:, 1, :], spare[:, :], kcols, ALU.subtract)
            last.then_inc(sel_sem, 1)
            dve.wait_ge(sel_sem, g + 1)
            nc.vector.scalar_tensor_tensor(out=tmp[:, 2, :], in0=tmp[:, 0, :], scalar=1.0, in1=tmp[:, 1, :],
                                           op0=ALU.min, op1=ALU.mult).then_inc(cnt_sem, 1)
            dve.wait_ge(cnt_sem, g + 1)
            nc.vector.tensor_tensor(target_t[slot][:, :], tmp[:, 2, :], kcols, ALU.add).then_inc(target_sem, 1)

        def spread_keys(g, keys, dg, spread):
            nc.vector.tensor_tensor(dg[:, :, :], ident[:, :].unsqueeze(1).to_broadcast([128, K, 128]),
                                    keys[:, bass.ds(g * K, K)].unsqueeze(2).to_broadcast([128, K, 128]),
                                    ALU.mult).then_inc(spread, 1)

        with ph, nc.Block() as block:
            @block.sync
            def _(sp):
                sp.wait_ge(consts_made, 1)
                zs = [0]

                def zero(z, slot, use):
                    sp.dma_start(agg_z[bass.ds(z, 1)].rearrange("a p r -> (a p) r"), zrows[:, :]).then_inc(table_zeroed, 16)

                over(sp, 0, sh.NZ, RING, zero)
                sp.wait_ge(table_zeroed, 16 * sh.NZ)

            @block.scalar
            def _(act):
                act.dma_start(w1f[:, :, :], W1.rearrange("(k p) n -> p k n", p=128)).then_inc(const_loaded, 16)
                act.dma_start(w2f[:, :, :], W2.rearrange("(k p) n -> p k n", p=128)).then_inc(const_loaded, 16)
                act.dma_start(lwf[:, :, :], LW.rearrange("(k p) n -> p k n", p=128)).then_inc(const_loaded, 16)
                act.dma_start(cc[:, :], eps_gin.rearrange("(a n) -> a n", a=1).to_broadcast([128, 1])).then_inc(const_loaded, 16)
                for j, v in enumerate((b1, g1, bt1)):
                    act.dma_start(b1c[:, j, :], v.rearrange("(m p) -> p m", p=128),
                                  allow_slow_non_contiguous=True).then_inc(const_loaded, 16)
                for j, v in enumerate((b2, g2, bt2)):
                    act.dma_start(rows2[:, j, :], v.rearrange("(a n) -> a n", a=1).to_broadcast([128, D])).then_inc(const_loaded, 16)
                act.wait_ge(idx_cleared, 5)
                load_edges(act, gsrc, src)
                load_edges(act, gdst, dst)
                load_edges(act, key_i[:, 0, :], dst)
                load_edges(act, key_i[:, 1, :], src)
                load_edges(act, wgt, ew)

                def evacuate(g, slot, use):
                    act.wait_ge(comb_ready, g + 1)
                    after(act, sums_added[slot], use * (16 * K))
                    nc.scalar.copy(sums[slot][:, :, :], comb[:, :].rearrange("p (k d) -> p k d", k=K)).then_inc(sums_ready, 1)

                over(act, 0, NG, 2, evacuate)

            @block.gpsimd
            def _(pool):
                nc.gpsimd.memset(ident[:, :], 0.0).then_inc(pool_consts, 1)
                nc.gpsimd.memset(ones[:, :], 1.0)
                nc.gpsimd.memset(before[:, :, :], 1.0).then_inc(pool_consts, 1)
                pool.wait_ge(pool_consts, 2)
                nc.gpsimd.affine_select(out=ident[:, :], in_=ident[:, :], compare_op=ALU.not_equal, fill=1.0,
                                        base=0, pattern=[[-1, 128]], channel_multiplier=1)
                for k in range(K):
                    nc.gpsimd.affine_select(out=before[:, k, :], in_=before[:, k, :], compare_op=ALU.is_gt, fill=0.0,
                                            base=128 * k, pattern=[[-1, K * 128]], channel_multiplier=1)
                nc.gpsimd.iota(spare_i[:, :], pattern=[[128, K]], base=N + 1, channel_multiplier=1).then_inc(pool_consts, 1)
                pool.wait_ge(idx_loaded, 16 * IDX_LOADS)

                def gather(g, slot, use):
                    after(pool, comb_ready, g - 1)
                    pool.sem_inc(pool_passed, 1)
                    nc.gpsimd.tensor_copy(picked[slot][:, :], gsrc[:, bass.ds(g * K, K)]).then_inc(x_picked, 1)
                    pool.wait_ge(x_picked, g + 1)
                    pool.sem_inc(pool_passed, 1)
                    for k in range(K):
                        pool.indirect_dma_start(rows_x[slot][:, k, :], None, x,
                                                IOA(ap=picked[slot][:, k:k + 1], axis=0)).then_inc(x_gathered[slot], 16)

                def add(g, slot, use):
                    pool.wait_ge(sums_ready, g + 1)
                    pool.wait_ge(target_ready, g + 1)
                    pool.wait_ge(table_zeroed, 16 * sh.NZ)
                    after(pool, sums_added[1 - slot], (use + slot) * (16 * K))
                    pool.sem_inc(pool_passed, 1)
                    for k in range(K):
                        pool.indirect_dma_start(agg, IOA(ap=target[slot][:, k:k + 1], axis=0), sums[slot][:, k, :], None,
                                                compute_op=ALU.add).then_inc(sums_added[slot], 16)

                def both(g, slot, use):
                    gather(g + 1, 1 - slot, use + slot)
                    add(g, slot, use)

                gather(0, 0, 0)
                both(0, 0, 0)
                over(pool, 1, NG - 1, 2, both)
                add(NG - 1, (NG - 1) % 2, (NG - 1) // 2)
                last = NG - 1
                pool.wait_ge(sums_added[last % 2], (last // 2 + 1) * 16 * K)
                pool.wait_ge(sums_added[1 - last % 2], ((last - 1) // 2 + 1) * 16 * K)

            @block.vector
            def _(dve):
                nc.vector.memset(zrows[:, :], 0.0).then_inc(consts_made, 1)
                nc.vector.memset(zeros16[:, :], 0.0)
                nc.vector.memset(ones16[:, :], 1.0)
                nc.vector.memset(gsrc[:, :], 0).then_inc(idx_cleared, 1)
                nc.vector.memset(gdst[:, :], 0).then_inc(idx_cleared, 1)
                nc.vector.memset(key_i[:, 0, :], N).then_inc(idx_cleared, 1)
                nc.vector.memset(key_i[:, 1, :], N).then_inc(idx_cleared, 1)
                nc.vector.memset(wgt[:, :], 0.0).then_inc(idx_cleared, 1)
                dve.wait_ge(const_loaded, 160)
                nc.vector.tensor_scalar(cc[:, :], cc[:, :], 1.0, None, ALU.add)
                for full, hi, lo in ((w1f, w1h, w1l), (w2f, w2h, w2l)):
                    nc.vector.tensor_scalar(hi[:, :, :], full[:, :, :], WS, None, ALU.mult).then_inc(dve_c, 1)
                dve.wait_ge(dve_c, 2)
                for full, hi, lo in ((w1f, w1h, w1l), (w2f, w2h, w2l)):
                    nc.vector.scalar_tensor_tensor(out=lo[:, :, :], in0=full[:, :, :], scalar=WS, in1=hi[:, :, :],
                                                   op0=ALU.mult, op1=ALU.subtract)
                dve.wait_ge(lw_turned, 1)
                nc.vector.tensor_copy(lwt[:, :, :], lwp[:, :].rearrange("p (k n) -> p k n", k=KD))
                dve.wait_ge(pool_consts, 3)
                dve.wait_ge(idx_loaded, 16 * IDX_LOADS)
                nc.vector.tensor_copy(spare[:, :], spare_i[:, :])
                nc.vector.tensor_copy(kdst[:, :], key_i[:, 0, :])
                nc.vector.tensor_copy(ksrc[:, :], key_i[:, 1, :]).then_inc(dve_c, 1)
                dve.wait_ge(dve_c, 3)
                names = (keys_spread, keyrow_ready, sel_ready, cnt_ready, target_ready, sel, keyrow, target, cnt, junk, diag)
                spread_keys(0, kdst, diag, keys_spread)

                def group(g, slot, use):
                    dve.wait_ge(keyrow_ready, g + 1)
                    spread_keys(g + 1, kdst, diag, keys_spread)
                    after(dve, comb_ready, g - 1)
                    after(dve, sums_added[slot], use * (16 * K))
                    select_edges(dve, g, slot, kdst, names)

                group(0, 0, 0)
                over(dve, 1, NG - 1, 2, group)
                last = NG - 1
                dve.wait_ge(comb_ready, last - 1)
                dve.wait_ge(sums_added[last % 2], (last // 2) * 16 * K)
                select_edges(dve, last, last % 2, kdst, names)

            @block.tensor
            def _(pe):
                pe.wait_ge(pool_consts, 3)
                pe.wait_ge(const_loaded, 160)
                for i in range(KD):
                    for j in range(KD):
                        turned = nc.tensor.transpose(lwp[:, i * D + j * 128:i * D + j * 128 + 128],
                                                     lwf[:, j, i * 128:(i + 1) * 128], ident[:, :])
                turned.then_inc(lw_turned, 1)

                def spread(g):
                    pe.wait_ge(keys_spread, g + 1)
                    nc.tensor.matmul(keyrow[:, :], ones[:, :], diag[:, :, :].rearrange("p k j -> p (k j)"),
                                     start=True, stop=True).then_inc(keyrow_ready, 1)

                def combine(g, slot, use):
                    pe.wait_ge(x_gathered[slot], (use + 1) * (16 * K))
                    pe.wait_ge(sel_ready, g + 1)
                    after(pe, sums_ready, g)
                    for k in range(K):
                        for j in range(K):
                            last = nc.tensor.matmul(comb[:, k * D:(k + 1) * D], sel[slot][:, j, k * 128:(k + 1) * 128],
                                                    rows_x[slot][:, j, :], start=(j == 0), stop=(j == K - 1))
                    last.then_inc(comb_ready, 1)

                def group(g, slot, use):
                    after(pe, target_ready, g)
                    spread(g)
                    combine(g - 1, 1 - slot, use - 1 + slot)

                spread(0)
                over(pe, 1, NG, 2, group)
                last = NG - 1
                combine(last, last % 2, last // 2)

        ph = ExitStack()
        xb = [sb(f"xb{s}", [128, G, D], f32, ph) for s in range(RING)]
        ab = [sb(f"ab{s}", [128, G, D], f32, ph) for s in range(RING)]
        zb = [sb(f"zb{s}", [128, G, D], f32, ph) for s in range(RING)]
        zz = [sb(f"zz{s}", [128, G, 2 * D], f16, ph) for s in range(RING)]
        gram = sb("gram", [128, KD, D], f32, ph)
        mcol = sb("mcol", [128, 4], f32, ph)
        mrow = sb("mrow", [1, D], f32, ph)
        prod = sb("prod", [128, KD, H], f32, ph)
        st1 = sb("st1", [128, 6, KH], f32, ph)
        pg = [ps(f"pg{h}", 512, ph) for h in range(KD)]
        psum_z = ps("psum_z", 512, ph)
        pv = [ps(f"pv{h}", 512, ph) for h in range(KD)]
        pm = ps("pm", 512, ph)
        pst = ps("pst", 512, ph)

        xa_loaded = [sem(f"xa_loaded{s}") for s in range(RING)]
        z_ready = sem("z_ready")
        hi_ready = sem("hi_ready")
        lo_ready = sem("lo_ready")
        z_used = sem("z_used")
        gram_done = sem("gram_done")
        s1 = sem("s1_step")
        p1 = sem("p1_step")
        a1 = sem("a1_step")

        def all_blocks(eng, step, lo=0):
            over(eng, lo, NB, RING, lambda b, s, u: step(b, s, u, 128))
            step(NB, NB % RING, NB // RING, TP)

        with ph, nc.Block() as block:
            @block.sync
            def _(sp):
                def load(b, s, u, P):
                    after(sp, z_ready, b - RING + 1)
                    sp.dma_start(xb[s][0:P].rearrange("p g d -> p (g d)"), block_of(xv, b, P)).then_inc(xa_loaded[s], 16)
                    sp.dma_start(ab[s][0:P].rearrange("p g d -> p (g d)"), block_of(aggv, b, P)).then_inc(xa_loaded[s], 16)
                for s in range(RING):
                    load(s, s, 0, 128)
                all_blocks(sp, load, RING)

            @block.vector
            def _(dve):
                def z_block(b, s, u, P):
                    dve.wait_ge(xa_loaded[s], (u + 1) * 32)
                    after(dve, z_used, b - RING + 1)
                    nc.vector.scalar_tensor_tensor(out=zb[s][0:P], in0=xb[s][0:P], scalar=cc[0:P, :], in1=ab[s][0:P],
                                                   op0=ALU.mult, op1=ALU.add).then_inc(z_ready, 1)

                def low(b, s, u, P):
                    dve.wait_ge(hi_ready, b + 1)
                    nc.vector.tensor_tensor(zz[s][0:P, :, D:2 * D], zb[s][0:P], zz[s][0:P, :, 0:D], ALU.subtract).then_inc(lo_ready, 1)

                def step(b, s, u, P):
                    z_block(b, s, u, P)
                    low(b - 1, (s - 1) % RING, None, 128)
                for s in range(RING):
                    z_block(s, s, 0, 128)
                    if s:
                        low(s - 1, s - 1, 0, 128)
                all_blocks(dve, step, RING)
                low(NB, NB % RING, None, TP)

                n = [0]

                def mark(ins):
                    n[0] += 1
                    ins.then_inc(s1, 1)
                    dve.wait_ge(s1, n[0])
                dve.wait_ge(gram_done, 1)
                mark(nc.vector.tensor_copy(mcol[:, 0:2], psum_z[:, 0:2]))
                mark(nc.vector.scalar_tensor_tensor(out=mcol[:, 0:2], in0=psum_z[:, 2:4], scalar=1.0, in1=mcol[:, 0:2],
                                                    op0=ALU.mult, op1=ALU.add))
                mark(nc.vector.tensor_scalar(mcol[:, 0:2], mcol[:, 0:2], 1.0 / N, None, ALU.mult))
                dve.wait_ge(p1, 1)
                mark(nc.vector.tensor_copy(mrow[0:1, :], pm[0:1, 0:D]))
                mark(nc.vector.tensor_copy(prod[:, 0, :], pg[0][:, :]))
                mark(nc.vector.tensor_copy(prod[:, 1, 0:D + 128], pg[1][:, 0:D + 128]))
                mark(nc.vector.scalar_tensor_tensor(out=gram[:, 0, :], in0=prod[:, 0, D:2 * D], scalar=2.0,
                                                    in1=prod[:, 0, 0:D], op0=ALU.mult, op1=ALU.add))
                mark(nc.vector.tensor_tensor(gram[:, 0, 128:D], gram[:, 0, 128:D], prod[:, 0, 128:D], ALU.add))
                mark(nc.vector.tensor_scalar(gram[:, 1, 0:128], prod[:, 1, 128:256], 2.0, None, ALU.mult))
                mark(nc.vector.scalar_tensor_tensor(out=gram[:, 1, 128:D], in0=prod[:, 1, 256:384], scalar=2.0,
                                                    in1=prod[:, 1, 0:128], op0=ALU.mult, op1=ALU.add))
                dve.wait_ge(p1, 2)
                mark(nc.vector.tensor_scalar(gram[:, :, :], gram[:, :, :], 1.0 / N, None, ALU.mult))
                mark(nc.vector.tensor_tensor(gram[:, 0, 0:128], gram[:, 0, 0:128], pm[:, 0:128], ALU.subtract))
                mark(nc.vector.scalar_tensor_tensor(out=gram[:, 0, 128:D], in0=pm[:, 128:D], scalar=-2.0,
                                                    in1=gram[:, 0, 128:D], op0=ALU.mult, op1=ALU.add))
                mark(nc.vector.tensor_tensor(gram[:, 1, 128:D], gram[:, 1, 128:D], pm[:, D + 128:2 * D], ALU.subtract))
                nc.vector.memset(st1[:, 5, :], 0.0).then_inc(a1, 1)
                dve.wait_ge(p1, 3)
                mark(nc.vector.tensor_tensor(prod[:, 0, :], pv[0][:, :], w1f[:, 0, :], ALU.mult))
                mark(nc.vector.tensor_tensor(prod[:, 1, :], pv[1][:, :], w1f[:, 1, :], ALU.mult))
                nc.vector.memset(st1[:, 5, :], 0.0).then_inc(a1, 1)
                dve.wait_ge(p1, 4)
                mark(nc.vector.tensor_scalar(st1[:, 0, :], pst[:, 0:KH], EPS, None, ALU.add))
                mark(nc.vector.tensor_tensor(st1[:, 1, :], pst[:, KH:2 * KH], b1c[:, 0, :], ALU.add))
                nc.vector.memset(st1[:, 5, :], 0.0).then_inc(a1, 1)
                dve.wait_ge(p1, 5)
                mark(nc.vector.reciprocal(st1[:, 3, :], st1[:, 2, :]))
                mark(nc.vector.tensor_tensor(st1[:, 3, :], st1[:, 3, :], b1c[:, 1, :], ALU.mult))
                mark(nc.vector.tensor_scalar(scale1[:, :], st1[:, 3, :], 1.0 / WS, None, ALU.mult))
                mark(nc.vector.tensor_tensor(st1[:, 4, :], b1c[:, 0, :], st1[:, 1, :], ALU.subtract))
                mark(nc.vector.tensor_tensor(st1[:, 4, :], st1[:, 4, :], st1[:, 3, :], ALU.mult))
                mark(nc.vector.tensor_tensor(bias1[:, :], st1[:, 4, :], b1c[:, 2, :], ALU.add))

            @block.scalar
            def _(act):
                def high(b, s, u, P):
                    act.wait_ge(z_ready, b + 1)
                    nc.scalar.copy(zz[s][0:P, :, 0:D], zb[s][0:P]).then_inc(hi_ready, 1)
                all_blocks(act, high)
                act.wait_ge(a1, 3)
                nc.scalar.activation(st1[:, 2, :], st1[:, 0, :], ACT.Sqrt).then_inc(p1, 1)

            @block.tensor
            def _(pe):
                for bank in (pg[0], pg[1], psum_z):
                    nc.tensor.matmul(bank[:, :], zeros16[:, 0:128], zeros16[:, :], start=True, stop=False)

                def gram_step(b, s, u, P):
                    pe.wait_ge(lo_ready, b + 1)
                    for g in range(G):
                        for h in range(KD):
                            w = zz[s][0:P, g, h * 128:(h + 1) * 128]
                            m = zz[s][0:P, g, h * 128:2 * D]
                            nc.tensor.matmul(pg[h][:, 0:2 * D - h * 128], w, m, start=False, stop=False, skip_group_check=True)
                            nc.tensor.matmul(psum_z[:, h:h + 1], w, ones16[0:P, :], start=False, stop=False, skip_group_check=True)
                        for h in range(KD):
                            last = nc.tensor.matmul(psum_z[:, 2 + h:3 + h], zz[s][0:P, g, D + h * 128:D + (h + 1) * 128],
                                                    ones16[0:P, :], start=False, stop=False, skip_group_check=True)
                    last.then_inc(z_used, 1)
                all_blocks(pe, gram_step)
                for bank in (pg[0], pg[1], psum_z):
                    last = nc.tensor.matmul(bank[:, :], zeros16[:, 0:128], zeros16[:, :], start=False, stop=True)
                last.then_inc(gram_done, 1)
                pe.wait_ge(s1, 3)
                for h in range(KD):
                    last = nc.tensor.transpose(pm[0:1, h * 128:(h + 1) * 128], mcol[:, h:h + 1], ident[:, :])
                last.then_inc(p1, 1)
                pe.wait_ge(s1, 4)
                for h in range(KD):
                    last = nc.tensor.matmul(pm[:, h * D:(h + 1) * D], mrow[0:1, h * 128:(h + 1) * 128], mrow[0:1, :], start=True, stop=True)
                last.then_inc(p1, 1)
                pe.wait_ge(a1, 1)
                for h in range(KD):
                    for k in range(KD):
                        last = nc.tensor.matmul(pv[h][:, :], gram[:, k, h * 128:(h + 1) * 128], w1f[:, k, :],
                                                start=(k == 0), stop=(k == KD - 1))
                last.then_inc(p1, 1)
                pe.wait_ge(a1, 2)
                for m in range(KH):
                    for k in range(KD):
                        nc.tensor.matmul(pst[:, m:m + 1], prod[:, k, m * 128:(m + 1) * 128], ones[:, 0:1], start=(k == 0), stop=(k == KD - 1))
                    for k in range(KD):
                        last = nc.tensor.matmul(pst[:, KH + m:KH + m + 1], w1f[:, k, m * 128:(m + 1) * 128], mcol[:, k:k + 1],
                                                start=(k == 0), stop=(k == KD - 1))
                last.then_inc(p1, 1)

        ph = ExitStack()
        xb = [sb(f"xc{s}", [128, G, D], f32, ph) for s in range(RING)]
        ab = [sb(f"ac{s}", [128, G, D], f32, ph) for s in range(2)]
        zb = sb("zc", [128, G, D], f32, ph)
        zh = sb("zh", [128, KD, 512], f16, ph)
        zl = sb("zl", [128, KD, 512], f16, ph)
        tf = sb("tf", [128, KH, 512], f32, ph)
        th = [sb(f"th{s}", [128, KH, 512], f16, ph) for s in range(2)]
        tl = [sb(f"tl{s}", [128, KH, 512], f16, ph) for s in range(2)]
        ub = [sb(f"ub{s}", [128, G, D], f32, ph) for s in range(2)]
        sq = sb("sq", [128, G, D], f32, ph)
        usum = sb("usum", [128, G, D], f32, ph)
        qsum = sb("qsum", [128, G, D], f32, ph)
        st2 = sb("st2", [128, 4, D], f32, ph)
        pzt = ps("pzt", KD * 512, ph)
        pt = [ps(f"pt{m}", 512, ph) for m in range(KH)]
        pc = ps("pc", G * D, ph)

        xc_loaded = [sem(f"xc_loaded{s}") for s in range(RING)]
        ac_loaded = [sem(f"ac_loaded{s}") for s in range(2)]
        zc_ready = sem("zc_ready")
        z_turned = sem("z_turned")
        zh_ready = sem("zh_ready")
        zl_ready = sem("zl_ready")
        t_ready = sem("t_ready")
        relu_done = sem("relu_done")
        th_ready = sem("th_ready")
        tl_ready = sem("tl_ready")
        conv_ready = sem("conv_ready")
        u_ready = sem("u_ready")
        sq_ready = sem("sq_ready")
        usum_done = sem("usum_done")
        u_summed = sem("u_summed")
        u_stored = [sem(f"u_stored{s}") for s in range(2)]
        table2_zeroed = sem("table2_zeroed")
        s2 = sem("s2_step")
        p2 = sem("p2_step")

        with ph, nc.Block() as block:
            @block.sync
            def _(sp):
                def load(b, s, u, P):
                    prev = b - RING + 1
                    after(sp, u_ready, prev)
                    sp.dma_start(xb[s][0:P].rearrange("p g d -> p (g d)"), block_of(xv, b, P)).then_inc(xc_loaded[s], 16)
                    after(sp, zc_ready, b - 1)
                    sp.dma_start(ab[s % 2][0:P].rearrange("p g d -> p (g d)"), block_of(aggv, b, P)).then_inc(ac_loaded[s % 2], 16)
                for s in range(RING):
                    load(s, s, 0, 128)
                per = -(-sh.NZ // ((NB - RING) // RING)) if NB // RING > 2 else sh.NZ
                zeroed = [0]

                def zero(z):
                    sp.dma_start(agg2_z[bass.ds(z, 1)].rearrange("a p r -> (a p) r"), zrows[:, :]).then_inc(table2_zeroed, 16)
                n = (NB - RING) // RING
                per = sh.NZ // n
                with sp.Fori(0, n) as i:
                    for s in range(RING):
                        load(i * RING + (RING + s), s, i + 1, 128)
                    for z in range(per):
                        zero(i * per + z)
                for b in range(RING + n * RING, NB):
                    load(b, b % RING, b // RING, 128)
                load(NB, NB % RING, NB // RING, TP)
                for z in range(n * per, sh.NZ):
                    zero(z)
                sp.wait_ge(table2_zeroed, 16 * sh.NZ)

            @block.tensor
            def _(pe):
                def turn(b, s, P):
                    pe.wait_ge(zc_ready, b + 1)
                    after(pe, zl_ready, b)
                    after(pe, zh_ready, b)
                    for h in range(KD):
                        for g in range(G):
                            last = nc.tensor.transpose(pzt[:, h * 512 + g * P:h * 512 + g * P + P],
                                                       zb[0:P, g, h * 128:(h + 1) * 128], ident[0:P, 0:P])
                    last.then_inc(z_turned, 1)

                def first(b, P):
                    n = G * P
                    pe.wait_ge(zh_ready, b + 1)
                    pe.wait_ge(zl_ready, b + 1)
                    for m in range(KH):
                        after(pe, relu_done, b * KH - (KH - 1 - m))
                        c = slice(m * 128, (m + 1) * 128)
                        terms = [(w1h[:, k, c], zh[:, k, 0:n]) for k in range(KD)]
                        terms += [(w1h[:, k, c], zl[:, k, 0:n]) for k in range(KD)]
                        terms += [(w1l[:, k, c], zh[:, k, 0:n]) for k in range(KD)]
                        for j, (w, mv) in enumerate(terms):
                            last = nc.tensor.matmul(pt[m][:, 0:n], w, mv, start=(j == 0), stop=(j == len(terms) - 1))
                        last.then_inc(t_ready, 1)

                def second(b, s, P):
                    pe.wait_ge(th_ready, (b + 1) * KH)
                    pe.wait_ge(tl_ready, (b + 1) * KH)
                    after(pe, u_ready, b)
                    for g in range(G):
                        c = slice(g * P, (g + 1) * P)
                        o = pc[0:P, g * D:(g + 1) * D]
                        for k in range(KH):
                            nc.tensor.matmul(o, th[s][:, k, c], w2h[:, k, :], start=(k == 0), stop=False)
                            nc.tensor.matmul(o, th[s][:, k, c], w2l[:, k, :], start=False, stop=False)
                            last = nc.tensor.matmul(o, tl[s][:, k, c], w2h[:, k, :], start=False, stop=(k == KH - 1))
                    last.then_inc(conv_ready, 1)

                def step(b, s, u, P=128, nextP=128):
                    first(b, P)
                    turn(b + 1, None, nextP)
                    second(b - 1, (s - 1) % 2, 128)
                turn(0, 0, 128)
                first(0, 128)
                turn(1, 1, 128)
                over(pe, 1, NB - 1, RING, step)
                step(NB - 1, (NB - 1) % RING, None, 128, TP)
                first(NB, TP)
                second(NB - 1, (NB - 1) % 2, 128)
                second(NB, NB % 2, TP)

                pe.wait_ge(s2, 1)
                for j, t in enumerate((usum, qsum)):
                    for g in range(G):
                        last = nc.tensor.matmul(pt[j][:, 0:D], ones[:, :], t[:, g, :], start=(g == 0), stop=(g == G - 1))
                last.then_inc(p2, 1)

            @block.scalar
            def _(act):
                def relus(b, s, u, P):
                    n = G * P
                    for m in range(KH):
                        act.wait_ge(t_ready, b * KH + (m + 1))
                        after(act, tl_ready, b * KH - (KH - 1 - m))
                        after(act, th_ready, b * KH - (KH - 1 - m))
                        nc.scalar.activation(tf[:, m, 0:n], pt[m][:, 0:n], ACT.Relu, bias=bias1[:, m:m + 1],
                                             scale=scale1[:, m:m + 1]).then_inc(relu_done, 1)

                def high(b, P):
                    n = G * P
                    act.wait_ge(z_turned, b + 1)
                    after(act, t_ready, b * KH)
                    nc.scalar.copy(zh[:, :, 0:n], pzt[:, :].rearrange("p (k n) -> p k n", k=KD)[:, :, 0:n]).then_inc(zh_ready, 1)

                def square(b, s, P):
                    act.wait_ge(u_ready, b + 1)
                    after(act, u_summed, b)
                    nc.scalar.square(sq[0:P], ub[s][0:P]).then_inc(sq_ready, 1)
                    act.dma_start(block_of(uv, b, P), ub[s][0:P].rearrange("p g d -> p (g d)")).then_inc(u_stored[s], 16)

                def step(b, s, u, P=128, nextP=128):
                    relus(b, s, u, P)
                    high(b + 1, nextP)
                    square(b - 1, (s - 1) % 2, 128)
                high(0, 128)
                relus(0, 0, 0, 128)
                high(1, 128)
                over(act, 1, NB - 1, RING, step)
                step(NB - 1, (NB - 1) % RING, None, 128, TP)
                relus(NB, None, None, TP)
                square(NB - 1, (NB - 1) % 2, 128)
                square(NB, NB % 2, TP)
                for s in range(2):
                    act.wait_ge(u_stored[s], ((NB - s) // 2 + 1) * 16)
                act.wait_ge(s2, 7)
                nc.scalar.activation(st2[:, 3, :], st2[:, 2, :], ACT.Sqrt).then_inc(p2, 1)

            @block.vector
            def _(dve):
                def make_z(b, s, u, P):
                    dve.wait_ge(xc_loaded[s], (u + 1) * 16)
                    dve.wait_ge(ac_loaded[s % 2], (u * (RING // 2) + s // 2 + 1) * 16)
                    after(dve, z_turned, b)
                    nc.vector.scalar_tensor_tensor(out=zb[0:P], in0=xb[s][0:P], scalar=cc[0:P, :], in1=ab[s % 2][0:P],
                                                   op0=ALU.mult, op1=ALU.add).then_inc(zc_ready, 1)

                def low_t(b, s, P):
                    n = G * P
                    for m in range(KH):
                        dve.wait_ge(th_ready, b * KH + (m + 1))
                        after(dve, conv_ready, b - 1)
                        nc.vector.tensor_tensor(tl[s][:, m, 0:n], tf[:, m, 0:n], th[s][:, m, 0:n], ALU.subtract).then_inc(tl_ready, 1)

                def low_z(b, P):
                    n = G * P
                    dve.wait_ge(zh_ready, b + 1)
                    nc.vector.tensor_tensor(zl[:, :, 0:n], pzt[:, :].rearrange("p (k n) -> p k n", k=KD)[:, :, 0:n], zh[:, :, 0:n],
                                            ALU.subtract).then_inc(zl_ready, 1)

                def add_x(b, s4, s, P, use2):
                    dve.wait_ge(conv_ready, b + 1)
                    after(dve, sq_ready, b - 1)
                    after(dve, usum_done, b - 1)
                    after(dve, u_stored[s], use2 * 16)
                    nc.vector.scalar_tensor_tensor(out=ub[s][0:P], in0=pc[0:P, :].rearrange("p (g d) -> p g d", g=G), scalar=1.0 / WS,
                                                   in1=xb[s4][0:P], op0=ALU.mult, op1=ALU.add).then_inc(u_ready, 1)

                def use_of(s, u):
                    return u * (RING // 2) + (s - 1) // 2

                def step(b, s, u, P=128, nextP=128):
                    make_z(b + 1, (s + 1) % RING, u + (s + 1) // RING, nextP)
                    low_t(b, s % 2, P)
                    low_z(b + 1, nextP)
                    add_x(b - 1, (s - 1) % RING, (s - 1) % 2, 128, use_of(s, u))
                make_z(0, 0, 0, 128)
                low_z(0, 128)
                make_z(1, 1, 0, 128)
                low_t(0, 0, 128)
                low_z(1, 128)
                over(dve, 1, NB - 1, RING, step)
                step(NB - 1, (NB - 1) % RING, (NB - 1) // RING, 128, TP)
                low_t(NB, NB % 2, TP)
                add_x(NB - 1, (NB - 1) % RING, (NB - 1) % 2, 128, (NB - 1) // 2)
                add_x(NB, NB % RING, NB % 2, TP, NB // 2)

                n = [1]

                def mark(ins):
                    n[0] += 1
                    ins.then_inc(s2, 1)
                    dve.wait_ge(s2, n[0])
                dve.wait_ge(p2, 1)
                mark(nc.vector.tensor_scalar(st2[:, 0, :], pt[0][:, 0:D], 1.0 / N, None, ALU.mult))
                mark(nc.vector.tensor_scalar(st2[:, 1, :], pt[1][:, 0:D], 1.0 / N, None, ALU.mult))
                mark(nc.vector.tensor_tensor(st2[:, 2, :], st2[:, 0, :], st2[:, 0, :], ALU.mult))
                mark(nc.vector.tensor_tensor(st2[:, 2, :], st2[:, 1, :], st2[:, 2, :], ALU.subtract))
                mark(nc.vector.tensor_scalar(st2[:, 2, :], st2[:, 2, :], 0.0, EPS, ALU.max, ALU.add))
                mark(nc.vector.tensor_tensor(st2[:, 0, :], st2[:, 0, :], rows2[:, 0, :], ALU.add))
                dve.wait_ge(p2, 2)
                mark(nc.vector.reciprocal(st2[:, 1, :], st2[:, 3, :]))
                mark(nc.vector.tensor_tensor(scale2[:, :], st2[:, 1, :], rows2[:, 1, :], ALU.mult))
                mark(nc.vector.tensor_tensor(st2[:, 2, :], rows2[:, 0, :], st2[:, 0, :], ALU.subtract))
                mark(nc.vector.tensor_tensor(st2[:, 2, :], st2[:, 2, :], scale2[:, :], ALU.mult))
                mark(nc.vector.tensor_tensor(bias2[:, :], st2[:, 2, :], rows2[:, 2, :], ALU.add))

            @block.gpsimd
            def _(pool):
                nc.gpsimd.memset(usum[:, :, :], 0.0)
                nc.gpsimd.memset(qsum[:, :, :], 0.0)

                def highs(b, s, P):
                    n = G * P
                    for m in range(KH):
                        pool.wait_ge(relu_done, b * KH + (m + 1))
                        after(pool, conv_ready, b - 1)
                        pool.sem_inc(pool_passed, 1)
                        nc.gpsimd.tensor_copy(th[s][:, m, 0:n], tf[:, m, 0:n]).then_inc(th_ready, 1)

                def summed(b, s, P):
                    pool.wait_ge(u_ready, b + 1)
                    after(pool, usum_done, b)
                    nc.gpsimd.tensor_tensor(usum[0:P], usum[0:P], ub[s][0:P], ALU.add).then_inc(usum_done, 1)
                    pool.wait_ge(sq_ready, b + 1)
                    after(pool, u_summed, b)
                    nc.gpsimd.tensor_tensor(qsum[0:P], qsum[0:P], sq[0:P], ALU.add).then_inc(u_summed, 1)

                def step(b, s, u, P=128):
                    highs(b, s % 2, P)
                    summed(b - 1, (s - 1) % 2, 128)
                highs(0, 0, 128)
                over(pool, 1, NB, RING, step)
                step(NB, NB % RING, None, TP)
                summed(NB, NB % 2, TP)
                pool.wait_ge(u_summed, NB + 1)
                pool.sem_inc(s2, 1)

        ph = ExitStack()
        rx = [sb(f"rx{s}", [128, K, D], f32, ph) for s in range(2)]
        ru = [sb(f"ru{s}", [128, K, D], f32, ph) for s in range(2)]
        msg = [sb(f"msg{s}", [128, K, D], f32, ph) for s in range(2)]
        sums = [sb(f"msums{s}", [128, K, D], f32, ph) for s in range(2)]
        turned = sb("turned", [128, KD, K * 128], f32, ph)
        sel = [sb(f"msel{s}", [128, K, K * 128], f32, ph) for s in range(2)]
        diag = sb("mdiag", [128, K, 128], f32, ph)
        junk = sb("mjunk", [128, K, K * 128], f16, ph)
        cnt = sb("mcnt", [128, 3, K], f32, ph)
        target = [sb(f"mtarget{s}", [128, K], i32, ph) for s in range(2)]
        stat = sb("mstat", [128, K, 6], f32, ph)
        mv = sb("mmv", [128, K, 2], f32, ph)
        mrs = sb("mrs", [128, 3, K], f32, ph)
        keyrow = ps("mkeyrow", K * 128, ph)
        pturn = ps("pturn", KD * K * 128, ph)
        comb = ps("mcomb", K * D, ph)

        xu_gathered = [sem(f"xu_gathered{s}") for s in range(2)]
        m_picked = sem("m_picked")
        m_spread = sem("m_spread")
        m_row = sem("m_row")
        m_sel = sem("m_sel")
        m_cnt = sem("m_cnt")
        m_target = sem("m_target")
        m_a = sem("m_scaled")
        m_b = sem("m_shifted")
        m_y = sem("m_y")
        m_s = sem("m_stats")
        m_mv = sem("m_mv")
        m_p = sem("m_pool")
        m_rstd = sem("m_rstd")
        m_msg = sem("m_msg")
        m_pt = sem("m_pturn")
        m_turned = sem("m_turned")
        m_comb = sem("m_comb")
        m_sums = sem("m_sums")
        m_added = [sem(f"m_added{s}") for s in range(2)]
        hset = sem("hset")

        with ph, nc.Block() as block:
            @block.gpsimd
            def _(pool):
                nc.gpsimd.memset(halves[:, :], -0.5).then_inc(hset, 1)
                pool.wait_ge(hset, 1)

                def gather(g, slot, use):
                    after(pool, m_msg, g - 1)
                    pool.sem_inc(pool_passed, 1)
                    nc.gpsimd.tensor_copy(picked[slot][:, :], gdst[:, bass.ds(g * K, K)]).then_inc(m_picked, 1)
                    pool.wait_ge(m_picked, g + 1)
                    pool.sem_inc(pool_passed, 1)
                    for k in range(K):
                        for to, of in ((rx, x), (ru, ubuf)):
                            pool.indirect_dma_start(to[slot][:, k, :], None, of,
                                                    IOA(ap=picked[slot][:, k:k + 1], axis=0)).then_inc(xu_gathered[slot], 16)

                def rstd(g):
                    pool.wait_ge(m_mv, g + 1)
                    after(pool, m_msg, g)
                    pool.sem_inc(pool_passed, 1)
                    nc.gpsimd.tensor_scalar(mrs[:, 0, :], mv[:, :, 1], EPS, None, ALU.add)
                    nc.gpsimd.tensor_scalar(mrs[:, 2, :], mv[:, :, 0], -1.0, None, ALU.mult).then_inc(m_p, 1)
                    pool.wait_ge(m_p, g * 3 + 1)
                    nc.gpsimd.tensor_tensor(mrs[:, 0, :], mrs[:, 0, :], halves[:, :], ALU.pow).then_inc(m_p, 1)
                    pool.wait_ge(m_p, g * 3 + 2)
                    nc.gpsimd.tensor_tensor(mrs[:, 1, :], mrs[:, 0, :], wgt[:, bass.ds(g * K, K)], ALU.mult).then_inc(m_p, 1)
                    pool.wait_ge(m_p, g * 3 + 3)
                    nc.gpsimd.tensor_tensor(mrs[:, 2, :], mrs[:, 2, :], mrs[:, 1, :], ALU.mult).then_inc(m_rstd, 1)

                def add(g, slot, use):
                    pool.wait_ge(m_sums, g + 1)
                    pool.wait_ge(m_target, g + 1)
                    after(pool, m_added[1 - slot], (use + slot) * (16 * K))
                    pool.sem_inc(pool_passed, 1)
                    for k in range(K):
                        pool.indirect_dma_start(agg2, IOA(ap=target[slot][:, k:k + 1], axis=0), sums[slot][:, k, :], None,
                                                compute_op=ALU.add).then_inc(m_added[slot], 16)

                def both(g, slot, use):
                    rstd(g)
                    gather(g + 1, 1 - slot, use + slot)
                    add(g - 1, 1 - slot, use - 1 + slot)

                gather(0, 0, 0)
                rstd(0)
                gather(1, 1, 0)
                over(pool, 1, NG - 1, 2, both)
                last = NG - 1
                rstd(last)
                add(last - 1, (last - 1) % 2, (last - 1) // 2)
                add(last, last % 2, last // 2)
                pool.wait_ge(m_added[last % 2], (last // 2 + 1) * 16 * K)
                pool.wait_ge(m_added[1 - last % 2], ((last - 1) // 2 + 1) * 16 * K)

            @block.vector
            def _(dve):
                names = (m_spread, m_row, m_sel, m_cnt, m_target, sel, keyrow, target, cnt, junk, diag)
                sc = scale2[:, :].unsqueeze(1).to_broadcast([128, K, D])
                bi = bias2[:, :].unsqueeze(1).to_broadcast([128, K, D])

                def normed(g, slot, use):
                    dve.wait_ge(xu_gathered[slot], (use + 1) * (32 * K))
                    nc.vector.tensor_tensor(ru[slot][:, :, :], ru[slot][:, :, :], sc, ALU.mult).then_inc(m_a, 1)
                    dve.wait_ge(m_a, g + 1)
                    nc.vector.tensor_tensor(ru[slot][:, :, :], ru[slot][:, :, :], bi, ALU.add).then_inc(m_b, 1)
                    dve.wait_ge(m_b, g + 1)
                    nc.vector.scalar_tensor_tensor(out=rx[slot][:, :, :], in0=ru[slot][:, :, :], scalar=0.0, in1=rx[slot][:, :, :],
                                                   op0=ALU.max, op1=ALU.add).then_inc(m_y, 1)
                    dve.wait_ge(m_y, g + 1)
                    after(dve, m_rstd, g)
                    for k in range(K):
                        last = nc.vector.bn_stats(stat[:, k, :], rx[slot][:, k, :])
                    last.then_inc(m_s, 1)
                    dve.wait_ge(m_s, g + 1)
                    dve.sem_inc(dve_passed, 1)
                    for k in range(K):
                        last = nc.vector.bn_aggr(mv[:, k, :], stat[:, k, :])
                    last.then_inc(m_mv, 1)

                def group(g, slot, use, more=True):
                    normed(g, slot, use)
                    if more:
                        dve.wait_ge(m_row, g + 1)
                        spread_keys(g + 1, ksrc, diag, m_spread)
                    after(dve, m_comb, g - 1)
                    after(dve, m_added[slot], use * (16 * K))
                    select_edges(dve, g, slot, ksrc, names)

                spread_keys(0, ksrc, diag, m_spread)
                group(0, 0, 0)
                group(1, 1, 0)
                over(dve, 2, NG - 1, 2, group)
                group(NG - 1, (NG - 1) % 2, (NG - 1) // 2, False)

            @block.scalar
            def _(act):
                def message(g, slot):
                    act.wait_ge(m_rstd, g + 1)
                    after(act, m_pt, g - 1)
                    for k in range(K):
                        last = nc.scalar.activation(msg[slot][:, k, :], rx[slot][:, k, :], ACT.Identity,
                                                    bias=mrs[:, 2, k:k + 1], scale=mrs[:, 1, k:k + 1])
                    last.then_inc(m_msg, 1)

                def evacuate(g, slot, use):
                    act.wait_ge(m_pt, g + 1)
                    after(act, m_comb, g)
                    nc.scalar.copy(turned[:, :, :], pturn[:, :].rearrange("p (h j) -> p h j", h=KD)).then_inc(m_turned, 1)
                    act.wait_ge(m_comb, g + 1)
                    after(act, m_added[slot], use * (16 * K))
                    nc.scalar.copy(sums[slot][:, :, :], comb[:, :].rearrange("p (k d) -> p k d", k=K)).then_inc(m_sums, 1)

                def step(g, slot, use):
                    message(g, slot)
                    evacuate(g - 1, 1 - slot, use - 1 + slot)
                message(0, 0)
                step(1, 1, 0)
                over(act, 2, NG, 2, step)
                evacuate(NG - 1, (NG - 1) % 2, (NG - 1) // 2)

            @block.tensor
            def _(pe):
                def spread(g):
                    pe.wait_ge(m_spread, g + 1)
                    nc.tensor.matmul(keyrow[:, :], ones[:, :], diag[:, :, :].rearrange("p k j -> p (k j)"),
                                     start=True, stop=True).then_inc(m_row, 1)

                def combine(g, slot):
                    pe.wait_ge(m_sel, g + 1)
                    pe.wait_ge(m_msg, g + 1)
                    after(pe, m_turned, g)
                    for h in range(KD):
                        for j in range(K):
                            last = nc.tensor.matmul(pturn[:, h * 512:h * 512 + K * 128], msg[slot][:, j, h * 128:(h + 1) * 128],
                                                    sel[slot][:, j, :], start=(j == 0), stop=(j == K - 1))
                    last.then_inc(m_pt, 1)
                    pe.wait_ge(m_turned, g + 1)
                    after(pe, m_sums, g)
                    for k in range(K):
                        for h in range(KD):
                            last = nc.tensor.matmul(comb[:, k * D:(k + 1) * D], turned[:, h, k * 128:(k + 1) * 128], lwt[:, h, :],
                                                    start=(h == 0), stop=(h == KD - 1))
                    last.then_inc(m_comb, 1)

                def group(g, slot, use):
                    after(pe, m_target, g)
                    spread(g)
                    combine(g - 1, 1 - slot)
                spread(0)
                over(pe, 1, NG, 2, group)
                combine(NG - 1, (NG - 1) % 2)

        ph = ExitStack()
        un = [sb(f"un{s}", [128, G, D], f32, ph) for s in range(RING)]
        xn = [sb(f"xn{s}", [128, G, D], f32, ph) for s in range(RING)]
        an = [sb(f"an{s}", [128, G, D], f32, ph) for s in range(RING)]
        vn = [sb(f"vn{s}", [128, G, D], f32, ph) for s in range(RING)]
        on = [sb(f"on{s}", [128, G, D], f32, ph) for s in range(RING)]
        nst = sb("nst", [128, 2, G, 6], f32, ph)
        nmv = sb("nmv", [128, 2, G, 2], f32, ph)
        nrs = sb("nrs", [128, 2, 3, G], f32, ph)
        n_loaded = [sem(f"n_loaded{s}") for s in range(RING)]
        n_scaled = sem("n_scaled")
        n_shift = sem("n_shifted")
        n_y = sem("n_y")
        n_s = [sem(f"n_stats{j}") for j in range(2)]
        n_mv = [sem(f"n_mv{j}") for j in range(2)]
        n_p = [sem(f"n_pool{j}") for j in range(2)]
        n_rstd = [sem(f"n_rstd{j}") for j in range(2)]
        n_x1 = sem("n_x1")
        n_v = sem("n_v")
        n_out = sem("n_out")
        n_stored = [sem(f"n_stored{s}") for s in range(RING)]

        with ph, nc.Block() as block:
            @block.sync
            def _(sp):
                def load(b, s, u, P):
                    after(sp, n_v, b - RING + 1)
                    for to, of in ((un, uv), (xn, xv), (an, agg2v)):
                        sp.dma_start(to[s][0:P].rearrange("p g d -> p (g d)"), block_of(of, b, P)).then_inc(n_loaded[s], 16)
                for s in range(RING):
                    load(s, s, 0, 128)
                all_blocks(sp, load, RING)

            @block.gpsimd
            def _(pool):
                sc = scale2[:, :].unsqueeze(1).to_broadcast([128, G, D])

                def scaled(b, s, u, P):
                    pool.wait_ge(n_loaded[s], (u + 1) * 48)
                    nc.gpsimd.tensor_tensor(un[s][0:P], un[s][0:P], sc[0:P], ALU.mult).then_inc(n_scaled, 1)

                def rstd(b, j, P):
                    pool.wait_ge(n_mv[j], b + 1)
                    after(pool, n_x1 if j == 0 else n_out, b)
                    r = nrs[0:P, j]
                    pool.sem_inc(pool_passed, 1)
                    nc.gpsimd.tensor_scalar(r[:, 0, :], nmv[0:P, j, :, 1], EPS, None, ALU.add)
                    nc.gpsimd.tensor_scalar(r[:, 1, :], nmv[0:P, j, :, 0], -1.0, None, ALU.mult).then_inc(n_p[j], 1)
                    pool.wait_ge(n_p[j], b * 2 + 1)
                    nc.gpsimd.tensor_tensor(r[:, 0, :], r[:, 0, :], halves[0:P, :], ALU.pow).then_inc(n_p[j], 1)
                    pool.wait_ge(n_p[j], b * 2 + 2)
                    nc.gpsimd.tensor_tensor(r[:, 2, :], r[:, 0, :], r[:, 1, :], ALU.mult).then_inc(n_rstd[j], 1)

                def step(b, s, u, P):
                    rstd(b - 1, 0, 128)
                    scaled(b, s, u, P)
                    rstd(b - 2, 1, 128)
                scaled(0, 0, 0, 128)
                rstd(0, 0, 128)
                scaled(1, 1, 0, 128)
                over(pool, 2, NB, RING, lambda b, s, u: step(b, s, u, 128))
                step(NB, NB % RING, NB // RING, TP)
                rstd(NB, 0, TP)
                rstd(NB - 1, 1, 128)
                rstd(NB, 1, TP)

            @block.vector
            def _(dve):
                bi = bias2[:, :].unsqueeze(1).to_broadcast([128, G, D])

                def stats(b, j, t, P):
                    after(dve, n_rstd[j], b)
                    for g in range(G):
                        last = nc.vector.bn_stats(nst[0:P, j, g, :], t[0:P, g, :])
                    last.then_inc(n_s[j], 1)
                    dve.wait_ge(n_s[j], b + 1)
                    dve.sem_inc(dve_passed, 1)
                    for g in range(G):
                        last = nc.vector.bn_aggr(nmv[0:P, j, g, :], nst[0:P, j, g, :])
                    last.then_inc(n_mv[j], 1)

                def y(b, s, P):
                    dve.wait_ge(n_scaled, b + 1)
                    nc.vector.tensor_tensor(un[s][0:P], un[s][0:P], bi[0:P], ALU.add).then_inc(n_shift, 1)
                    dve.wait_ge(n_shift, b + 1)
                    nc.vector.scalar_tensor_tensor(out=xn[s][0:P], in0=un[s][0:P], scalar=0.0, in1=xn[s][0:P],
                                                   op0=ALU.max, op1=ALU.add).then_inc(n_y, 1)
                    dve.wait_ge(n_y, b + 1)
                    stats(b, 0, xn[s], P)

                def v(b, s, P):
                    dve.wait_ge(n_x1, b + 1)
                    after(dve, n_out, b - RING + 1)
                    nc.vector.tensor_tensor(vn[s][0:P], xn[s][0:P], an[s][0:P], ALU.add).then_inc(n_v, 1)
                    dve.wait_ge(n_v, b + 1)
                    stats(b, 1, vn[s], P)

                def step(b, s, P):
                    y(b, s, P)
                    v(b - 1, (s - 1) % RING, 128)
                y(0, 0, 128)
                over(dve, 1, NB, RING, lambda b, s, u: step(b, s, 128))
                step(NB, NB % RING, TP)
                v(NB, NB % RING, TP)

            @block.scalar
            def _(act):
                def norm(to, of, j, P, done):
                    for g in range(G):
                        last = nc.scalar.activation(to[0:P, g, :], of[0:P, g, :], ACT.Identity,
                                                    bias=nrs[0:P, j, 2, g:g + 1], scale=nrs[0:P, j, 0, g:g + 1])
                    last.then_inc(done, 1)

                def x1(b, s, P):
                    act.wait_ge(n_rstd[0], b + 1)
                    norm(xn[s], xn[s], 0, P, n_x1)

                def result(b, s, u, P):
                    act.wait_ge(n_rstd[1], b + 1)
                    after(act, n_stored[s], u * 16)
                    norm(on[s], vn[s], 1, P, n_out)
                    act.wait_ge(n_out, b + 1)
                    act.dma_start(block_of(outv, b, P), on[s][0:P].rearrange("p g d -> p (g d)")).then_inc(n_stored[s], 16)

                def step(b, s, u, P):
                    x1(b, s, P)
                    result(b - 2, (s - 2) % RING, u + (s - 2) // RING, 128)
                x1(0, 0, 128)
                x1(1, 1, 128)
                over(act, 2, NB, RING, lambda b, s, u: step(b, s, u, 128))
                step(NB, NB % RING, NB // RING, TP)
                result(NB - 1, (NB - 1) % RING, (NB - 1) // RING, 128)
                result(NB, NB % RING, NB // RING, TP)
                for s in range(RING):
                    act.wait_ge(n_stored[s], ((NB - s) // RING + 1) * 16)


_INS = ['x', 'src', 'dst', 'edge_weight', 'L0_gnn_W1', 'L0_gnn_b1', 'L0_gnn_g1', 'L0_gnn_bt1', 'L0_gnn_W2', 'L0_gnn_b2',
        'L0_gnn_g2', 'L0_gnn_bt2', 'L0_gnn_eps_gin', 'L1_gnn_W']


def kernel(**inputs):
    import numpy as _np
    import concourse.bacc as _bacc
    from concourse import mybir as _mybir
    from concourse.bass_utils import run_bass_kernel_spmd as _run

    nc = _bacc.Bacc("TRN2", target_bir_lowering=False, num_devices=1)
    arrays, args = {}, []
    for name in _INS:
        a = _np.ascontiguousarray(inputs[name])
        a = a.reshape(a.shape or (1,))
        arrays[f"in_{name}"] = a
        args.append(nc.dram_tensor(f"in_{name}", a.shape, _mybir.dt.from_np(a.dtype), kind="ExternalInput").ap())
    shape = _np.shape(inputs['x'])
    o = nc.dram_tensor("out_dram", shape, _mybir.dt.float32, kind="ExternalOutput").ap()
    gnn(nc, *args, o)
    r = _run(nc, [arrays], core_ids=[0])
    return r.results[0]["out_dram"]
```

```python
import concourse.bass as bass
from concourse import mybir
from contextlib import ExitStack

f32 = mybir.dt.float32
f16 = mybir.dt.float16
i32 = mybir.dt.int32
ALU = mybir.AluOpType
ACT = mybir.ActivationFunctionType
IOA = bass.IndirectOffsetOnAxis

EPS = 1e-5
WS = 64.0
K = 2
G = 4
RING = 4
NRING = 6
ERING = 4


class Shapes:

    def __init__(s, n, d, h, e):
        s.N, s.D, s.H, s.E = n, d, h, e
        s.KD, s.KH = d // 128, h // 128
        s.BR = 128 * G
        s.NB = n // s.BR
        s.TP = (n - s.NB * s.BR) // G
        assert s.NB * s.BR + s.TP * G == n and 0 < s.TP < 128
        s.C = -(-e // (128 * K)) * K
        s.NG = s.C // K
        s.ZR = 8
        s.NZ = -(-(n + 1 + K * 128) // (128 * s.ZR))
        s.T = s.NZ * 128 * s.ZR


def over(eng, lo, hi, unroll, step):
    first = max(lo, 2 * unroll)
    n = (hi - first) // unroll
    if n < 2:
        first, n = hi, 0
    for b in range(lo, first):
        step(b, b % unroll, b // unroll)
    if n:
        with eng.Fori(0, n) as i:
            for s in range(unroll):
                b = first + s
                step(i * unroll + b, b % unroll, i + b // unroll)
    for b in range(first + n * unroll, hi):
        step(b, b % unroll, b // unroll)


def back(slot, use, d):
    return (slot - d) % ERING, use + (slot - d) // ERING


def after(eng, sem, value):
    if not isinstance(value, int) or value > 0:
        eng.wait_ge(sem, value)


def row_blocks(ap, sh):
    full = ap[0:sh.NB * sh.BR, :].rearrange("(b p g) d -> b p (g d)", p=128, g=G)
    tail = ap[sh.NB * sh.BR:sh.N, :].rearrange("(p g) d -> p (g d)", g=G)
    return full, tail


def block_of(views, b, P):
    full, tail = views
    return full[bass.ds(b, 1)].rearrange("a p d -> (a p) d") if P == 128 else tail


def gnn(nc, x, src, dst, ew, W1, b1, g1, bt1, W2, b2, g2, bt2, eps_gin, LW, out):
    sh = Shapes(x.shape[0], x.shape[1], W1.shape[1], src.shape[0])
    N, D, H, E, C, NG, NB, TP = sh.N, sh.D, sh.H, sh.E, sh.C, sh.NG, sh.NB, sh.TP
    KD, KH = sh.KD, sh.KH
    agg = nc.dram_tensor("agg", (sh.T, D), f32).ap()
    agg2 = nc.dram_tensor("agg2", (sh.T, D), f32).ap()
    ubuf = nc.dram_tensor("ubuf", (N, D), f32).ap()
    agg_z = agg.rearrange("(z p r) d -> z p (r d)", p=128, r=sh.ZR)
    agg2_z = agg2.rearrange("(z p r) d -> z p (r d)", p=128, r=sh.ZR)
    xv, aggv, agg2v, uv, outv = (row_blocks(t, sh) for t in (x, agg, agg2, ubuf, out))
    whole = ExitStack()
    with whole:
        def sb(name, shape, dt, scope=whole):
            return scope.enter_context(nc.sbuf_tensor(name, shape, dt))

        def ps(name, cols, scope):
            return scope.enter_context(nc.psum_tensor(name, [128, cols], f32))

        def sem(name):
            return whole.enter_context(nc.semaphore(name))

        ident = sb("ident", [128, 128], f32)
        ones = sb("ones", [128, 128], f32)
        ones16 = sb("ones16", [128, 1], f16)
        zeros16 = sb("zeros16", [128, 512], f16)
        zrows = sb("zrows", [128, sh.ZR * D], f32)
        w1f = sb("w1f", [128, KD, H], f32)
        w1h = sb("w1h", [128, KD, H], f16)
        w1l = sb("w1l", [128, KD, H], f16)
        w2h = sb("w2h", [128, KH, D], f16)
        w2l = sb("w2l", [128, KH, D], f16)
        lwt = sb("lwt", [128, KD, D], f32)
        cc = sb("cc", [128, 1], f32)
        b1c = sb("b1c", [128, 3, KH], f32)
        scale1 = sb("scale1", [128, KH], f32)
        bias1 = sb("bias1", [128, KH], f32)
        rows2 = sb("rows2", [128, 3, D], f32)
        scale2 = sb("scale2", [128, D], f32)
        bias2 = sb("bias2", [128, D], f32)
        gsrc = sb("gsrc", [128, C], i32)
        gdst = sb("gdst", [128, C], i32)
        key_i = sb("key_i", [128, 2, C], i32)
        kdst = sb("kdst", [128, C], f32)
        ksrc = sb("ksrc", [128, C], f32)
        wgt = sb("wgt", [128, C], f32)
        picked = [sb(f"picked{s}", [128, K], i32) for s in range(ERING)]
        epsc = sb("epsc", [128, 1], f32)
        before = sb("before", [128, K, K * 128], f32)
        spare = sb("spare", [128, K], f32)
        spare_i = sb("spare_i", [128, K], i32)

        def refine(mark, r, var, tmp):
            mark(nc.vector.tensor_tensor(tmp, var, r, ALU.mult))
            mark(nc.vector.scalar_tensor_tensor(out=tmp, in0=tmp, scalar=-0.5, in1=r, op0=ALU.mult, op1=ALU.mult))
            mark(nc.vector.scalar_tensor_tensor(out=r, in0=tmp, scalar=1.5, in1=r, op0=ALU.add, op1=ALU.mult))

        ph = ExitStack()
        w2f = sb("w2f", [128, KH, D], f32, ph)
        lwf = sb("lwf", [128, KD, D], f32, ph)
        rows_x = [sb(f"rows_x{s}", [128, K, D], f32, ph) for s in range(ERING)]
        sums = [sb(f"sums{s}", [128, K, D], f32, ph) for s in range(ERING)]
        sel = [sb(f"sel{s}", [128, K, K * 128], f32, ph) for s in range(ERING)]
        diag = sb("diag", [128, K, 128], f32, ph)
        junk = sb("junk", [128, K, K * 128], f16, ph)
        cnt = sb("cnt", [128, 3, K], f32, ph)
        target = [sb(f"target{s}", [128, K], i32, ph) for s in range(ERING)]
        keyrow = ps("keyrow", K * 128, ph)
        comb = ps("comb", K * D, ph)
        lwp = ps("lwp", 512, ph)

        pool_passed, dve_passed = sem("pool_passed"), sem("dve_passed")
        const_loaded = sem("const_loaded")
        idx_cleared = sem("idx_cleared")
        idx_loaded = sem("idx_loaded")
        consts_made = sem("consts_made")
        pool_consts = sem("pool_consts")
        dve_c = sem("dve_c")
        lw_turned = sem("lw_turned")
        table_zeroed = sem("table_zeroed")
        x_gathered = [sem(f"x_gathered{s}") for s in range(ERING)]
        x_picked = sem("x_picked")
        keys_spread = sem("keys_spread")
        keyrow_ready = sem("keyrow_ready")
        sel_ready = sem("sel_ready")
        cnt_ready = sem("cnt_ready")
        target_ready = sem("target_ready")
        comb_ready = sem("comb_ready")
        sums_ready = sem("sums_ready")
        sums_added = [sem(f"sums_added{s}") for s in range(ERING)]

        full_p, rest = E // C, E % C

        def load_edges(eng, to, ap):
            eng.dma_start(to[0:full_p, :], ap[0:full_p * C].rearrange("(p c) -> p c", c=C)).then_inc(idx_loaded, 16)
            n = 1
            if rest:
                eng.dma_start(to[full_p:full_p + 1, 0:rest],
                              ap[full_p * C:E].rearrange("(a c) -> a c", a=1)).then_inc(idx_loaded, 16)
                n = 2
            return n

        IDX_LOADS = 5 * (2 if rest else 1)

        def select_edges(dve, g, slot, keys, ready):
            spread, row_ready, sel_sem, cnt_sem, target_sem, sel_t, key_row, target_t, tmp, jnk, dg = ready
            kcols = keys[:, bass.ds(g * K, K)]
            dve.wait_ge(row_ready, g + 1)
            for k in range(K):
                last = nc.vector.tensor_scalar(sel_t[slot][:, k, :], key_row[:, :], keys[:, bass.ds(g * K + k, 1)], None,
                                               ALU.is_equal)
            for k in range(K):
                last = nc.vector.scalar_tensor_tensor(out=jnk[:, k, :], in0=key_row[:, :], scalar=keys[:, bass.ds(g * K + k, 1)],
                                                      in1=before[:, k, :], op0=ALU.is_equal, op1=ALU.mult,
                                                      accum_out=tmp[:, 0, k:k + 1])
            last = nc.vector.tensor_tensor(tmp[:, 1, :], spare[:, :], kcols, ALU.subtract)
            last.then_inc(sel_sem, 1)
            dve.wait_ge(sel_sem, g + 1)
            nc.vector.scalar_tensor_tensor(out=tmp[:, 2, :], in0=tmp[:, 0, :], scalar=1.0, in1=tmp[:, 1, :],
                                           op0=ALU.min, op1=ALU.mult).then_inc(cnt_sem, 1)
            dve.wait_ge(cnt_sem, g + 1)
            nc.vector.tensor_tensor(target_t[slot][:, :], tmp[:, 2, :], kcols, ALU.add).then_inc(target_sem, 1)

        def spread_keys(g, keys, dg, spread):
            nc.vector.tensor_tensor(dg[:, :, :], ident[:, :].unsqueeze(1).to_broadcast([128, K, 128]),
                                    keys[:, bass.ds(g * K, K)].unsqueeze(2).to_broadcast([128, K, 128]),
                                    ALU.mult).then_inc(spread, 1)

        with ph, nc.Block() as block:
            @block.sync
            def _(sp):
                sp.wait_ge(consts_made, 1)
                zs = [0]

                def zero(z, slot, use):
                    sp.dma_start(agg_z[bass.ds(z, 1)].rearrange("a p r -> (a p) r"), zrows[:, :]).then_inc(table_zeroed, 16)

                over(sp, 0, sh.NZ, RING, zero)
                sp.wait_ge(table_zeroed, 16 * sh.NZ)

            @block.scalar
            def _(act):
                act.dma_start(w1f[:, :, :], W1.rearrange("(k p) n -> p k n", p=128)).then_inc(const_loaded, 16)
                act.dma_start(w2f[:, :, :], W2.rearrange("(k p) n -> p k n", p=128)).then_inc(const_loaded, 16)
                act.dma_start(lwf[:, :, :], LW.rearrange("(k p) n -> p k n", p=128)).then_inc(const_loaded, 16)
                act.dma_start(cc[:, :], eps_gin.rearrange("(a n) -> a n", a=1).to_broadcast([128, 1])).then_inc(const_loaded, 16)
                for j, v in enumerate((b1, g1, bt1)):
                    act.dma_start(b1c[:, j, :], v.rearrange("(m p) -> p m", p=128),
                                  allow_slow_non_contiguous=True).then_inc(const_loaded, 16)
                for j, v in enumerate((b2, g2, bt2)):
                    act.dma_start(rows2[:, j, :], v.rearrange("(a n) -> a n", a=1).to_broadcast([128, D])).then_inc(const_loaded, 16)
                act.wait_ge(idx_cleared, 5)
                load_edges(act, gsrc, src)
                load_edges(act, gdst, dst)
                load_edges(act, key_i[:, 0, :], dst)
                load_edges(act, key_i[:, 1, :], src)
                load_edges(act, wgt, ew)

                def evacuate(g, slot, use):
                    act.wait_ge(comb_ready, g + 1)
                    after(act, sums_added[slot], use * (16 * K))
                    nc.scalar.copy(sums[slot][:, :, :], comb[:, :].rearrange("p (k d) -> p k d", k=K)).then_inc(sums_ready, 1)

                over(act, 0, NG, ERING, evacuate)

            @block.gpsimd
            def _(pool):
                nc.gpsimd.memset(ident[:, :], 0.0).then_inc(pool_consts, 1)
                nc.gpsimd.memset(ones[:, :], 1.0)
                nc.gpsimd.memset(before[:, :, :], 1.0).then_inc(pool_consts, 1)
                pool.wait_ge(pool_consts, 2)
                nc.gpsimd.affine_select(out=ident[:, :], in_=ident[:, :], compare_op=ALU.not_equal, fill=1.0,
                                        base=0, pattern=[[-1, 128]], channel_multiplier=1)
                for k in range(K):
                    nc.gpsimd.affine_select(out=before[:, k, :], in_=before[:, k, :], compare_op=ALU.is_gt, fill=0.0,
                                            base=128 * k, pattern=[[-1, K * 128]], channel_multiplier=1)
                nc.gpsimd.iota(spare_i[:, :], pattern=[[128, K]], base=N + 1, channel_multiplier=1).then_inc(pool_consts, 1)
                pool.wait_ge(idx_loaded, 16 * IDX_LOADS)

                def gather(g, slot, use):
                    after(pool, comb_ready, g - ERING + 1)
                    pool.sem_inc(pool_passed, 1)
                    nc.gpsimd.tensor_copy(picked[slot][:, :], gsrc[:, bass.ds(g * K, K)]).then_inc(x_picked, 1)
                    pool.wait_ge(x_picked, g + 1)
                    pool.sem_inc(pool_passed, 1)
                    for k in range(K):
                        pool.indirect_dma_start(rows_x[slot][:, k, :], None, x,
                                                IOA(ap=picked[slot][:, k:k + 1], axis=0)).then_inc(x_gathered[slot], 16)

                def add(g, slot, use):
                    pool.wait_ge(sums_ready, g + 1)
                    pool.wait_ge(target_ready, g + 1)
                    pool.wait_ge(table_zeroed, 16 * sh.NZ)
                    before_s, before_u = back(slot, use, 1)
                    after(pool, sums_added[before_s], (before_u + 1) * (16 * K))
                    pool.sem_inc(pool_passed, 1)
                    for k in range(K):
                        pool.indirect_dma_start(agg, IOA(ap=target[slot][:, k:k + 1], axis=0), sums[slot][:, k, :], None,
                                                compute_op=ALU.add).then_inc(sums_added[slot], 16)

                def both(g, slot, use):
                    gather(g + 2, *back(slot, use, -2))
                    add(g, slot, use)

                gather(0, 0, 0)
                gather(1, 1, 0)
                over(pool, 0, NG - 2, ERING, both)
                for g in range(NG - 2, NG):
                    add(g, g % ERING, g // ERING)
                pool.wait_ge(sums_added[g % ERING], (g // ERING + 1) * 16 * K)

            @block.vector
            def _(dve):
                nc.vector.memset(zrows[:, :], 0.0).then_inc(consts_made, 1)
                nc.vector.memset(zeros16[:, :], 0.0)
                nc.vector.memset(epsc[:, :], EPS)
                nc.vector.memset(ones16[:, :], 1.0)
                nc.vector.memset(gsrc[:, :], 0).then_inc(idx_cleared, 1)
                nc.vector.memset(gdst[:, :], 0).then_inc(idx_cleared, 1)
                nc.vector.memset(key_i[:, 0, :], N).then_inc(idx_cleared, 1)
                nc.vector.memset(key_i[:, 1, :], N).then_inc(idx_cleared, 1)
                nc.vector.memset(wgt[:, :], 0.0).then_inc(idx_cleared, 1)
                dve.wait_ge(const_loaded, 160)
                nc.vector.tensor_scalar(cc[:, :], cc[:, :], 1.0, None, ALU.add)
                for full, hi, lo in ((w1f, w1h, w1l), (w2f, w2h, w2l)):
                    nc.vector.tensor_scalar(hi[:, :, :], full[:, :, :], WS, None, ALU.mult).then_inc(dve_c, 1)
                dve.wait_ge(dve_c, 2)
                for full, hi, lo in ((w1f, w1h, w1l), (w2f, w2h, w2l)):
                    nc.vector.scalar_tensor_tensor(out=lo[:, :, :], in0=full[:, :, :], scalar=WS, in1=hi[:, :, :],
                                                   op0=ALU.mult, op1=ALU.subtract)
                dve.wait_ge(lw_turned, 1)
                nc.vector.tensor_copy(lwt[:, :, :], lwp[:, :].rearrange("p (k n) -> p k n", k=KD))
                dve.wait_ge(pool_consts, 3)
                dve.wait_ge(idx_loaded, 16 * IDX_LOADS)
                nc.vector.tensor_copy(spare[:, :], spare_i[:, :])
                nc.vector.tensor_copy(kdst[:, :], key_i[:, 0, :])
                nc.vector.tensor_copy(ksrc[:, :], key_i[:, 1, :]).then_inc(dve_c, 1)
                dve.wait_ge(dve_c, 3)
                names = (keys_spread, keyrow_ready, sel_ready, cnt_ready, target_ready, sel, keyrow, target, cnt, junk, diag)
                spread_keys(0, kdst, diag, keys_spread)

                def group(g, slot, use):
                    dve.wait_ge(keyrow_ready, g + 1)
                    spread_keys(g + 1, kdst, diag, keys_spread)
                    after(dve, comb_ready, g - ERING + 1)
                    after(dve, sums_added[slot], use * (16 * K))
                    select_edges(dve, g, slot, kdst, names)

                over(dve, 0, NG - 1, ERING, group)
                last = NG - 1
                dve.wait_ge(comb_ready, last - ERING + 1)
                dve.wait_ge(sums_added[last % ERING], (last // ERING) * 16 * K)
                select_edges(dve, last, last % ERING, kdst, names)

            @block.tensor
            def _(pe):
                pe.wait_ge(pool_consts, 3)
                pe.wait_ge(const_loaded, 160)
                for i in range(KD):
                    for j in range(KD):
                        turned = nc.tensor.transpose(lwp[:, i * D + j * 128:i * D + j * 128 + 128],
                                                     lwf[:, j, i * 128:(i + 1) * 128], ident[:, :])
                turned.then_inc(lw_turned, 1)

                def spread(g):
                    pe.wait_ge(keys_spread, g + 1)
                    nc.tensor.matmul(keyrow[:, :], ones[:, :], diag[:, :, :].rearrange("p k j -> p (k j)"),
                                     start=True, stop=True).then_inc(keyrow_ready, 1)

                def combine(g, slot, use):
                    pe.wait_ge(x_gathered[slot], (use + 1) * (16 * K))
                    pe.wait_ge(sel_ready, g + 1)
                    after(pe, sums_ready, g)
                    for k in range(K):
                        for j in range(K):
                            last = nc.tensor.matmul(comb[:, k * D:(k + 1) * D], sel[slot][:, j, k * 128:(k + 1) * 128],
                                                    rows_x[slot][:, j, :], start=(j == 0), stop=(j == K - 1))
                    last.then_inc(comb_ready, 1)

                def group(g, slot, use):
                    after(pe, target_ready, g)
                    spread(g)
                    combine(g - 1, *back(slot, use, 1))

                spread(0)
                over(pe, 1, NG, ERING, group)
                last = NG - 1
                combine(last, last % ERING, last // ERING)

        ph = ExitStack()
        xb = [sb(f"xb{s}", [128, G, D], f32, ph) for s in range(RING)]
        ab = [sb(f"ab{s}", [128, G, D], f32, ph) for s in range(RING)]
        zb = [sb(f"zb{s}", [128, G, D], f32, ph) for s in range(RING)]
        zz = [sb(f"zz{s}", [128, G, 2 * D], f16, ph) for s in range(RING)]
        gram = sb("gram", [128, KD, D], f32, ph)
        mcol = sb("mcol", [128, 4], f32, ph)
        mrow = sb("mrow", [1, D], f32, ph)
        prod = sb("prod", [128, KD, H], f32, ph)
        st1 = sb("st1", [128, 6, KH], f32, ph)
        pg = [ps(f"pg{h}", 512, ph) for h in range(KD)]
        psum_z = ps("psum_z", 512, ph)
        pv = [ps(f"pv{h}", 512, ph) for h in range(KD)]
        pm = ps("pm", 512, ph)
        pst = ps("pst", 512, ph)

        xa_loaded = [sem(f"xa_loaded{s}") for s in range(RING)]
        z_ready = sem("z_ready")
        hi_ready = sem("hi_ready")
        lo_ready = sem("lo_ready")
        z_used = sem("z_used")
        gram_done = sem("gram_done")
        s1 = sem("s1_step")
        p1 = sem("p1_step")
        a1 = sem("a1_step")

        def all_blocks(eng, step, lo=0):
            over(eng, lo, NB, RING, lambda b, s, u: step(b, s, u, 128))
            step(NB, NB % RING, NB // RING, TP)

        with ph, nc.Block() as block:
            @block.sync
            def _(sp):
                def load(b, s, u, P):
                    after(sp, z_ready, b - RING + 1)
                    sp.dma_start(xb[s][0:P].rearrange("p g d -> p (g d)"), block_of(xv, b, P)).then_inc(xa_loaded[s], 16)
                    sp.dma_start(ab[s][0:P].rearrange("p g d -> p (g d)"), block_of(aggv, b, P)).then_inc(xa_loaded[s], 16)
                for s in range(RING):
                    load(s, s, 0, 128)
                all_blocks(sp, load, RING)

            @block.vector
            def _(dve):
                def z_block(b, s, u, P):
                    dve.wait_ge(xa_loaded[s], (u + 1) * 32)
                    after(dve, z_used, b - RING + 1)
                    nc.vector.scalar_tensor_tensor(out=zb[s][0:P], in0=xb[s][0:P], scalar=cc[0:P, :], in1=ab[s][0:P],
                                                   op0=ALU.mult, op1=ALU.add).then_inc(z_ready, 1)

                def low(b, s, u, P):
                    dve.wait_ge(hi_ready, b + 1)
                    nc.vector.tensor_tensor(zz[s][0:P, :, D:2 * D], zb[s][0:P], zz[s][0:P, :, 0:D], ALU.subtract).then_inc(lo_ready, 1)

                def step(b, s, u, P):
                    z_block(b, s, u, P)
                    low(b - 1, (s - 1) % RING, None, 128)
                for s in range(RING):
                    z_block(s, s, 0, 128)
                    if s:
                        low(s - 1, s - 1, 0, 128)
                all_blocks(dve, step, RING)
                low(NB, NB % RING, None, TP)

                n = [0]

                def mark(ins):
                    n[0] += 1
                    ins.then_inc(s1, 1)
                    dve.wait_ge(s1, n[0])
                dve.wait_ge(gram_done, 1)
                mark(nc.vector.tensor_copy(mcol[:, 0:2], psum_z[:, 0:2]))
                mark(nc.vector.scalar_tensor_tensor(out=mcol[:, 0:2], in0=psum_z[:, 2:4], scalar=1.0, in1=mcol[:, 0:2],
                                                    op0=ALU.mult, op1=ALU.add))
                mark(nc.vector.tensor_scalar(mcol[:, 0:2], mcol[:, 0:2], 1.0 / N, None, ALU.mult))
                dve.wait_ge(p1, 1)
                mark(nc.vector.tensor_copy(mrow[0:1, :], pm[0:1, 0:D]))
                mark(nc.vector.tensor_copy(prod[:, 0, :], pg[0][:, :]))
                mark(nc.vector.tensor_copy(prod[:, 1, 0:D + 128], pg[1][:, 0:D + 128]))
                mark(nc.vector.scalar_tensor_tensor(out=gram[:, 0, :], in0=prod[:, 0, D:2 * D], scalar=2.0,
                                                    in1=prod[:, 0, 0:D], op0=ALU.mult, op1=ALU.add))
                mark(nc.vector.tensor_tensor(gram[:, 0, 128:D], gram[:, 0, 128:D], prod[:, 0, 128:D], ALU.add))
                mark(nc.vector.tensor_scalar(gram[:, 1, 0:128], prod[:, 1, 128:256], 2.0, None, ALU.mult))
                mark(nc.vector.scalar_tensor_tensor(out=gram[:, 1, 128:D], in0=prod[:, 1, 256:384], scalar=2.0,
                                                    in1=prod[:, 1, 0:128], op0=ALU.mult, op1=ALU.add))
                dve.wait_ge(p1, 2)
                mark(nc.vector.tensor_scalar(gram[:, :, :], gram[:, :, :], 1.0 / N, None, ALU.mult))
                mark(nc.vector.tensor_tensor(gram[:, 0, 0:128], gram[:, 0, 0:128], pm[:, 0:128], ALU.subtract))
                mark(nc.vector.scalar_tensor_tensor(out=gram[:, 0, 128:D], in0=pm[:, 128:D], scalar=-2.0,
                                                    in1=gram[:, 0, 128:D], op0=ALU.mult, op1=ALU.add))
                mark(nc.vector.tensor_tensor(gram[:, 1, 128:D], gram[:, 1, 128:D], pm[:, D + 128:2 * D], ALU.subtract))
                nc.vector.memset(st1[:, 5, :], 0.0).then_inc(a1, 1)
                dve.wait_ge(p1, 3)
                mark(nc.vector.tensor_tensor(prod[:, 0, :], pv[0][:, :], w1f[:, 0, :], ALU.mult))
                mark(nc.vector.tensor_tensor(prod[:, 1, :], pv[1][:, :], w1f[:, 1, :], ALU.mult))
                nc.vector.memset(st1[:, 5, :], 0.0).then_inc(a1, 1)
                dve.wait_ge(p1, 4)
                mark(nc.vector.tensor_scalar(st1[:, 0, :], pst[:, 0:KH], EPS, None, ALU.add))
                mark(nc.vector.tensor_tensor(st1[:, 1, :], pst[:, KH:2 * KH], b1c[:, 0, :], ALU.add))
                nc.vector.memset(st1[:, 5, :], 0.0).then_inc(a1, 1)
                dve.wait_ge(p1, 5)
                mark(nc.vector.reciprocal(st1[:, 3, :], st1[:, 2, :]))
                refine(mark, st1[:, 3, :], st1[:, 0, :], st1[:, 4, :])
                mark(nc.vector.tensor_tensor(st1[:, 3, :], st1[:, 3, :], b1c[:, 1, :], ALU.mult))
                mark(nc.vector.tensor_scalar(scale1[:, :], st1[:, 3, :], 1.0 / WS, None, ALU.mult))
                mark(nc.vector.tensor_tensor(st1[:, 4, :], b1c[:, 0, :], st1[:, 1, :], ALU.subtract))
                mark(nc.vector.tensor_tensor(st1[:, 4, :], st1[:, 4, :], st1[:, 3, :], ALU.mult))
                mark(nc.vector.tensor_tensor(bias1[:, :], st1[:, 4, :], b1c[:, 2, :], ALU.add))

            @block.scalar
            def _(act):
                def high(b, s, u, P):
                    act.wait_ge(z_ready, b + 1)
                    nc.scalar.copy(zz[s][0:P, :, 0:D], zb[s][0:P]).then_inc(hi_ready, 1)
                all_blocks(act, high)
                act.wait_ge(a1, 3)
                nc.scalar.activation(st1[:, 2, :], st1[:, 0, :], ACT.Sqrt).then_inc(p1, 1)

            @block.tensor
            def _(pe):
                for bank in (pg[0], pg[1], psum_z):
                    nc.tensor.matmul(bank[:, :], zeros16[:, 0:128], zeros16[:, :], start=True, stop=False)

                def gram_step(b, s, u, P):
                    pe.wait_ge(lo_ready, b + 1)
                    for g in range(G):
                        for h in range(KD):
                            w = zz[s][0:P, g, h * 128:(h + 1) * 128]
                            m = zz[s][0:P, g, h * 128:2 * D]
                            nc.tensor.matmul(pg[h][:, 0:2 * D - h * 128], w, m, start=False, stop=False, skip_group_check=True)
                            nc.tensor.matmul(psum_z[:, h:h + 1], w, ones16[0:P, :], start=False, stop=False, skip_group_check=True)
                        for h in range(KD):
                            last = nc.tensor.matmul(psum_z[:, 2 + h:3 + h], zz[s][0:P, g, D + h * 128:D + (h + 1) * 128],
                                                    ones16[0:P, :], start=False, stop=False, skip_group_check=True)
                    last.then_inc(z_used, 1)
                all_blocks(pe, gram_step)
                for bank in (pg[0], pg[1], psum_z):
                    last = nc.tensor.matmul(bank[:, :], zeros16[:, 0:128], zeros16[:, :], start=False, stop=True)
                last.then_inc(gram_done, 1)
                pe.wait_ge(s1, 3)
                for h in range(KD):
                    last = nc.tensor.transpose(pm[0:1, h * 128:(h + 1) * 128], mcol[:, h:h + 1], ident[:, :])
                last.then_inc(p1, 1)
                pe.wait_ge(s1, 4)
                for h in range(KD):
                    last = nc.tensor.matmul(pm[:, h * D:(h + 1) * D], mrow[0:1, h * 128:(h + 1) * 128], mrow[0:1, :], start=True, stop=True)
                last.then_inc(p1, 1)
                pe.wait_ge(a1, 1)
                for h in range(KD):
                    for k in range(KD):
                        last = nc.tensor.matmul(pv[h][:, :], gram[:, k, h * 128:(h + 1) * 128], w1f[:, k, :],
                                                start=(k == 0), stop=(k == KD - 1))
                last.then_inc(p1, 1)
                pe.wait_ge(a1, 2)
                for m in range(KH):
                    for k in range(KD):
                        nc.tensor.matmul(pst[:, m:m + 1], prod[:, k, m * 128:(m + 1) * 128], ones[:, 0:1], start=(k == 0), stop=(k == KD - 1))
                    for k in range(KD):
                        last = nc.tensor.matmul(pst[:, KH + m:KH + m + 1], w1f[:, k, m * 128:(m + 1) * 128], mcol[:, k:k + 1],
                                                start=(k == 0), stop=(k == KD - 1))
                last.then_inc(p1, 1)

        ph = ExitStack()
        xb = [sb(f"xc{s}", [128, G, D], f32, ph) for s in range(RING)]
        ab = [sb(f"ac{s}", [128, G, D], f32, ph) for s in range(2)]
        zb = sb("zc", [128, G, D], f32, ph)
        zh = sb("zh", [128, KD, 512], f16, ph)
        zl = sb("zl", [128, KD, 512], f16, ph)
        tf = sb("tf", [128, KH, 512], f32, ph)
        th = [sb(f"th{s}", [128, KH, 512], f16, ph) for s in range(2)]
        tl = [sb(f"tl{s}", [128, KH, 512], f16, ph) for s in range(2)]
        ub = [sb(f"ub{s}", [128, G, D], f32, ph) for s in range(2)]
        sq = sb("sq", [128, G, D], f32, ph)
        usum = sb("usum", [128, G, D], f32, ph)
        qsum = sb("qsum", [128, G, D], f32, ph)
        st2 = sb("st2", [128, 4, D], f32, ph)
        pzt = ps("pzt", KD * 512, ph)
        pt = [ps(f"pt{m}", 512, ph) for m in range(KH)]
        pc = ps("pc", G * D, ph)

        xc_loaded = [sem(f"xc_loaded{s}") for s in range(RING)]
        ac_loaded = [sem(f"ac_loaded{s}") for s in range(2)]
        zc_ready = sem("zc_ready")
        z_turned = sem("z_turned")
        zh_ready = sem("zh_ready")
        zl_ready = sem("zl_ready")
        t_ready = sem("t_ready")
        relu_done = sem("relu_done")
        tl_ready = sem("tl_ready")
        conv_ready = sem("conv_ready")
        u_ready = sem("u_ready")
        sq_ready = sem("sq_ready")
        usum_done = sem("usum_done")
        u_summed = sem("u_summed")
        u_stored = [sem(f"u_stored{s}") for s in range(2)]
        table2_zeroed = sem("table2_zeroed")
        sums_cleared = sem("sums_cleared")
        s2 = sem("s2_step")
        p2 = sem("p2_step")

        with ph, nc.Block() as block:
            @block.sync
            def _(sp):
                def load(b, s, u, P):
                    prev = b - RING + 1
                    after(sp, u_ready, prev)
                    sp.dma_start(xb[s][0:P].rearrange("p g d -> p (g d)"), block_of(xv, b, P)).then_inc(xc_loaded[s], 16)
                    after(sp, zc_ready, b - 1)
                    sp.dma_start(ab[s % 2][0:P].rearrange("p g d -> p (g d)"), block_of(aggv, b, P)).then_inc(ac_loaded[s % 2], 16)
                for s in range(RING):
                    load(s, s, 0, 128)
                per = -(-sh.NZ // ((NB - RING) // RING)) if NB // RING > 2 else sh.NZ
                zeroed = [0]

                def zero(z):
                    sp.dma_start(agg2_z[bass.ds(z, 1)].rearrange("a p r -> (a p) r"), zrows[:, :]).then_inc(table2_zeroed, 16)
                n = (NB - RING) // RING
                per = sh.NZ // n
                with sp.Fori(0, n) as i:
                    for s in range(RING):
                        load(i * RING + (RING + s), s, i + 1, 128)
                    for z in range(per):
                        zero(i * per + z)
                for b in range(RING + n * RING, NB):
                    load(b, b % RING, b // RING, 128)
                load(NB, NB % RING, NB // RING, TP)
                for z in range(n * per, sh.NZ):
                    zero(z)
                sp.wait_ge(table2_zeroed, 16 * sh.NZ)

            @block.tensor
            def _(pe):
                def turn(b, s, P):
                    pe.wait_ge(zc_ready, b + 1)
                    after(pe, zl_ready, b)
                    after(pe, zh_ready, b)
                    for h in range(KD):
                        for g in range(G):
                            last = nc.tensor.transpose(pzt[:, h * 512 + g * P:h * 512 + g * P + P],
                                                       zb[0:P, g, h * 128:(h + 1) * 128], ident[0:P, 0:P])
                    last.then_inc(z_turned, 1)

                def first(b, P):
                    n = G * P
                    pe.wait_ge(zh_ready, b + 1)
                    pe.wait_ge(zl_ready, b + 1)
                    for m in range(KH):
                        after(pe, relu_done, b * KH - (KH - 1 - m))
                        c = slice(m * 128, (m + 1) * 128)
                        terms = [(w1h[:, k, c], zh[:, k, 0:n]) for k in range(KD)]
                        terms += [(w1h[:, k, c], zl[:, k, 0:n]) for k in range(KD)]
                        terms += [(w1l[:, k, c], zh[:, k, 0:n]) for k in range(KD)]
                        for j, (w, mv) in enumerate(terms):
                            last = nc.tensor.matmul(pt[m][:, 0:n], w, mv, start=(j == 0), stop=(j == len(terms) - 1))
                        last.then_inc(t_ready, 1)

                def second(b, s, P):
                    pe.wait_ge(tl_ready, (b + 1) * KH)
                    after(pe, u_ready, b)
                    for g in range(G):
                        c = slice(g * P, (g + 1) * P)
                        o = pc[0:P, g * D:(g + 1) * D]
                        for k in range(KH):
                            nc.tensor.matmul(o, th[s][:, k, c], w2h[:, k, :], start=(k == 0), stop=False)
                            nc.tensor.matmul(o, th[s][:, k, c], w2l[:, k, :], start=False, stop=False)
                            last = nc.tensor.matmul(o, tl[s][:, k, c], w2h[:, k, :], start=False, stop=(k == KH - 1))
                    last.then_inc(conv_ready, 1)

                def step(b, s, u, P=128, nextP=128):
                    first(b, P)
                    turn(b + 1, None, nextP)
                    second(b - 1, (s - 1) % 2, 128)
                turn(0, 0, 128)
                first(0, 128)
                turn(1, 1, 128)
                over(pe, 1, NB - 1, RING, step)
                step(NB - 1, (NB - 1) % RING, None, 128, TP)
                first(NB, TP)
                second(NB - 1, (NB - 1) % 2, 128)
                second(NB, NB % 2, TP)

                pe.wait_ge(s2, 1)
                for j, t in enumerate((usum, qsum)):
                    for g in range(G):
                        last = nc.tensor.matmul(pt[j][:, 0:D], ones[:, :], t[:, g, :], start=(g == 0), stop=(g == G - 1))
                last.then_inc(p2, 1)

            @block.scalar
            def _(act):
                def relus(b, s, u, P):
                    n = G * P
                    b2 = s % 2
                    for m in range(KH):
                        act.wait_ge(t_ready, b * KH + (m + 1))
                        after(act, tl_ready, b * KH - (KH - 1 - m))
                        nc.scalar.activation(tf[:, m, 0:n], pt[m][:, 0:n], ACT.Relu, bias=bias1[:, m:m + 1],
                                             scale=scale1[:, m:m + 1])
                        after(act, conv_ready, b - 1)
                        nc.scalar.activation(th[b2][:, m, 0:n], pt[m][:, 0:n], ACT.Relu, bias=bias1[:, m:m + 1],
                                             scale=scale1[:, m:m + 1]).then_inc(relu_done, 1)

                def high(b, P):
                    n = G * P
                    act.wait_ge(z_turned, b + 1)
                    after(act, t_ready, b * KH)
                    nc.scalar.copy(zh[:, :, 0:n], pzt[:, :].rearrange("p (k n) -> p k n", k=KD)[:, :, 0:n]).then_inc(zh_ready, 1)

                def square(b, s, P):
                    act.wait_ge(u_ready, b + 1)
                    after(act, u_summed, b)
                    nc.scalar.square(sq[0:P], ub[s][0:P]).then_inc(sq_ready, 1)
                    act.dma_start(block_of(uv, b, P), ub[s][0:P].rearrange("p g d -> p (g d)")).then_inc(u_stored[s], 16)

                def step(b, s, u, P=128, nextP=128):
                    relus(b, s, u, P)
                    high(b + 1, nextP)
                    square(b - 1, (s - 1) % 2, 128)
                high(0, 128)
                relus(0, 0, 0, 128)
                high(1, 128)
                over(act, 1, NB - 1, RING, step)
                step(NB - 1, (NB - 1) % RING, None, 128, TP)
                relus(NB, NB % RING, None, TP)
                square(NB - 1, (NB - 1) % 2, 128)
                square(NB, NB % 2, TP)
                for s in range(2):
                    act.wait_ge(u_stored[s], ((NB - s) // 2 + 1) * 16)
                act.wait_ge(s2, 6)
                nc.scalar.activation(st2[:, 3, :], st2[:, 2, :], ACT.Sqrt).then_inc(p2, 1)

            @block.vector
            def _(dve):
                def make_z(b, s, u, P):
                    dve.wait_ge(xc_loaded[s], (u + 1) * 16)
                    dve.wait_ge(ac_loaded[s % 2], (u * (RING // 2) + s // 2 + 1) * 16)
                    after(dve, z_turned, b)
                    nc.vector.scalar_tensor_tensor(out=zb[0:P], in0=xb[s][0:P], scalar=cc[0:P, :], in1=ab[s % 2][0:P],
                                                   op0=ALU.mult, op1=ALU.add).then_inc(zc_ready, 1)

                def low_t(b, s, P):
                    n = G * P
                    for m in range(KH):
                        dve.wait_ge(relu_done, b * KH + (m + 1))
                        after(dve, conv_ready, b - 1)
                        nc.vector.tensor_tensor(tl[s][:, m, 0:n], tf[:, m, 0:n], th[s][:, m, 0:n], ALU.subtract).then_inc(tl_ready, 1)

                def low_z(b, P):
                    n = G * P
                    dve.wait_ge(zh_ready, b + 1)
                    nc.vector.tensor_tensor(zl[:, :, 0:n], pzt[:, :].rearrange("p (k n) -> p k n", k=KD)[:, :, 0:n], zh[:, :, 0:n],
                                            ALU.subtract).then_inc(zl_ready, 1)

                def add_x(b, s4, s, P, use2):
                    dve.wait_ge(conv_ready, b + 1)
                    after(dve, sq_ready, b - 1)
                    after(dve, usum_done, b - 1)
                    after(dve, u_stored[s], use2 * 16)
                    nc.vector.scalar_tensor_tensor(out=ub[s][0:P], in0=pc[0:P, :].rearrange("p (g d) -> p g d", g=G), scalar=1.0 / WS,
                                                   in1=xb[s4][0:P], op0=ALU.mult, op1=ALU.add).then_inc(u_ready, 1)

                def use_of(s, u):
                    return u * (RING // 2) + (s - 1) // 2

                def step(b, s, u, P=128, nextP=128):
                    make_z(b + 1, (s + 1) % RING, u + (s + 1) // RING, nextP)
                    low_t(b, s % 2, P)
                    low_z(b + 1, nextP)
                    add_x(b - 1, (s - 1) % RING, (s - 1) % 2, 128, use_of(s, u))
                make_z(0, 0, 0, 128)
                low_z(0, 128)
                make_z(1, 1, 0, 128)
                low_t(0, 0, 128)
                low_z(1, 128)
                over(dve, 1, NB - 1, RING, step)
                step(NB - 1, (NB - 1) % RING, (NB - 1) // RING, 128, TP)
                low_t(NB, NB % 2, TP)
                add_x(NB - 1, (NB - 1) % RING, (NB - 1) % 2, 128, (NB - 1) // 2)
                add_x(NB, NB % RING, NB % 2, TP, NB // 2)

                n = [1]

                def mark(ins):
                    n[0] += 1
                    ins.then_inc(s2, 1)
                    dve.wait_ge(s2, n[0])
                dve.wait_ge(p2, 1)
                mark(nc.vector.tensor_scalar(st2[:, 0, :], pt[0][:, 0:D], 1.0 / N, None, ALU.mult))
                mark(nc.vector.tensor_scalar(st2[:, 1, :], pt[1][:, 0:D], 1.0 / N, None, ALU.mult))
                mark(nc.vector.tensor_tensor(st2[:, 2, :], st2[:, 0, :], st2[:, 0, :], ALU.mult))
                mark(nc.vector.tensor_tensor(st2[:, 2, :], st2[:, 1, :], st2[:, 2, :], ALU.subtract))
                mark(nc.vector.tensor_scalar(st2[:, 2, :], st2[:, 2, :], 0.0, EPS, ALU.max, ALU.add))
                mark(nc.vector.tensor_tensor(st2[:, 0, :], st2[:, 0, :], rows2[:, 0, :], ALU.add))
                dve.wait_ge(p2, 2)
                mark(nc.vector.reciprocal(st2[:, 1, :], st2[:, 3, :]))
                refine(mark, st2[:, 1, :], st2[:, 2, :], st2[:, 3, :])
                mark(nc.vector.tensor_tensor(scale2[:, :], st2[:, 1, :], rows2[:, 1, :], ALU.mult))
                mark(nc.vector.tensor_tensor(st2[:, 2, :], rows2[:, 0, :], st2[:, 0, :], ALU.subtract))
                mark(nc.vector.tensor_tensor(st2[:, 2, :], st2[:, 2, :], scale2[:, :], ALU.mult))
                mark(nc.vector.tensor_tensor(bias2[:, :], st2[:, 2, :], rows2[:, 2, :], ALU.add))

            @block.gpsimd
            def _(pool):
                nc.gpsimd.memset(usum[:, :, :], 0.0)
                nc.gpsimd.memset(qsum[:, :, :], 0.0).then_inc(sums_cleared, 1)
                pool.wait_ge(sums_cleared, 1)

                def summed(b, s, P):
                    pool.wait_ge(u_ready, b + 1)
                    after(pool, usum_done, b)
                    nc.gpsimd.tensor_tensor(usum[0:P], usum[0:P], ub[s][0:P], ALU.add).then_inc(usum_done, 1)
                    pool.wait_ge(sq_ready, b + 1)
                    after(pool, u_summed, b)
                    nc.gpsimd.tensor_tensor(qsum[0:P], qsum[0:P], sq[0:P], ALU.add).then_inc(u_summed, 1)

                over(pool, 0, NB, RING, lambda b, s, u: summed(b, s % 2, 128))
                summed(NB, NB % 2, TP)
                pool.wait_ge(u_summed, NB + 1)
                pool.sem_inc(s2, 1)

        ph = ExitStack()
        rx = [sb(f"rx{s}", [128, K, D], f32, ph) for s in range(ERING)]
        ru = [sb(f"ru{s}", [128, K, D], f32, ph) for s in range(ERING)]
        msg = [sb(f"msg{s}", [128, K, D], f32, ph) for s in range(ERING)]
        sums = [sb(f"msums{s}", [128, K, D], f32, ph) for s in range(ERING)]
        turned = sb("turned", [128, KD, K * 128], f32, ph)
        sel = [sb(f"msel{s}", [128, K, K * 128], f32, ph) for s in range(ERING)]
        diag = sb("mdiag", [128, K, 128], f32, ph)
        junk = sb("mjunk", [128, K, K * 128], f16, ph)
        cnt = sb("mcnt", [128, 3, K], f32, ph)
        target = [sb(f"mtarget{s}", [128, K], i32, ph) for s in range(ERING)]
        stat = sb("mstat", [128, K, 6], f32, ph)
        mv = sb("mmv", [128, K, 2], f32, ph)
        mrs = sb("mrs", [128, 4, K], f32, ph)
        keyrow = ps("mkeyrow", K * 128, ph)
        pturn = ps("pturn", KD * K * 128, ph)
        comb = ps("mcomb", K * D, ph)

        xu_gathered = [sem(f"xu_gathered{s}") for s in range(ERING)]
        m_picked = sem("m_picked")
        m_spread = sem("m_spread")
        m_row = sem("m_row")
        m_sel = sem("m_sel")
        m_cnt = sem("m_cnt")
        m_target = sem("m_target")
        m_a = sem("m_scaled")
        m_b = sem("m_shifted")
        m_y = sem("m_y")
        m_s = sem("m_stats")
        m_mv = sem("m_mv")
        m_sd = sem("m_sd")
        m_inv = sem("m_inv")
        m_w = sem("m_w")
        m_n1 = sem("m_n1")
        m_n2 = sem("m_n2")
        m_rstd = sem("m_rstd")
        m_msg = sem("m_msg")
        m_pt = sem("m_pturn")
        m_turned = sem("m_turned")
        m_comb = sem("m_comb")
        m_sums = sem("m_sums")
        m_added = [sem(f"m_added{s}") for s in range(ERING)]

        with ph, nc.Block() as block:
            @block.gpsimd
            def _(pool):
                def gather(g, slot, use):
                    after(pool, m_msg, g - ERING + 1)
                    pool.sem_inc(pool_passed, 1)
                    nc.gpsimd.tensor_copy(picked[slot][:, :], gdst[:, bass.ds(g * K, K)]).then_inc(m_picked, 1)
                    pool.wait_ge(m_picked, g + 1)
                    pool.sem_inc(pool_passed, 1)
                    for k in range(K):
                        for to, of in ((rx, x), (ru, ubuf)):
                            pool.indirect_dma_start(to[slot][:, k, :], None, of,
                                                    IOA(ap=picked[slot][:, k:k + 1], axis=0)).then_inc(xu_gathered[slot], 16)

                def add(g, slot, use):
                    pool.wait_ge(m_sums, g + 1)
                    pool.wait_ge(m_target, g + 1)
                    before_s, before_u = back(slot, use, 1)
                    after(pool, m_added[before_s], (before_u + 1) * (16 * K))
                    pool.sem_inc(pool_passed, 1)
                    for k in range(K):
                        pool.indirect_dma_start(agg2, IOA(ap=target[slot][:, k:k + 1], axis=0), sums[slot][:, k, :], None,
                                                compute_op=ALU.add).then_inc(m_added[slot], 16)

                def both(g, slot, use):
                    gather(g + 2, *back(slot, use, -2))
                    add(g - 2, *back(slot, use, 2))

                for g in range(4):
                    gather(g, g, 0)
                over(pool, 2, NG - 2, ERING, both)
                for g in range(NG - 4, NG):
                    add(g, g % ERING, g // ERING)
                pool.wait_ge(m_added[g % ERING], (g // ERING + 1) * 16 * K)

            @block.vector
            def _(dve):
                names = (m_spread, m_row, m_sel, m_cnt, m_target, sel, keyrow, target, cnt, junk, diag)
                sc = scale2[:, :].unsqueeze(1).to_broadcast([128, K, D])
                bi = bias2[:, :].unsqueeze(1).to_broadcast([128, K, D])

                def normed(g, slot, use):
                    dve.wait_ge(xu_gathered[slot], (use + 1) * (32 * K))
                    nc.vector.tensor_tensor(ru[slot][:, :, :], ru[slot][:, :, :], sc, ALU.mult).then_inc(m_a, 1)
                    dve.wait_ge(m_a, g + 1)
                    nc.vector.tensor_tensor(ru[slot][:, :, :], ru[slot][:, :, :], bi, ALU.add).then_inc(m_b, 1)
                    dve.wait_ge(m_b, g + 1)
                    nc.vector.scalar_tensor_tensor(out=rx[slot][:, :, :], in0=ru[slot][:, :, :], scalar=0.0, in1=rx[slot][:, :, :],
                                                   op0=ALU.max, op1=ALU.add).then_inc(m_y, 1)
                    dve.wait_ge(m_y, g + 1)
                    for k in range(K):
                        last = nc.vector.bn_stats(stat[:, k, :], rx[slot][:, k, :])
                    last.then_inc(m_s, 1)
                    dve.wait_ge(m_s, g + 1)
                    dve.sem_inc(dve_passed, 1)
                    for k in range(K):
                        last = nc.vector.bn_aggr(mv[:, k, :], stat[:, k, :])
                    last.then_inc(m_mv, 1)

                def scales(g):
                    dve.wait_ge(m_sd, g + 1)
                    after(dve, m_msg, g)
                    r, t = mrs[:, 1, :], mrs[:, 3, :]
                    nc.vector.reciprocal(r, mrs[:, 0, :]).then_inc(m_inv, 1)
                    dve.wait_ge(m_inv, g + 1)
                    nc.vector.scalar_tensor_tensor(out=t, in0=mv[:, :, 1], scalar=EPS, in1=r, op0=ALU.add, op1=ALU.mult).then_inc(m_n1, 1)
                    dve.wait_ge(m_n1, g * 2 + 1)
                    nc.vector.scalar_tensor_tensor(out=t, in0=t, scalar=-0.5, in1=r, op0=ALU.mult, op1=ALU.mult).then_inc(m_n1, 1)
                    dve.wait_ge(m_n1, g * 2 + 2)
                    nc.vector.scalar_tensor_tensor(out=r, in0=t, scalar=1.5, in1=r, op0=ALU.add, op1=ALU.mult).then_inc(m_n2, 1)
                    dve.wait_ge(m_n2, g + 1)
                    nc.vector.tensor_tensor(r, r, wgt[:, bass.ds(g * K, K)], ALU.mult).then_inc(m_w, 1)
                    dve.wait_ge(m_w, g + 1)
                    nc.vector.scalar_tensor_tensor(out=mrs[:, 2, :], in0=mv[:, :, 0], scalar=-1.0, in1=r,
                                                   op0=ALU.mult, op1=ALU.mult).then_inc(m_rstd, 1)

                def group(g, slot, use, more=True):
                    normed(g, slot, use)
                    dve.wait_ge(m_row, g + 1)
                    if more:
                        spread_keys(g + 1, ksrc, diag, m_spread)
                    after(dve, m_comb, g - ERING + 1)
                    after(dve, m_added[slot], use * (16 * K))
                    select_edges(dve, g, slot, ksrc, names)
                    scales(g)

                spread_keys(0, ksrc, diag, m_spread)
                over(dve, 0, NG - 1, ERING, group)
                group(NG - 1, (NG - 1) % ERING, (NG - 1) // ERING, False)

            @block.scalar
            def _(act):
                def deviation(g):
                    act.wait_ge(m_mv, g + 1)
                    nc.scalar.activation(mrs[:, 0, :], mv[:, :, 1], ACT.Sqrt, bias=epsc[:, :]).then_inc(m_sd, 1)

                def message(g, slot):
                    act.wait_ge(m_rstd, g + 1)
                    after(act, m_pt, g - ERING + 1)
                    for k in range(K):
                        last = nc.scalar.activation(msg[slot][:, k, :], rx[slot][:, k, :], ACT.Identity,
                                                    bias=mrs[:, 2, k:k + 1], scale=mrs[:, 1, k:k + 1])
                    last.then_inc(m_msg, 1)

                def turn(g):
                    act.wait_ge(m_pt, g + 1)
                    after(act, m_comb, g)
                    nc.scalar.copy(turned[:, :, :], pturn[:, :].rearrange("p (h j) -> p h j", h=KD)).then_inc(m_turned, 1)

                def evacuate(g, slot, use):
                    act.wait_ge(m_comb, g + 1)
                    after(act, m_added[slot], use * (16 * K))
                    nc.scalar.copy(sums[slot][:, :, :], comb[:, :].rearrange("p (k d) -> p k d", k=K)).then_inc(m_sums, 1)

                def step(g, slot, use):
                    turn(g - 1)
                    deviation(g)
                    evacuate(g - 1, *back(slot, use, 1))
                    message(g, slot)
                deviation(0)
                message(0, 0)
                over(act, 1, NG, ERING, step)
                turn(NG - 1)
                evacuate(NG - 1, (NG - 1) % ERING, (NG - 1) // ERING)

            @block.tensor
            def _(pe):
                def spread(g):
                    pe.wait_ge(m_spread, g + 1)
                    nc.tensor.matmul(keyrow[:, :], ones[:, :], diag[:, :, :].rearrange("p k j -> p (k j)"),
                                     start=True, stop=True).then_inc(m_row, 1)

                def combine(g, slot):
                    pe.wait_ge(m_sel, g + 1)
                    pe.wait_ge(m_msg, g + 1)
                    after(pe, m_turned, g)
                    for h in range(KD):
                        for j in range(K):
                            last = nc.tensor.matmul(pturn[:, h * K * 128:(h + 1) * K * 128], msg[slot][:, j, h * 128:(h + 1) * 128],
                                                    sel[slot][:, j, :], start=(j == 0), stop=(j == K - 1))
                    last.then_inc(m_pt, 1)
                    pe.wait_ge(m_turned, g + 1)
                    after(pe, m_sums, g)
                    for k in range(K):
                        for h in range(KD):
                            last = nc.tensor.matmul(comb[:, k * D:(k + 1) * D], turned[:, h, k * 128:(k + 1) * 128], lwt[:, h, :],
                                                    start=(h == 0), stop=(h == KD - 1))
                    last.then_inc(m_comb, 1)

                def group(g, slot, use):
                    after(pe, m_target, g)
                    spread(g)
                    combine(g - 1, (slot - 1) % ERING)
                spread(0)
                over(pe, 1, NG, ERING, group)
                combine(NG - 1, (NG - 1) % ERING)

        ph = ExitStack()
        un = [sb(f"un{s}", [128, G, D], f32, ph) for s in range(NRING)]
        xn = [sb(f"xn{s}", [128, G, D], f32, ph) for s in range(NRING)]
        an = [sb(f"an{s}", [128, G, D], f32, ph) for s in range(NRING)]
        on = [sb(f"on{s}", [128, G, D], f32, ph) for s in range(2)]
        nst = sb("nst", [128, 2, G, 6], f32, ph)
        nmv = sb("nmv", [128, 2, G, 2], f32, ph)
        nsd = sb("nsd", [128, 2, G], f32, ph)
        nrs = sb("nrs", [128, 2, 3, G], f32, ph)
        pv2 = [ps(f"pv2{s}", G * D, ph) for s in range(3)]
        n_loaded = [sem(f"n_loaded{s}") for s in range(NRING)]
        n_scaled = sem("n_scaled")
        n_shift = sem("n_shifted")
        n_y = sem("n_y")
        n_s = [sem(f"n_stats{j}") for j in range(2)]
        n_mv = [sem(f"n_mv{j}") for j in range(2)]
        n_sd = [sem(f"n_sd{j}") for j in range(2)]
        n_inv = [sem(f"n_inv{j}") for j in range(2)]
        n_t = [sem(f"n_t{j}") for j in range(2)]
        n_new = [sem(f"n_new{j}") for j in range(2)]
        n_rstd = [sem(f"n_rstd{j}") for j in range(2)]
        n_x1 = sem("n_x1")
        n_v = sem("n_v")
        n_out = sem("n_out")
        n_stored = [sem(f"n_stored{s}") for s in range(2)]

        def norm_blocks(eng, step, lo=0):
            over(eng, lo, NB, NRING, lambda b, s, u: step(b, s, u, 128))
            step(NB, NB % NRING, NB // NRING, TP)

        with ph, nc.Block() as block:
            @block.sync
            def _(sp):
                def load(b, s, u, P):
                    after(sp, n_v, b - NRING + 1)
                    for to, of in ((un, uv), (xn, xv), (an, agg2v)):
                        sp.dma_start(to[s][0:P].rearrange("p g d -> p (g d)"), block_of(of, b, P)).then_inc(n_loaded[s], 16)
                norm_blocks(sp, load)

            @block.gpsimd
            def _(pool):
                sc = scale2[:, :].unsqueeze(1).to_broadcast([128, G, D])
                bi = bias2[:, :].unsqueeze(1).to_broadcast([128, G, D])

                def bn(b, s, u, P):
                    pool.wait_ge(n_loaded[s], (u + 1) * 48)
                    nc.gpsimd.tensor_tensor(un[s][0:P], un[s][0:P], sc[0:P], ALU.mult).then_inc(n_scaled, 1)
                    pool.wait_ge(n_scaled, b + 1)
                    nc.gpsimd.tensor_tensor(un[s][0:P], un[s][0:P], bi[0:P], ALU.add).then_inc(n_shift, 1)
                norm_blocks(pool, bn)

            @block.tensor
            def _(pe):
                def v(b, s, u, P):
                    pe.wait_ge(n_x1, b + 1)
                    after(pe, n_out, b - 2)
                    for g in range(G):
                        o = pv2[s % 3][0:P, g * D:(g + 1) * D]
                        nc.tensor.matmul(o, ident[0:P, 0:P], an[s][0:P, g, :], start=True, stop=False)
                        last = nc.tensor.matmul(o, ident[0:P, 0:P], xn[s][0:P, g, :], start=False, stop=True)
                    last.then_inc(n_v, 1)
                norm_blocks(pe, v)

            @block.vector
            def _(dve):
                def inverse(b, j, P):
                    r, m, t = (nrs[0:P, j, i, :] for i in range(3))

                    def first():
                        dve.wait_ge(n_sd[j], b + 1)
                        after(dve, n_x1 if j == 0 else n_out, b)
                        nc.vector.reciprocal(r, nsd[0:P, j, :]).then_inc(n_inv[j], 1)

                    def second():
                        dve.wait_ge(n_inv[j], b + 1)
                        nc.vector.scalar_tensor_tensor(out=t, in0=nmv[0:P, j, :, 1], scalar=EPS, in1=r,
                                                       op0=ALU.add, op1=ALU.mult).then_inc(n_t[j], 1)

                    def third():
                        dve.wait_ge(n_t[j], b * 2 + 1)
                        nc.vector.scalar_tensor_tensor(out=t, in0=t, scalar=-0.5, in1=r,
                                                       op0=ALU.mult, op1=ALU.mult).then_inc(n_t[j], 1)

                    def fourth():
                        dve.wait_ge(n_t[j], b * 2 + 2)
                        nc.vector.scalar_tensor_tensor(out=r, in0=t, scalar=1.5, in1=r,
                                                       op0=ALU.add, op1=ALU.mult).then_inc(n_new[j], 1)

                    def fifth():
                        dve.wait_ge(n_new[j], b + 1)
                        nc.vector.scalar_tensor_tensor(out=m, in0=nmv[0:P, j, :, 0], scalar=-1.0, in1=r,
                                                       op0=ALU.mult, op1=ALU.mult).then_inc(n_rstd[j], 1)
                    return [first, second, third, fourth, fifth]

                def add_x(b, s, P):
                    dve.wait_ge(n_shift, b + 1)
                    nc.vector.scalar_tensor_tensor(out=xn[s][0:P], in0=un[s][0:P], scalar=0.0, in1=xn[s][0:P],
                                                   op0=ALU.max, op1=ALU.add).then_inc(n_y, 1)

                def stats(b, j, tile, P, between):
                    for g in range(G):
                        last = nc.vector.bn_stats(nst[0:P, j, g, :], tile(g))
                        if between:
                            between.pop(0)()
                    last.then_inc(n_s[j], 1)

                def gather_stats(b, j, P):
                    dve.wait_ge(n_s[j], b + 1)
                    dve.sem_inc(dve_passed, 1)
                    for g in range(G):
                        last = nc.vector.bn_aggr(nmv[0:P, j, g, :], nst[0:P, j, g, :])
                    last.then_inc(n_mv[j], 1)

                def y_stats(b, s, P, between):
                    dve.wait_ge(n_y, b + 1)
                    stats(b, 0, lambda g: xn[s][0:P, g, :], P, between)

                def v_stats(b, s, P, between):
                    dve.wait_ge(n_v, b + 1)
                    stats(b, 1, lambda g: pv2[s % 3][0:P, g * D:(g + 1) * D], P, between)

                def step(b, s, P):
                    small = inverse(b - 3, 1, 128)
                    add_x(b, s, P)
                    small.pop(0)()
                    y_stats(b, s, P, small)
                    gather_stats(b, 0, P)
                    small = inverse(b, 0, P)
                    v_stats(b - 2, (s - 2) % NRING, 128, small)
                    small.pop(0)()
                    gather_stats(b - 2, 1, 128)

                def all_of(steps):
                    for small in steps:
                        small()

                for b in range(3):
                    add_x(b, b, 128)
                    y_stats(b, b, 128, [])
                    gather_stats(b, 0, 128)
                    all_of(inverse(b, 0, 128))
                    if b == 2:
                        v_stats(0, 0, 128, [])
                        gather_stats(0, 1, 128)
                over(dve, 3, NB, NRING, lambda b, s, u: step(b, s, 128))
                step(NB, NB % NRING, TP)
                all_of(inverse(NB - 2, 1, 128))
                for b, P in ((NB - 1, 128), (NB, TP)):
                    v_stats(b, b % NRING, P, [])
                    gather_stats(b, 1, P)
                    all_of(inverse(b, 1, P))

            @block.scalar
            def _(act):
                def norm(to, tile, j, P, done):
                    for g in range(G):
                        last = nc.scalar.activation(to[0:P, g, :], tile(g), ACT.Identity,
                                                    bias=nrs[0:P, j, 1, g:g + 1], scale=nrs[0:P, j, 0, g:g + 1])
                    last.then_inc(done, 1)

                def deviation(b, j, P):
                    act.wait_ge(n_mv[j], b + 1)
                    nc.scalar.activation(nsd[0:P, j, :], nmv[0:P, j, :, 1], ACT.Sqrt, bias=epsc[0:P, :]).then_inc(n_sd[j], 1)

                def x1(b, s, P):
                    act.wait_ge(n_rstd[0], b + 1)
                    norm(xn[s], lambda g: xn[s][0:P, g, :], 0, P, n_x1)

                def result(b, s, u, P):
                    act.wait_ge(n_rstd[1], b + 1)
                    after(act, n_stored[s % 2], u * (NRING // 2 * 16) + (s // 2 * 16))
                    norm(on[s % 2], lambda g: pv2[s % 3][0:P, g * D:(g + 1) * D], 1, P, n_out)
                    act.wait_ge(n_out, b + 1)
                    act.dma_start(block_of(outv, b, P), on[s % 2][0:P].rearrange("p g d -> p (g d)")).then_inc(n_stored[s % 2], 16)

                def step(b, s, u, P):
                    x1(b - 1, (s - 1) % NRING, 128)
                    deviation(b, 0, P)
                    result(b - 3, (s - 3) % NRING, u + (s - 3) // NRING, 128)
                    deviation(b - 2, 1, 128)
                deviation(0, 0, 128)
                x1(0, 0, 128)
                deviation(1, 0, 128)
                x1(1, 1, 128)
                deviation(2, 0, 128)
                deviation(0, 1, 128)
                over(act, 3, NB, NRING, lambda b, s, u: step(b, s, u, 128))
                step(NB, NB % NRING, NB // NRING, TP)
                x1(NB, NB % NRING, TP)
                result(NB - 2, (NB - 2) % NRING, (NB - 2) // NRING, 128)
                for b, P in ((NB - 1, 128), (NB, TP)):
                    deviation(b, 1, P)
                    result(b, b % NRING, b // NRING, P)
                for s in range(2):
                    act.wait_ge(n_stored[s], ((NB - s) // 2 + 1) * 16)


_INS = ['x', 'src', 'dst', 'edge_weight', 'L0_gnn_W1', 'L0_gnn_b1', 'L0_gnn_g1', 'L0_gnn_bt1', 'L0_gnn_W2', 'L0_gnn_b2',
        'L0_gnn_g2', 'L0_gnn_bt2', 'L0_gnn_eps_gin', 'L1_gnn_W']


def kernel(**inputs):
    import numpy as _np
    import concourse.bacc as _bacc
    from concourse import mybir as _mybir
    from concourse.bass_utils import run_bass_kernel_spmd as _run

    nc = _bacc.Bacc("TRN2", target_bir_lowering=False, num_devices=1)
    arrays, args = {}, []
    for name in _INS:
        a = _np.ascontiguousarray(inputs[name])
        a = a.reshape(a.shape or (1,))
        arrays[f"in_{name}"] = a
        args.append(nc.dram_tensor(f"in_{name}", a.shape, _mybir.dt.from_np(a.dtype), kind="ExternalInput").ap())
    shape = _np.shape(inputs['x'])
    o = nc.dram_tensor("out_dram", shape, _mybir.dt.float32, kind="ExternalOutput").ap()
    gnn(nc, *args, o)
    r = _run(nc, [arrays], core_ids=[0])
    return r.results[0]["out_dram"]
```

```python
import concourse.bass as bass
from concourse import mybir
from contextlib import ExitStack

f32 = mybir.dt.float32
f16 = mybir.dt.float16
i32 = mybir.dt.int32
ALU = mybir.AluOpType
ACT = mybir.ActivationFunctionType
IOA = bass.IndirectOffsetOnAxis

EPS = 1e-5
WS = 64.0
K = 2
G = 4
RING = 4
NRING = 6
XRING = 12
ERING = 4


class Shapes:

    def __init__(s, n, d, h, e):
        s.N, s.D, s.H, s.E = n, d, h, e
        s.KD, s.KH = d // 128, h // 128
        s.BR = 128 * G
        s.NB = n // s.BR
        s.TP = (n - s.NB * s.BR) // G
        assert s.NB * s.BR + s.TP * G == n and 0 < s.TP < 128
        s.C = -(-e // (128 * K)) * K
        s.NG = s.C // K
        assert s.NG >= -(-s.NB // 2)
        s.ZR = 8
        s.NZ = -(-(n + 1 + K * 128) // (128 * s.ZR))
        s.T = s.NZ * 128 * s.ZR


def over(eng, lo, hi, unroll, step):
    first = max(lo, 2 * unroll)
    n = (hi - first) // unroll
    if n < 2:
        first, n = hi, 0
    for b in range(lo, first):
        step(b, b % unroll, b // unroll)
    if n:
        with eng.Fori(0, n) as i:
            for s in range(unroll):
                b = first + s
                step(i * unroll + b, b % unroll, i + b // unroll)
    for b in range(first + n * unroll, hi):
        step(b, b % unroll, b // unroll)


def back(slot, use, d):
    return (slot - d) % ERING, use + (slot - d) // ERING


def after(eng, sem, value):
    if not isinstance(value, int) or value > 0:
        eng.wait_ge(sem, value)


def row_blocks(ap, sh):
    full = ap[0:sh.NB * sh.BR, :].rearrange("(b p g) d -> b p (g d)", p=128, g=G)
    tail = ap[sh.NB * sh.BR:sh.N, :].rearrange("(p g) d -> p (g d)", g=G)
    return full, tail


def block_of(views, b, P):
    full, tail = views
    return full[bass.ds(b, 1)].rearrange("a p d -> (a p) d") if P == 128 else tail


def gnn(nc, x, src, dst, ew, W1, b1, g1, bt1, W2, b2, g2, bt2, eps_gin, LW, out):
    sh = Shapes(x.shape[0], x.shape[1], W1.shape[1], src.shape[0])
    N, D, H, E, C, NG, NB, TP = sh.N, sh.D, sh.H, sh.E, sh.C, sh.NG, sh.NB, sh.TP
    KD, KH = sh.KD, sh.KH
    agg = nc.dram_tensor("agg", (sh.T, D), f32).ap()
    agg2 = nc.dram_tensor("agg2", (sh.T, D), f32).ap()
    ubuf = nc.dram_tensor("ubuf", (N, D), f32).ap()
    xdst = nc.dram_tensor("xdst", (NG, 128, K * D), f32).ap()
    agg_z = agg.rearrange("(z p r) d -> z p (r d)", p=128, r=sh.ZR)
    agg2_z = agg2.rearrange("(z p r) d -> z p (r d)", p=128, r=sh.ZR)
    xv, aggv, agg2v, uv, outv = (row_blocks(t, sh) for t in (x, agg, agg2, ubuf, out))
    whole = ExitStack()
    with whole:
        def sb(name, shape, dt, scope=whole):
            return scope.enter_context(nc.sbuf_tensor(name, shape, dt))

        def ps(name, cols, scope):
            return scope.enter_context(nc.psum_tensor(name, [128, cols], f32))

        def sem(name):
            return whole.enter_context(nc.semaphore(name))

        ident = sb("ident", [128, 128], f32)
        ones = sb("ones", [128, 128], f32)
        ones16 = sb("ones16", [128, 1], f16)
        zeros16 = sb("zeros16", [128, 512], f16)
        zrows = sb("zrows", [128, sh.ZR * D], f32)
        w1f = sb("w1f", [128, KD, H], f32)
        w1h = sb("w1h", [128, KD, H], f16)
        w1l = sb("w1l", [128, KD, H], f16)
        w2h = sb("w2h", [128, KH, D], f16)
        w2l = sb("w2l", [128, KH, D], f16)
        lwt = sb("lwt", [128, KD, D], f32)
        cc = sb("cc", [128, 1], f32)
        b1c = sb("b1c", [128, 3, KH], f32)
        scale1 = sb("scale1", [128, KH], f32)
        bias1 = sb("bias1", [128, KH], f32)
        rows2 = sb("rows2", [128, 3, D], f32)
        scale2 = sb("scale2", [128, D], f32)
        bias2 = sb("bias2", [128, D], f32)
        gsrc = sb("gsrc", [128, C], i32)
        gdst = sb("gdst", [128, C], i32)
        key_i = sb("key_i", [128, 2, C], i32)
        kdst = sb("kdst", [128, C], f32)
        ksrc = sb("ksrc", [128, C], f32)
        wgt = sb("wgt", [128, C], f32)
        tdst = sb("tdst", [128, C], i32)
        tsrc = sb("tsrc", [128, C], i32)
        picked = [sb(f"picked{s}", [128, K], i32) for s in range(ERING)]
        epsc = sb("epsc", [128, 1], f32)
        before = sb("before", [128, K, K * 128], f32)
        spare = sb("spare", [128, K], f32)
        spare_i = sb("spare_i", [128, K], i32)

        def refine(mark, r, var, tmp):
            mark(nc.vector.tensor_tensor(tmp, var, r, ALU.mult))
            mark(nc.vector.scalar_tensor_tensor(out=tmp, in0=tmp, scalar=-0.5, in1=r, op0=ALU.mult, op1=ALU.mult))
            mark(nc.vector.scalar_tensor_tensor(out=r, in0=tmp, scalar=1.5, in1=r, op0=ALU.add, op1=ALU.mult))

        next_ph = ExitStack()
        xb = [sb(f"xb{s}", [128, G, D], f32, next_ph) for s in range(XRING)]
        x_loaded = [sem(f"x_loaded{s}") for s in range(XRING)]
        ph = ExitStack()
        w2f = sb("w2f", [128, KH, D], f32, ph)
        lwf = sb("lwf", [128, KD, D], f32, ph)
        rows_x = [sb(f"rows_x{s}", [128, K, D], f32, ph) for s in range(ERING)]
        sums = [sb(f"sums{s}", [128, K, D], f32, ph) for s in range(ERING)]
        sel = [sb(f"sel{s}", [128, K, K * 128], f32, ph) for s in range(ERING)]
        diag = sb("diag", [128, K, 128], f32, ph)
        junk = sb("junk", [128, K, K * 128], f16, ph)
        cnt = sb("cnt", [128, 2, C], f32, ph)
        diff = sb("diff", [128, C], f32, ph)
        diag2 = sb("diag2", [128, K, 128], f32, ph)
        target = [sb(f"target{s}", [128, K], i32, ph) for s in range(ERING)]
        keyrow = [ps(f"keyrow{s}", 512, ph) for s in range(2)]
        srcrow = ps("srcrow", 512, ph)
        comb = ps("comb", K * D, ph)
        lwp = ps("lwp", 512, ph)

        pool_passed, dve_passed = sem("pool_passed"), sem("dve_passed")
        const_loaded = sem("const_loaded")
        idx_cleared = sem("idx_cleared")
        idx_loaded = sem("idx_loaded")
        consts_made = sem("consts_made")
        pool_consts = sem("pool_consts")
        dve_c = sem("dve_c")
        lw_turned = sem("lw_turned")
        table_zeroed = sem("table_zeroed")
        x_gathered = [sem(f"x_gathered{s}") for s in range(ERING)]
        keys_spread = sem("keys_spread")
        keyrow_ready = sem("keyrow_ready")
        sel_ready = sem("sel_ready")
        cnt_spread = sem("cnt_spread")
        cnt_row = sem("cnt_row")
        cnt_ready = sem("cnt_ready")
        src_spread = sem("src_spread")
        src_row = sem("src_row")
        rows_picked = sem("rows_picked")
        comb_ready = sem("comb_ready")
        sums_ready = sem("sums_ready")
        sums_added = sem("sums_added")

        full_p, rest = E // C, E % C

        def load_edges(eng, to, ap):
            eng.dma_start(to[0:full_p, :], ap[0:full_p * C].rearrange("(p c) -> p c", c=C)).then_inc(idx_loaded, 16)
            n = 1
            if rest:
                eng.dma_start(to[full_p:full_p + 1, 0:rest],
                              ap[full_p * C:E].rearrange("(a c) -> a c", a=1)).then_inc(idx_loaded, 16)
                n = 2
            return n

        IDX_LOADS = 5 * (2 if rest else 1)

        def group_columns(g):
            return bass.ds(g * K, K)

        def spread_keys(g, keys, dg, done):
            nc.vector.tensor_tensor(dg[:, :, :], ident[:, :].unsqueeze(1).to_broadcast([128, K, 128]),
                                    keys[:, group_columns(g)].unsqueeze(2).to_broadcast([128, K, 128]),
                                    ALU.mult).then_inc(done, 1)

        def key_row(g, row, dg, done):
            nc.tensor.matmul(row[:, 0:K * 128], ones[:, :], dg[:, :, :].rearrange("p k j -> p (k j)"),
                             start=True, stop=True).then_inc(done, 1)

        def select_chunk(g, k, keys, row, to):
            return nc.vector.tensor_scalar(to[:, k, :], row[:, 0:K * 128], keys[:, bass.ds(g * K + k, 1)], None, ALU.is_equal)

        with ph, nc.Block() as block:
            @block.sync
            def _(sp):
                sp.wait_ge(consts_made, 1)

                def zero(z, slot, use):
                    sp.dma_start(agg_z[bass.ds(z, 1)].rearrange("a p r -> (a p) r"), zrows[:, :]).then_inc(table_zeroed, 16)

                over(sp, 0, sh.NZ, RING, zero)
                sp.wait_ge(table_zeroed, 16 * sh.NZ)
                for s in range(XRING):
                    sp.wait_ge(sums_ready, min(3 * s + 1, NG))
                    sp.dma_start(xb[s][:, :, :].rearrange("p g d -> p (g d)"), block_of(xv, s, 128)).then_inc(x_loaded[s], 16)

            @block.scalar
            def _(act):
                act.dma_start(w1f[:, :, :], W1.rearrange("(k p) n -> p k n", p=128)).then_inc(const_loaded, 16)
                act.dma_start(w2f[:, :, :], W2.rearrange("(k p) n -> p k n", p=128)).then_inc(const_loaded, 16)
                act.dma_start(lwf[:, :, :], LW.rearrange("(k p) n -> p k n", p=128)).then_inc(const_loaded, 16)
                act.dma_start(cc[:, :], eps_gin.rearrange("(a n) -> a n", a=1).to_broadcast([128, 1])).then_inc(const_loaded, 16)
                for j, v in enumerate((b1, g1, bt1)):
                    act.dma_start(b1c[:, j, :], v.rearrange("(m p) -> p m", p=128),
                                  allow_slow_non_contiguous=True).then_inc(const_loaded, 16)
                for j, v in enumerate((b2, g2, bt2)):
                    act.dma_start(rows2[:, j, :], v.rearrange("(a n) -> a n", a=1).to_broadcast([128, D])).then_inc(const_loaded, 16)
                act.wait_ge(idx_cleared, 5)
                load_edges(act, gsrc, src)
                load_edges(act, gdst, dst)
                load_edges(act, key_i[:, 0, :], dst)
                load_edges(act, key_i[:, 1, :], src)
                load_edges(act, wgt, ew)

                def evacuate(g, slot, use):
                    act.wait_ge(comb_ready, g + 1)
                    after(act, sums_added, (g - ERING + 1) * (16 * K))
                    nc.scalar.copy(sums[slot][:, :, :], comb[:, :].rearrange("p (k d) -> p k d", k=K)).then_inc(sums_ready, 1)

                over(act, 0, NG, ERING, evacuate)

            @block.gpsimd
            def _(pool):
                nc.gpsimd.memset(ident[:, :], 0.0).then_inc(pool_consts, 1)
                nc.gpsimd.memset(ones[:, :], 1.0)
                nc.gpsimd.memset(before[:, :, :], 1.0).then_inc(pool_consts, 1)
                pool.wait_ge(pool_consts, 2)
                nc.gpsimd.affine_select(out=ident[:, :], in_=ident[:, :], compare_op=ALU.not_equal, fill=1.0,
                                        base=0, pattern=[[-1, 128]], channel_multiplier=1)
                for k in range(K):
                    nc.gpsimd.affine_select(out=before[:, k, :], in_=before[:, k, :], compare_op=ALU.is_gt, fill=0.0,
                                            base=128 * k, pattern=[[-1, K * 128]], channel_multiplier=1)
                nc.gpsimd.iota(spare_i[:, :], pattern=[[128, K]], base=N + 1, channel_multiplier=1).then_inc(pool_consts, 1)
                pool.wait_ge(idx_loaded, 16 * IDX_LOADS)

                def gather(g, slot, use):
                    after(pool, comb_ready, g - ERING + 1)
                    pool.wait_ge(rows_picked, g + 1)
                    pool.sem_inc(pool_passed, 1)
                    for k in range(K):
                        pool.indirect_dma_start(rows_x[slot][:, k, :], None, x,
                                                IOA(ap=picked[slot][:, k:k + 1], axis=0)).then_inc(x_gathered[slot], 16)

                def add(g, slot, use):
                    pool.wait_ge(sums_ready, g + 1)
                    pool.wait_ge(table_zeroed, 16 * sh.NZ)
                    after(pool, sums_added, g * (16 * K))
                    pool.sem_inc(pool_passed, 1)
                    for k in range(K):
                        pool.indirect_dma_start(agg, IOA(ap=target[slot][:, k:k + 1], axis=0), sums[slot][:, k, :], None,
                                                compute_op=ALU.add).then_inc(sums_added, 16)

                def both(g, slot, use):
                    gather(g + 2, *back(slot, use, -2))
                    add(g, slot, use)

                for g in range(2):
                    gather(g, g, 0)
                over(pool, 0, NG - 2, ERING, both)
                for g in range(NG - 2, NG):
                    add(g, g % ERING, g // ERING)
                pool.wait_ge(sums_added, NG * 16 * K)

            @block.vector
            def _(dve):
                nc.vector.memset(zrows[:, :], 0.0).then_inc(consts_made, 1)
                nc.vector.memset(zeros16[:, :], 0.0)
                nc.vector.memset(epsc[:, :], EPS)
                nc.vector.memset(ones16[:, :], 1.0)
                nc.vector.memset(gsrc[:, :], 0).then_inc(idx_cleared, 1)
                nc.vector.memset(gdst[:, :], 0).then_inc(idx_cleared, 1)
                nc.vector.memset(key_i[:, 0, :], N).then_inc(idx_cleared, 1)
                nc.vector.memset(key_i[:, 1, :], N).then_inc(idx_cleared, 1)
                nc.vector.memset(wgt[:, :], 0.0).then_inc(idx_cleared, 1)
                dve.wait_ge(const_loaded, 160)
                nc.vector.tensor_scalar(cc[:, :], cc[:, :], 1.0, None, ALU.add)
                for full, hi, lo in ((w1f, w1h, w1l), (w2f, w2h, w2l)):
                    nc.vector.tensor_scalar(hi[:, :, :], full[:, :, :], WS, None, ALU.mult).then_inc(dve_c, 1)
                dve.wait_ge(dve_c, 2)
                for full, hi, lo in ((w1f, w1h, w1l), (w2f, w2h, w2l)):
                    nc.vector.scalar_tensor_tensor(out=lo[:, :, :], in0=full[:, :, :], scalar=WS, in1=hi[:, :, :],
                                                   op0=ALU.mult, op1=ALU.subtract)
                dve.wait_ge(lw_turned, 1)
                nc.vector.tensor_copy(lwt[:, :, :], lwp[:, :].rearrange("p (k n) -> p k n", k=KD))
                dve.wait_ge(pool_consts, 3)
                dve.wait_ge(idx_loaded, 16 * IDX_LOADS)
                nc.vector.tensor_copy(spare[:, :], spare_i[:, :])
                nc.vector.tensor_copy(kdst[:, :], key_i[:, 0, :])
                nc.vector.tensor_copy(ksrc[:, :], key_i[:, 1, :]).then_inc(dve_c, 1)
                dve.wait_ge(dve_c, 3)

                def count(g, j, keys, row):
                    for k in range(K):
                        last = nc.vector.scalar_tensor_tensor(
                            out=junk[:, k, :], in0=row[:, 0:K * 128], scalar=keys[:, bass.ds(g * K + k, 1)],
                            in1=before[:, k, :], op0=ALU.is_equal, op1=ALU.mult, accum_out=cnt[:, j, bass.ds(g * K + k, 1)])
                    last.then_inc(cnt_ready, 1)

                def targets(j, keys, to, done):
                    dve.wait_ge(cnt_ready, done)
                    nc.vector.tensor_tensor(diff[:, :].rearrange("p (g k) -> p g k", k=K),
                                            spare[:, :].unsqueeze(1).to_broadcast([128, NG, K]),
                                            keys[:, :].rearrange("p (g k) -> p g k", k=K), ALU.subtract).then_inc(cnt_ready, 1)
                    dve.wait_ge(cnt_ready, done + 1)
                    nc.vector.scalar_tensor_tensor(out=diff[:, :], in0=cnt[:, j, :], scalar=1.0, in1=diff[:, :],
                                                   op0=ALU.min, op1=ALU.mult).then_inc(cnt_ready, 1)
                    dve.wait_ge(cnt_ready, done + 2)
                    nc.vector.tensor_tensor(to[:, :], diff[:, :], keys[:, :], ALU.add).then_inc(cnt_ready, 1)
                    dve.wait_ge(cnt_ready, done + 3)

                def count_dst(g, slot, use):
                    dve.wait_ge(cnt_row, g + 1)
                    if not isinstance(g, int) or g < NG - 1:
                        spread_keys(g + 1, kdst, diag, cnt_spread)
                    after(dve, cnt_ready, g)
                    count(g, 0, kdst, keyrow[slot % 2])
                spread_keys(0, kdst, diag, cnt_spread)
                over(dve, 0, NG - 1, ERING, count_dst)
                count_dst(NG - 1, (NG - 1) % ERING, None)
                targets(0, kdst, tdst, NG)

                def pick(g, slot, use):
                    after(dve, comb_ready, g - ERING + 1)
                    nc.vector.tensor_copy(picked[slot][:, :], gsrc[:, group_columns(g)]).then_inc(rows_picked, 1)

                def group(g, slot, use, picks=True, more=True):
                    if picks:
                        pick(g + 2, *back(slot, use, -2))
                    dve.wait_ge(keyrow_ready, g + 1)
                    if more:
                        spread_keys(g + 1, kdst, diag, keys_spread)
                    after(dve, src_row, g)
                    spread_keys(g, ksrc, diag2, src_spread)
                    after(dve, sums_added, (g - ERING + 1) * (16 * K))
                    nc.vector.tensor_copy(target[slot][:, :], tdst[:, group_columns(g)])
                    after(dve, comb_ready, g - ERING + 1)
                    for k in range(K):
                        last = select_chunk(g, k, kdst, keyrow[slot % 2], sel[slot])
                    last.then_inc(sel_ready, 1)
                    dve.wait_ge(src_row, g + 1)
                    dve.wait_ge(cnt_ready, g + (NG + 3))
                    count(g, 1, ksrc, srcrow)

                for g in range(2):
                    pick(g, g, 0)
                spread_keys(0, kdst, diag, keys_spread)
                over(dve, 0, NG - 2, ERING, group)
                for g in range(NG - 2, NG):
                    group(g, g % ERING, g // ERING, False, g < NG - 1)
                targets(1, ksrc, tsrc, 2 * NG + 3)

            @block.tensor
            def _(pe):
                pe.wait_ge(pool_consts, 3)
                pe.wait_ge(const_loaded, 160)
                for i in range(KD):
                    for j in range(KD):
                        turned = nc.tensor.transpose(lwp[:, i * D + j * 128:i * D + j * 128 + 128],
                                                     lwf[:, j, i * 128:(i + 1) * 128], ident[:, :])
                turned.then_inc(lw_turned, 1)

                def count_row(g, slot, use):
                    pe.wait_ge(cnt_spread, g + 1)
                    after(pe, cnt_ready, g - 1)
                    key_row(g, keyrow[slot % 2], diag, cnt_row)
                over(pe, 0, NG, ERING, count_row)
                pe.wait_ge(cnt_ready, NG)

                def spread(g, slot):
                    pe.wait_ge(keys_spread, g + 1)
                    after(pe, sel_ready, g - 1)
                    key_row(g, keyrow[slot % 2], diag, keyrow_ready)

                def combine(g, slot, use):
                    pe.wait_ge(x_gathered[slot], (use + 1) * (16 * K))
                    pe.wait_ge(sel_ready, g + 1)
                    after(pe, sums_ready, g)
                    for k in range(K):
                        for j in range(K):
                            last = nc.tensor.matmul(comb[:, k * D:(k + 1) * D], sel[slot][:, j, k * 128:(k + 1) * 128],
                                                    rows_x[slot][:, j, :], start=(j == 0), stop=(j == K - 1))
                    last.then_inc(comb_ready, 1)

                def spread_src(g):
                    pe.wait_ge(src_spread, g + 1)
                    pe.wait_ge(cnt_ready, g + (NG + 3))
                    key_row(g, srcrow, diag2, src_row)

                def group(g, slot, use):
                    spread(g, slot)
                    spread_src(g)
                    combine(g - 1, *back(slot, use, 1))

                spread(0, 0)
                spread_src(0)
                over(pe, 1, NG, ERING, group)
                last = NG - 1
                combine(last, last % ERING, last // ERING)

        ph = next_ph
        ab = [sb(f"ab{s}", [128, G, D], f32, ph) for s in range(RING)]
        zb = [sb(f"zb{s}", [128, G, D], f32, ph) for s in range(RING)]
        zz = [sb(f"zz{s}", [128, G, 2 * D], f16, ph) for s in range(RING)]
        gram = sb("gram", [128, KD, D], f32, ph)
        mcol = sb("mcol", [128, 4], f32, ph)
        mrow = sb("mrow", [1, D], f32, ph)
        prod = sb("prod", [128, KD, H], f32, ph)
        st1 = sb("st1", [128, 6, KH], f32, ph)
        pg = [ps(f"pg{h}", 512, ph) for h in range(KD)]
        psum_z = ps("psum_z", 512, ph)
        pv = [ps(f"pv{h}", 512, ph) for h in range(KD)]
        pm = ps("pm", 512, ph)
        pst = ps("pst", 512, ph)

        a_loaded = [sem(f"a_loaded{s}") for s in range(RING)]
        z_ready = sem("z_ready")
        hi_ready = sem("hi_ready")
        lo_ready = sem("lo_ready")
        z_used = sem("z_used")
        gram_done = sem("gram_done")
        s1 = sem("s1_step")
        p1 = sem("p1_step")
        a1 = sem("a1_step")

        def all_blocks(eng, step, lo=0):
            over(eng, lo, NB, RING, lambda b, s, u: step(b, s, u, 128))
            step(NB, NB % RING, NB // RING, TP)

        def z_blocks(eng, step, lo=0):
            over(eng, lo, NB, XRING, lambda b, s, u: step(b, s, u, 128))
            step(NB, NB % XRING, NB // XRING, TP)

        with ph, nc.Block() as block:
            @block.sync
            def _(sp):
                def load(b, s, u, P):
                    if not isinstance(b, int) or b >= XRING:
                        sp.wait_ge(z_ready, b - XRING + 1)
                        sp.dma_start(xb[s][0:P].rearrange("p g d -> p (g d)"), block_of(xv, b, P)).then_inc(x_loaded[s], 16)
                    after(sp, z_ready, b - RING + 1)
                    sp.dma_start(ab[s % RING][0:P].rearrange("p g d -> p (g d)"), block_of(aggv, b, P)).then_inc(a_loaded[s % RING], 16)
                z_blocks(sp, load)

            @block.vector
            def _(dve):
                def z_block(b, s, u, P):
                    r = s % RING
                    dve.wait_ge(x_loaded[s], (u + 1) * 16)
                    dve.wait_ge(a_loaded[r], (u * (XRING // RING) + (s // RING + 1)) * 16)
                    after(dve, z_used, b - RING + 1)
                    nc.vector.scalar_tensor_tensor(out=zb[r][0:P], in0=xb[s][0:P], scalar=cc[0:P, :], in1=ab[r][0:P],
                                                   op0=ALU.mult, op1=ALU.add).then_inc(z_ready, 1)

                def low(b, s, P):
                    dve.wait_ge(hi_ready, b + 1)
                    nc.vector.tensor_tensor(zz[s][0:P, :, D:2 * D], zb[s][0:P], zz[s][0:P, :, 0:D], ALU.subtract).then_inc(lo_ready, 1)

                def step(b, s, u, P):
                    z_block(b, s, u, P)
                    low(b - 1, (s - 1) % RING, 128)
                z_block(0, 0, 0, 128)
                z_blocks(dve, step, 1)
                low(NB, NB % RING, TP)

                n = [0]

                def mark(ins):
                    n[0] += 1
                    ins.then_inc(s1, 1)
                    dve.wait_ge(s1, n[0])
                dve.wait_ge(gram_done, 1)
                mark(nc.vector.tensor_copy(mcol[:, 0:2], psum_z[:, 0:2]))
                mark(nc.vector.scalar_tensor_tensor(out=mcol[:, 0:2], in0=psum_z[:, 2:4], scalar=1.0, in1=mcol[:, 0:2],
                                                    op0=ALU.mult, op1=ALU.add))
                mark(nc.vector.tensor_scalar(mcol[:, 0:2], mcol[:, 0:2], 1.0 / N, None, ALU.mult))
                dve.wait_ge(p1, 1)
                mark(nc.vector.tensor_copy(mrow[0:1, :], pm[0:1, 0:D]))
                mark(nc.vector.tensor_copy(prod[:, 0, :], pg[0][:, :]))
                mark(nc.vector.tensor_copy(prod[:, 1, 0:D + 128], pg[1][:, 0:D + 128]))
                mark(nc.vector.scalar_tensor_tensor(out=gram[:, 0, :], in0=prod[:, 0, D:2 * D], scalar=2.0,
                                                    in1=prod[:, 0, 0:D], op0=ALU.mult, op1=ALU.add))
                mark(nc.vector.tensor_tensor(gram[:, 0, 128:D], gram[:, 0, 128:D], prod[:, 0, 128:D], ALU.add))
                mark(nc.vector.tensor_scalar(gram[:, 1, 0:128], prod[:, 1, 128:256], 2.0, None, ALU.mult))
                mark(nc.vector.scalar_tensor_tensor(out=gram[:, 1, 128:D], in0=prod[:, 1, 256:384], scalar=2.0,
                                                    in1=prod[:, 1, 0:128], op0=ALU.mult, op1=ALU.add))
                dve.wait_ge(p1, 2)
                mark(nc.vector.tensor_scalar(gram[:, :, :], gram[:, :, :], 1.0 / N, None, ALU.mult))
                mark(nc.vector.tensor_tensor(gram[:, 0, 0:128], gram[:, 0, 0:128], pm[:, 0:128], ALU.subtract))
                mark(nc.vector.scalar_tensor_tensor(out=gram[:, 0, 128:D], in0=pm[:, 128:D], scalar=-2.0,
                                                    in1=gram[:, 0, 128:D], op0=ALU.mult, op1=ALU.add))
                mark(nc.vector.tensor_tensor(gram[:, 1, 128:D], gram[:, 1, 128:D], pm[:, D + 128:2 * D], ALU.subtract))
                nc.vector.memset(st1[:, 5, :], 0.0).then_inc(a1, 1)
                dve.wait_ge(p1, 3)
                mark(nc.vector.tensor_tensor(prod[:, 0, :], pv[0][:, :], w1f[:, 0, :], ALU.mult))
                mark(nc.vector.tensor_tensor(prod[:, 1, :], pv[1][:, :], w1f[:, 1, :], ALU.mult))
                nc.vector.memset(st1[:, 5, :], 0.0).then_inc(a1, 1)
                dve.wait_ge(p1, 4)
                mark(nc.vector.tensor_scalar(st1[:, 0, :], pst[:, 0:KH], EPS, None, ALU.add))
                mark(nc.vector.tensor_tensor(st1[:, 1, :], pst[:, KH:2 * KH], b1c[:, 0, :], ALU.add))
                nc.vector.memset(st1[:, 5, :], 0.0).then_inc(a1, 1)
                dve.wait_ge(p1, 5)
                mark(nc.vector.reciprocal(st1[:, 3, :], st1[:, 2, :]))
                refine(mark, st1[:, 3, :], st1[:, 0, :], st1[:, 4, :])
                mark(nc.vector.tensor_tensor(st1[:, 3, :], st1[:, 3, :], b1c[:, 1, :], ALU.mult))
                mark(nc.vector.tensor_scalar(scale1[:, :], st1[:, 3, :], 1.0 / WS, None, ALU.mult))
                mark(nc.vector.tensor_tensor(st1[:, 4, :], b1c[:, 0, :], st1[:, 1, :], ALU.subtract))
                mark(nc.vector.tensor_tensor(st1[:, 4, :], st1[:, 4, :], st1[:, 3, :], ALU.mult))
                mark(nc.vector.tensor_tensor(bias1[:, :], st1[:, 4, :], b1c[:, 2, :], ALU.add))

            @block.scalar
            def _(act):
                def high(b, s, u, P):
                    act.wait_ge(z_ready, b + 1)
                    nc.scalar.copy(zz[s][0:P, :, 0:D], zb[s][0:P]).then_inc(hi_ready, 1)
                all_blocks(act, high)
                act.wait_ge(a1, 3)
                nc.scalar.activation(st1[:, 2, :], st1[:, 0, :], ACT.Sqrt).then_inc(p1, 1)

            @block.tensor
            def _(pe):
                for bank in (pg[0], pg[1], psum_z):
                    nc.tensor.matmul(bank[:, :], zeros16[:, 0:128], zeros16[:, :], start=True, stop=False)

                def gram_step(b, s, u, P):
                    pe.wait_ge(lo_ready, b + 1)
                    for g in range(G):
                        for h in range(KD):
                            w = zz[s][0:P, g, h * 128:(h + 1) * 128]
                            m = zz[s][0:P, g, h * 128:2 * D]
                            nc.tensor.matmul(pg[h][:, 0:2 * D - h * 128], w, m, start=False, stop=False, skip_group_check=True)
                            nc.tensor.matmul(psum_z[:, h:h + 1], w, ones16[0:P, :], start=False, stop=False, skip_group_check=True)
                        for h in range(KD):
                            last = nc.tensor.matmul(psum_z[:, 2 + h:3 + h], zz[s][0:P, g, D + h * 128:D + (h + 1) * 128],
                                                    ones16[0:P, :], start=False, stop=False, skip_group_check=True)
                    last.then_inc(z_used, 1)
                all_blocks(pe, gram_step)
                for bank in (pg[0], pg[1], psum_z):
                    last = nc.tensor.matmul(bank[:, :], zeros16[:, 0:128], zeros16[:, :], start=False, stop=True)
                last.then_inc(gram_done, 1)
                pe.wait_ge(s1, 3)
                for h in range(KD):
                    last = nc.tensor.transpose(pm[0:1, h * 128:(h + 1) * 128], mcol[:, h:h + 1], ident[:, :])
                last.then_inc(p1, 1)
                pe.wait_ge(s1, 4)
                for h in range(KD):
                    last = nc.tensor.matmul(pm[:, h * D:(h + 1) * D], mrow[0:1, h * 128:(h + 1) * 128], mrow[0:1, :], start=True, stop=True)
                last.then_inc(p1, 1)
                pe.wait_ge(a1, 1)
                for h in range(KD):
                    for k in range(KD):
                        last = nc.tensor.matmul(pv[h][:, :], gram[:, k, h * 128:(h + 1) * 128], w1f[:, k, :],
                                                start=(k == 0), stop=(k == KD - 1))
                last.then_inc(p1, 1)
                pe.wait_ge(a1, 2)
                for m in range(KH):
                    for k in range(KD):
                        nc.tensor.matmul(pst[:, m:m + 1], prod[:, k, m * 128:(m + 1) * 128], ones[:, 0:1], start=(k == 0), stop=(k == KD - 1))
                    for k in range(KD):
                        last = nc.tensor.matmul(pst[:, KH + m:KH + m + 1], w1f[:, k, m * 128:(m + 1) * 128], mcol[:, k:k + 1],
                                                start=(k == 0), stop=(k == KD - 1))
                last.then_inc(p1, 1)

        ph = ExitStack()
        xb = [sb(f"xc{s}", [128, G, D], f32, ph) for s in range(RING)]
        ab = [sb(f"ac{s}", [128, G, D], f32, ph) for s in range(2)]
        zb = sb("zc", [128, G, D], f32, ph)
        zh = sb("zh", [128, KD, 512], f16, ph)
        zl = sb("zl", [128, KD, 512], f16, ph)
        tf = sb("tf", [128, KH, 512], f32, ph)
        th = [sb(f"th{s}", [128, KH, 512], f16, ph) for s in range(2)]
        tl = [sb(f"tl{s}", [128, KH, 512], f16, ph) for s in range(2)]
        ub = [sb(f"ub{s}", [128, G, D], f32, ph) for s in range(2)]
        sq = sb("sq", [128, G, D], f32, ph)
        usum = sb("usum", [128, G, D], f32, ph)
        qsum = sb("qsum", [128, G, D], f32, ph)
        st2 = sb("st2", [128, 4, D], f32, ph)
        xs = [sb(f"xs{s}", [128, K, D], f32, ph) for s in range(2)]
        pzt = ps("pzt", KD * 512, ph)
        pt = [ps(f"pt{m}", 512, ph) for m in range(KH)]
        pc = ps("pc", G * D, ph)

        xc_loaded = [sem(f"xc_loaded{s}") for s in range(RING)]
        ac_loaded = [sem(f"ac_loaded{s}") for s in range(2)]
        zc_ready = sem("zc_ready")
        z_turned = sem("z_turned")
        zh_ready = sem("zh_ready")
        zl_ready = sem("zl_ready")
        t_ready = sem("t_ready")
        relu_done = sem("relu_done")
        tl_ready = sem("tl_ready")
        conv_ready = sem("conv_ready")
        u_ready = sem("u_ready")
        sq_ready = sem("sq_ready")
        usum_done = sem("usum_done")
        u_summed = sem("u_summed")
        u_stored = [sem(f"u_stored{s}") for s in range(2)]
        table2_zeroed = sem("table2_zeroed")
        xs_picked = sem("xs_picked")
        xs_gathered = [sem(f"xs_gathered{s}") for s in range(2)]
        xs_stored = [sem(f"xs_stored{s}") for s in range(2)]
        sums_cleared = sem("sums_cleared")
        s2 = sem("s2_step")
        p2 = sem("p2_step")

        with ph, nc.Block() as block:
            @block.sync
            def _(sp):
                def load(b, s, u, P):
                    prev = b - RING + 1
                    after(sp, u_ready, prev)
                    sp.dma_start(xb[s][0:P].rearrange("p g d -> p (g d)"), block_of(xv, b, P)).then_inc(xc_loaded[s], 16)
                    after(sp, zc_ready, b - 1)
                    sp.dma_start(ab[s % 2][0:P].rearrange("p g d -> p (g d)"), block_of(aggv, b, P)).then_inc(ac_loaded[s % 2], 16)

                def store_xs(g, slot, use):
                    sp.wait_ge(xs_gathered[slot], (use + 1) * (16 * K))
                    sp.dma_start(xdst[bass.ds(g, 1)].rearrange("a p r -> (a p) r"),
                                 xs[slot][:, :, :].rearrange("p k d -> p (k d)")).then_inc(xs_stored[slot], 16)

                def zero(z):
                    sp.dma_start(agg2_z[bass.ds(z, 1)].rearrange("a p r -> (a p) r"), zrows[:, :]).then_inc(table2_zeroed, 16)

                def step(b, s, u):
                    load(b, s, u, 128)
                    if s % 2 == 0:
                        store_xs(u * 2 + (s // 2 - 2), s // 2, u - 1)

                for s in range(RING):
                    load(s, s, 0, 128)
                n = (NB - RING) // RING
                per = sh.NZ // n
                for s in range(RING):
                    step(RING + s, s, 1)
                with sp.Fori(0, n - 1) as i:
                    for s in range(RING):
                        step(i * RING + (2 * RING + s), s, i + 2)
                    for z in range(per):
                        zero(i * per + z)
                for b in range(RING + n * RING, NB):
                    step(b, b % RING, b // RING)
                load(NB, NB % RING, NB // RING, TP)
                for g in range(-(-(NB - RING) // 2), NG):
                    store_xs(g, g % 2, g // 2)
                for z in range((n - 1) * per, sh.NZ):
                    zero(z)
                sp.wait_ge(table2_zeroed, 16 * sh.NZ)
                for g in (NG - 2, NG - 1):
                    sp.wait_ge(xs_stored[g % 2], (g // 2 + 1) * 16)

            @block.tensor
            def _(pe):
                def turn(b, s, P):
                    pe.wait_ge(zc_ready, b + 1)
                    after(pe, zl_ready, b)
                    after(pe, zh_ready, b)
                    for h in range(KD):
                        for g in range(G):
                            last = nc.tensor.transpose(pzt[:, h * 512 + g * P:h * 512 + g * P + P],
                                                       zb[0:P, g, h * 128:(h + 1) * 128], ident[0:P, 0:P])
                    last.then_inc(z_turned, 1)

                def first(b, P):
                    n = G * P
                    pe.wait_ge(zh_ready, b + 1)
                    pe.wait_ge(zl_ready, b + 1)
                    for m in range(KH):
                        after(pe, relu_done, b * KH - (KH - 1 - m))
                        c = slice(m * 128, (m + 1) * 128)
                        terms = [(w1h[:, k, c], zh[:, k, 0:n]) for k in range(KD)]
                        terms += [(w1h[:, k, c], zl[:, k, 0:n]) for k in range(KD)]
                        terms += [(w1l[:, k, c], zh[:, k, 0:n]) for k in range(KD)]
                        for j, (w, mv) in enumerate(terms):
                            last = nc.tensor.matmul(pt[m][:, 0:n], w, mv, start=(j == 0), stop=(j == len(terms) - 1))
                        last.then_inc(t_ready, 1)

                def second(b, s, P):
                    pe.wait_ge(tl_ready, (b + 1) * KH)
                    after(pe, u_ready, b)
                    for g in range(G):
                        c = slice(g * P, (g + 1) * P)
                        o = pc[0:P, g * D:(g + 1) * D]
                        for k in range(KH):
                            nc.tensor.matmul(o, th[s][:, k, c], w2h[:, k, :], start=(k == 0), stop=False)
                            nc.tensor.matmul(o, th[s][:, k, c], w2l[:, k, :], start=False, stop=False)
                            last = nc.tensor.matmul(o, tl[s][:, k, c], w2h[:, k, :], start=False, stop=(k == KH - 1))
                    last.then_inc(conv_ready, 1)

                def step(b, s, u, P=128, nextP=128):
                    first(b, P)
                    turn(b + 1, None, nextP)
                    second(b - 1, (s - 1) % 2, 128)
                turn(0, 0, 128)
                first(0, 128)
                turn(1, 1, 128)
                over(pe, 1, NB - 1, RING, step)
                step(NB - 1, (NB - 1) % RING, None, 128, TP)
                first(NB, TP)
                second(NB - 1, (NB - 1) % 2, 128)
                second(NB, NB % 2, TP)

                pe.wait_ge(s2, 1)
                for j, t in enumerate((usum, qsum)):
                    for g in range(G):
                        last = nc.tensor.matmul(pt[j][:, 0:D], ones[:, :], t[:, g, :], start=(g == 0), stop=(g == G - 1))
                last.then_inc(p2, 1)

            @block.scalar
            def _(act):
                def relus(b, s, u, P):
                    n = G * P
                    b2 = s % 2
                    for m in range(KH):
                        act.wait_ge(t_ready, b * KH + (m + 1))
                        after(act, tl_ready, b * KH - (KH - 1 - m))
                        nc.scalar.activation(tf[:, m, 0:n], pt[m][:, 0:n], ACT.Relu, bias=bias1[:, m:m + 1],
                                             scale=scale1[:, m:m + 1])
                        after(act, conv_ready, b - 1)
                        nc.scalar.activation(th[b2][:, m, 0:n], pt[m][:, 0:n], ACT.Relu, bias=bias1[:, m:m + 1],
                                             scale=scale1[:, m:m + 1]).then_inc(relu_done, 1)

                def high(b, P):
                    n = G * P
                    act.wait_ge(z_turned, b + 1)
                    after(act, t_ready, b * KH)
                    nc.scalar.copy(zh[:, :, 0:n], pzt[:, :].rearrange("p (k n) -> p k n", k=KD)[:, :, 0:n]).then_inc(zh_ready, 1)

                def square(b, s, P):
                    act.wait_ge(u_ready, b + 1)
                    after(act, u_summed, b)
                    nc.scalar.square(sq[0:P], ub[s][0:P]).then_inc(sq_ready, 1)
                    act.dma_start(block_of(uv, b, P), ub[s][0:P].rearrange("p g d -> p (g d)")).then_inc(u_stored[s], 16)

                def step(b, s, u, P=128, nextP=128):
                    relus(b, s, u, P)
                    high(b + 1, nextP)
                    square(b - 1, (s - 1) % 2, 128)
                high(0, 128)
                relus(0, 0, 0, 128)
                high(1, 128)
                over(act, 1, NB - 1, RING, step)
                step(NB - 1, (NB - 1) % RING, None, 128, TP)
                relus(NB, NB % RING, None, TP)
                square(NB - 1, (NB - 1) % 2, 128)
                square(NB, NB % 2, TP)
                for s in range(2):
                    act.wait_ge(u_stored[s], ((NB - s) // 2 + 1) * 16)
                act.wait_ge(s2, 6)
                nc.scalar.activation(st2[:, 3, :], st2[:, 2, :], ACT.Sqrt).then_inc(p2, 1)

            @block.vector
            def _(dve):
                def make_z(b, s, u, P):
                    dve.wait_ge(xc_loaded[s], (u + 1) * 16)
                    dve.wait_ge(ac_loaded[s % 2], (u * (RING // 2) + s // 2 + 1) * 16)
                    after(dve, z_turned, b)
                    nc.vector.scalar_tensor_tensor(out=zb[0:P], in0=xb[s][0:P], scalar=cc[0:P, :], in1=ab[s % 2][0:P],
                                                   op0=ALU.mult, op1=ALU.add).then_inc(zc_ready, 1)

                def low_t(b, s, P):
                    n = G * P
                    for m in range(KH):
                        dve.wait_ge(relu_done, b * KH + (m + 1))
                        after(dve, conv_ready, b - 1)
                        nc.vector.tensor_tensor(tl[s][:, m, 0:n], tf[:, m, 0:n], th[s][:, m, 0:n], ALU.subtract).then_inc(tl_ready, 1)

                def low_z(b, P):
                    n = G * P
                    dve.wait_ge(zh_ready, b + 1)
                    nc.vector.tensor_tensor(zl[:, :, 0:n], pzt[:, :].rearrange("p (k n) -> p k n", k=KD)[:, :, 0:n], zh[:, :, 0:n],
                                            ALU.subtract).then_inc(zl_ready, 1)

                def add_x(b, s4, s, P, use2):
                    dve.wait_ge(conv_ready, b + 1)
                    after(dve, sq_ready, b - 1)
                    after(dve, usum_done, b - 1)
                    after(dve, u_stored[s], use2 * 16)
                    nc.vector.scalar_tensor_tensor(out=ub[s][0:P], in0=pc[0:P, :].rearrange("p (g d) -> p g d", g=G), scalar=1.0 / WS,
                                                   in1=xb[s4][0:P], op0=ALU.mult, op1=ALU.add).then_inc(u_ready, 1)

                def use_of(s, u):
                    return u * (RING // 2) + (s - 1) // 2

                def step(b, s, u, P=128, nextP=128):
                    make_z(b + 1, (s + 1) % RING, u + (s + 1) // RING, nextP)
                    low_t(b, s % 2, P)
                    low_z(b + 1, nextP)
                    add_x(b - 1, (s - 1) % RING, (s - 1) % 2, 128, use_of(s, u))
                make_z(0, 0, 0, 128)
                low_z(0, 128)
                make_z(1, 1, 0, 128)
                low_t(0, 0, 128)
                low_z(1, 128)
                over(dve, 1, NB - 1, RING, step)
                step(NB - 1, (NB - 1) % RING, (NB - 1) // RING, 128, TP)
                low_t(NB, NB % 2, TP)
                add_x(NB - 1, (NB - 1) % RING, (NB - 1) % 2, 128, (NB - 1) // 2)
                add_x(NB, NB % RING, NB % 2, TP, NB // 2)

                n = [1]

                def mark(ins):
                    n[0] += 1
                    ins.then_inc(s2, 1)
                    dve.wait_ge(s2, n[0])
                dve.wait_ge(p2, 1)
                mark(nc.vector.tensor_scalar(st2[:, 0, :], pt[0][:, 0:D], 1.0 / N, None, ALU.mult))
                mark(nc.vector.tensor_scalar(st2[:, 1, :], pt[1][:, 0:D], 1.0 / N, None, ALU.mult))
                mark(nc.vector.tensor_tensor(st2[:, 2, :], st2[:, 0, :], st2[:, 0, :], ALU.mult))
                mark(nc.vector.tensor_tensor(st2[:, 2, :], st2[:, 1, :], st2[:, 2, :], ALU.subtract))
                mark(nc.vector.tensor_scalar(st2[:, 2, :], st2[:, 2, :], 0.0, EPS, ALU.max, ALU.add))
                mark(nc.vector.tensor_tensor(st2[:, 0, :], st2[:, 0, :], rows2[:, 0, :], ALU.add))
                dve.wait_ge(p2, 2)
                mark(nc.vector.reciprocal(st2[:, 1, :], st2[:, 3, :]))
                refine(mark, st2[:, 1, :], st2[:, 2, :], st2[:, 3, :])
                mark(nc.vector.tensor_tensor(scale2[:, :], st2[:, 1, :], rows2[:, 1, :], ALU.mult))
                mark(nc.vector.tensor_tensor(st2[:, 2, :], rows2[:, 0, :], st2[:, 0, :], ALU.subtract))
                mark(nc.vector.tensor_tensor(st2[:, 2, :], st2[:, 2, :], scale2[:, :], ALU.mult))
                mark(nc.vector.tensor_tensor(bias2[:, :], st2[:, 2, :], rows2[:, 2, :], ALU.add))

            @block.gpsimd
            def _(pool):
                nc.gpsimd.memset(usum[:, :, :], 0.0)
                nc.gpsimd.memset(qsum[:, :, :], 0.0).then_inc(sums_cleared, 1)
                pool.wait_ge(sums_cleared, 1)

                def summed(b, s, P):
                    pool.wait_ge(u_ready, b + 1)
                    after(pool, usum_done, b)
                    nc.gpsimd.tensor_tensor(usum[0:P], usum[0:P], ub[s][0:P], ALU.add).then_inc(usum_done, 1)
                    pool.wait_ge(sq_ready, b + 1)
                    after(pool, u_summed, b)
                    nc.gpsimd.tensor_tensor(qsum[0:P], qsum[0:P], sq[0:P], ALU.add).then_inc(u_summed, 1)

                def gather_xs(g, slot, use):
                    after(pool, xs_stored[slot], use * 16)
                    pool.sem_inc(pool_passed, 1)
                    nc.gpsimd.tensor_copy(picked[slot][:, :], gdst[:, group_columns(g)]).then_inc(xs_picked, 1)
                    pool.wait_ge(xs_picked, g + 1)
                    pool.sem_inc(pool_passed, 1)
                    for k in range(K):
                        pool.indirect_dma_start(xs[slot][:, k, :], None, x,
                                                IOA(ap=picked[slot][:, k:k + 1], axis=0)).then_inc(xs_gathered[slot], 16)

                def step(b, s, u):
                    if s % 2 == 0:
                        gather_xs(u * 2 + s // 2, s // 2, u)
                    summed(b, s % 2, 128)
                over(pool, 0, NB, RING, step)
                for g in range(-(-NB // 2), NG):
                    gather_xs(g, g % 2, g // 2)
                summed(NB, NB % 2, TP)
                pool.wait_ge(u_summed, NB + 1)
                pool.sem_inc(s2, 1)

        next_ph = ExitStack()
        un = [sb(f"un{s}", [128, G, D], f32, next_ph) for s in range(XRING)]
        xn = [sb(f"xn{s}", [128, G, D], f32, next_ph) for s in range(XRING)]
        n_loaded = [sem(f"n_loaded{s}") for s in range(XRING)]
        ph = ExitStack()
        rx = [sb(f"rx{s}", [128, K, D], f32, ph) for s in range(ERING)]
        ru = [sb(f"ru{s}", [128, K, D], f32, ph) for s in range(ERING)]
        msg = [sb(f"msg{s}", [128, K, D], f32, ph) for s in range(ERING)]
        sums = [sb(f"msums{s}", [128, K, D], f32, ph) for s in range(ERING)]
        turned = [sb(f"turned{s}", [128, KD, K * 128], f32, ph) for s in range(2)]
        sel = [sb(f"msel{s}", [128, K, K * 128], f32, ph) for s in range(ERING)]
        diag = [sb(f"mdiag{s}", [128, K, 128], f32, ph) for s in range(2)]
        target = [sb(f"mtarget{s}", [128, K], i32, ph) for s in range(ERING)]
        stat = sb("mstat", [128, K, 6], f32, ph)
        mv = sb("mmv", [128, K, 2], f32, ph)
        mrs = sb("mrs", [128, 4, K], f32, ph)
        keyrow = [ps(f"mkeyrow{s}", 512, ph) for s in range(2)]
        pturn = [ps(f"pturn{s}", KD * K * 128, ph) for s in range(2)]
        comb = [ps(f"mcomb{s}", K * D, ph) for s in range(2)]

        mx_loaded = [sem(f"mx_loaded{s}") for s in range(ERING)]
        mu_gathered = [sem(f"mu_gathered{s}") for s in range(ERING)]
        m_picked = sem("m_picked")
        m_spread = sem("m_spread")
        m_row = sem("m_row")
        m_sel = sem("m_sel")
        m_target = sem("m_target")
        m_a = sem("m_scaled")
        m_b = sem("m_shifted")
        m_y = sem("m_y")
        m_s = sem("m_stats")
        m_mv = sem("m_mv")
        m_sd = sem("m_sd")
        m_small = sem("m_small")
        m_rstd = sem("m_rstd")
        m_msg = sem("m_msg")
        m_pt = sem("m_pturn")
        m_turned = sem("m_turned")
        m_comb = sem("m_comb")
        m_sums = sem("m_sums")
        m_added = sem("m_added")

        with ph, nc.Block() as block:
            @block.sync
            def _(sp):
                def load(g, slot, use):
                    after(sp, m_msg, g - ERING + 1)
                    sp.dma_start(rx[slot][:, :, :].rearrange("p k d -> p (k d)"),
                                 xdst[bass.ds(g, 1)].rearrange("a p r -> (a p) r")).then_inc(mx_loaded[slot], 16)
                first = max(0, NG - 3 * XRING)
                over(sp, 0, first, ERING, load)
                for s in range(XRING):
                    for g in range(first + 3 * s, min(first + 3 * s + 3, NG)):
                        load(g, g % ERING, g // ERING)
                    for to, of in ((un, uv), (xn, xv)):
                        sp.dma_start(to[s][:, :, :].rearrange("p g d -> p (g d)"), block_of(of, s, 128)).then_inc(n_loaded[s], 16)
                for g in range(first + 3 * XRING, NG):
                    load(g, g % ERING, g // ERING)

            @block.gpsimd
            def _(pool):
                def gather(g, slot, use):
                    pool.wait_ge(m_picked, g + 1)
                    pool.sem_inc(pool_passed, 1)
                    for k in range(K):
                        pool.indirect_dma_start(ru[slot][:, k, :], None, ubuf,
                                                IOA(ap=picked[slot][:, k:k + 1], axis=0)).then_inc(mu_gathered[slot], 16)

                def add(g, slot, use):
                    pool.wait_ge(m_sums, g + 1)
                    pool.wait_ge(m_target, g + 1)
                    after(pool, m_added, g * (16 * K))
                    pool.sem_inc(pool_passed, 1)
                    for k in range(K):
                        pool.indirect_dma_start(agg2, IOA(ap=target[slot][:, k:k + 1], axis=0), sums[slot][:, k, :], None,
                                                compute_op=ALU.add).then_inc(m_added, 16)

                def both(g, slot, use):
                    gather(g + 2, *back(slot, use, -2))
                    add(g - 4, slot, use - 1)

                for g in range(6):
                    gather(g, g % ERING, g // ERING)
                over(pool, 4, NG - 2, ERING, both)
                for g in range(NG - 6, NG):
                    add(g, g % ERING, g // ERING)
                pool.wait_ge(m_added, NG * 16 * K)

            @block.vector
            def _(dve):
                sc = scale2[:, :].unsqueeze(1).to_broadcast([128, K, D])
                bi = bias2[:, :].unsqueeze(1).to_broadcast([128, K, D])

                def pick(g, slot):
                    after(dve, m_y, g - ERING + 1)
                    nc.vector.tensor_copy(picked[slot][:, :], gdst[:, group_columns(g)]).then_inc(m_picked, 1)

                def scales(g):
                    r, t = mrs[:, 1, :], mrs[:, 3, :]

                    def invert():
                        dve.wait_ge(m_sd, g + 1)
                        after(dve, m_msg, g)
                        nc.vector.reciprocal(r, mrs[:, 0, :]).then_inc(m_small, 1)

                    def newton1():
                        dve.wait_ge(m_small, g * 5 + 1)
                        nc.vector.scalar_tensor_tensor(out=t, in0=mv[:, :, 1], scalar=EPS, in1=r, op0=ALU.add, op1=ALU.mult).then_inc(m_small, 1)

                    def newton2():
                        dve.wait_ge(m_small, g * 5 + 2)
                        nc.vector.scalar_tensor_tensor(out=t, in0=t, scalar=-0.5, in1=r, op0=ALU.mult, op1=ALU.mult).then_inc(m_small, 1)

                    def newton3():
                        dve.wait_ge(m_small, g * 5 + 3)
                        nc.vector.scalar_tensor_tensor(out=r, in0=t, scalar=1.5, in1=r, op0=ALU.add, op1=ALU.mult).then_inc(m_small, 1)

                    def weigh():
                        dve.wait_ge(m_small, g * 5 + 4)
                        nc.vector.tensor_tensor(r, r, wgt[:, group_columns(g)], ALU.mult).then_inc(m_small, 1)

                    def shift():
                        dve.wait_ge(m_small, g * 5 + 5)
                        nc.vector.scalar_tensor_tensor(out=mrs[:, 2, :], in0=mv[:, :, 0], scalar=-1.0, in1=r,
                                                       op0=ALU.mult, op1=ALU.mult).then_inc(m_rstd, 1)
                    return [invert, newton1, newton2, newton3, weigh, shift]

                def aim(g, slot, use):
                    after(dve, m_added, (g - ERING + 1) * (16 * K))
                    nc.vector.tensor_copy(target[slot][:, :], tsrc[:, group_columns(g)]).then_inc(m_target, 1)

                def group(g, slot, use, small, picks=True, aims=True):
                    def between():
                        if small:
                            small.pop(0)()
                    dve.wait_ge(mu_gathered[slot], (use + 1) * (16 * K))
                    nc.vector.tensor_tensor(ru[slot][:, :, :], ru[slot][:, :, :], sc, ALU.mult).then_inc(m_a, 1)
                    between()
                    between()
                    dve.wait_ge(m_a, g + 1)
                    nc.vector.tensor_tensor(ru[slot][:, :, :], ru[slot][:, :, :], bi, ALU.add).then_inc(m_b, 1)
                    between()
                    if picks:
                        pick(g + 3, (slot + 3) % ERING)
                    dve.wait_ge(m_row, g + 1)
                    after(dve, m_pt, g - ERING + 1)
                    for k in range(K):
                        last = select_chunk(g, k, ksrc, keyrow[slot % 2], sel[slot])
                    last.then_inc(m_sel, 1)
                    between()
                    dve.wait_ge(m_b, g + 1)
                    dve.wait_ge(mx_loaded[slot], (use + 1) * 16)
                    nc.vector.scalar_tensor_tensor(out=rx[slot][:, :, :], in0=ru[slot][:, :, :], scalar=0.0, in1=rx[slot][:, :, :],
                                                   op0=ALU.max, op1=ALU.add).then_inc(m_y, 1)
                    between()
                    dve.wait_ge(m_y, g + 1)
                    for k in range(K):
                        last = nc.vector.bn_stats(stat[:, k, :], rx[slot][:, k, :])
                        between()
                    last.then_inc(m_s, 1)
                    if aims:
                        aim(g - 2, *back(slot, use, 2))
                    dve.wait_ge(m_s, g + 1)
                    dve.sem_inc(dve_passed, 1)
                    for k in range(K):
                        last = nc.vector.bn_aggr(mv[:, k, :], stat[:, k, :])
                    last.then_inc(m_mv, 1)

                for g in range(3):
                    pick(g, g)
                group(0, 0, 0, [], aims=False)
                group(1, 1, 0, scales(0), aims=False)
                over(dve, 2, NG - 3, ERING, lambda g, slot, use: group(g, slot, use, scales(g - 1)))
                for g in range(NG - 3, NG):
                    group(g, g % ERING, g // ERING, scales(g - 1), False)
                for small in scales(NG - 1):
                    small()
                for g in (NG - 2, NG - 1):
                    aim(g, g % ERING, g // ERING)

            @block.scalar
            def _(act):
                def spread(g, slot):
                    after(act, m_row, g - 1)
                    for k in range(K):
                        last = nc.scalar.activation(diag[slot % 2][:, k, :], ident[:, :], ACT.Identity,
                                                    scale=ksrc[:, bass.ds(g * K + k, 1)])
                    last.then_inc(m_spread, 1)

                def deviation(g):
                    act.wait_ge(m_mv, g + 1)
                    nc.scalar.activation(mrs[:, 0, :], mv[:, :, 1], ACT.Sqrt, bias=epsc[:, :]).then_inc(m_sd, 1)

                def message(g, slot):
                    act.wait_ge(m_rstd, g + 1)
                    after(act, m_pt, g - ERING + 1)
                    for k in range(K):
                        last = nc.scalar.activation(msg[slot][:, k, :], rx[slot][:, k, :], ACT.Identity,
                                                    bias=mrs[:, 2, k:k + 1], scale=mrs[:, 1, k:k + 1])
                    last.then_inc(m_msg, 1)

                def turn(g, slot):
                    act.wait_ge(m_pt, g + 1)
                    after(act, m_comb, g - 1)
                    nc.scalar.copy(turned[slot % 2][:, :, :],
                                   pturn[slot % 2][:, :].rearrange("p (h j) -> p h j", h=KD)).then_inc(m_turned, 1)

                def evacuate(g, slot, use):
                    act.wait_ge(m_comb, g + 1)
                    after(act, m_added, (g - ERING + 1) * (16 * K))
                    nc.scalar.copy(sums[slot][:, :, :], comb[slot % 2][:, :].rearrange("p (k d) -> p k d", k=K)).then_inc(m_sums, 1)

                def step(g, slot, use, more=True):
                    turn(g - 2, (slot - 2) % ERING)
                    message(g - 1, (slot - 1) % ERING)
                    deviation(g)
                    if more:
                        spread(g + 2, slot)
                    evacuate(g - 3, *back(slot, use, 3))
                for g in range(3):
                    spread(g, g)
                deviation(0)
                message(0, 0)
                deviation(1)
                spread(3, 3)
                turn(0, 0)
                message(1, 1)
                deviation(2)
                spread(4, 4)
                over(act, 3, NG - 2, ERING, step)
                for g in (NG - 2, NG - 1):
                    step(g, g % ERING, g // ERING, False)
                turn(NG - 2, NG - 2)
                message(NG - 1, (NG - 1) % ERING)
                evacuate(NG - 3, (NG - 3) % ERING, (NG - 3) // ERING)
                turn(NG - 1, NG - 1)
                for g in (NG - 2, NG - 1):
                    evacuate(g, g % ERING, g // ERING)

            @block.tensor
            def _(pe):
                def spread(g, slot):
                    pe.wait_ge(m_spread, g + 1)
                    after(pe, m_sel, g - 1)
                    key_row(g, keyrow[slot % 2], diag[slot % 2], m_row)

                def turn(g, slot):
                    pe.wait_ge(m_sel, g + 1)
                    pe.wait_ge(m_msg, g + 1)
                    after(pe, m_turned, g - 1)
                    for h in range(KD):
                        for j in range(K):
                            last = nc.tensor.matmul(pturn[slot % 2][:, h * K * 128:(h + 1) * K * 128],
                                                    msg[slot][:, j, h * 128:(h + 1) * 128],
                                                    sel[slot][:, j, :], start=(j == 0), stop=(j == K - 1))
                    last.then_inc(m_pt, 1)

                def combine(g, slot):
                    pe.wait_ge(m_turned, g + 1)
                    after(pe, m_sums, g - 1)
                    for k in range(K):
                        for h in range(KD):
                            last = nc.tensor.matmul(comb[slot % 2][:, k * D:(k + 1) * D], turned[slot % 2][:, h, k * 128:(k + 1) * 128],
                                                    lwt[:, h, :], start=(h == 0), stop=(h == KD - 1))
                    last.then_inc(m_comb, 1)

                def group(g, slot, use, more=True):
                    turn(g - 2, (slot - 2) % ERING)
                    if more:
                        spread(g + 1, slot + 1)
                    combine(g - 3, (slot - 3) % ERING)
                for g in range(3):
                    spread(g, g)
                spread(3, 3)
                turn(0, 0)
                over(pe, 3, NG - 1, ERING, group)
                group(NG - 1, (NG - 1) % ERING, None, False)
                turn(NG - 2, (NG - 2) % ERING)
                combine(NG - 3, (NG - 3) % ERING)
                turn(NG - 1, (NG - 1) % ERING)
                combine(NG - 2, (NG - 2) % ERING)
                combine(NG - 1, (NG - 1) % ERING)

        ph = next_ph
        an = [sb(f"an{s}", [128, G, D], f32, ph) for s in range(NRING)]
        on = [sb(f"on{s}", [128, G, D], f32, ph) for s in range(2)]
        nst = sb("nst", [128, 2, G, 6], f32, ph)
        nmv = sb("nmv", [128, 2, G, 2], f32, ph)
        nsd = sb("nsd", [128, 2, G], f32, ph)
        nrs = sb("nrs", [128, 2, 3, G], f32, ph)
        pv2 = [ps(f"pv2{s}", G * D, ph) for s in range(3)]
        an_loaded = [sem(f"an_loaded{s}") for s in range(NRING)]
        n_scaled = sem("n_scaled")
        n_shift = sem("n_shifted")
        n_y = sem("n_y")
        n_s = [sem(f"n_stats{j}") for j in range(2)]
        n_mv = [sem(f"n_mv{j}") for j in range(2)]
        n_sd = [sem(f"n_sd{j}") for j in range(2)]
        n_small = [sem(f"n_small{j}") for j in range(2)]
        n_rstd = [sem(f"n_rstd{j}") for j in range(2)]
        n_x1 = sem("n_x1")
        n_v = sem("n_v")
        n_out = sem("n_out")
        n_stored = [sem(f"n_stored{s}") for s in range(2)]

        def norm_blocks(eng, step, lo=0):
            over(eng, lo, NB, XRING, lambda b, s, u: step(b, s, u, 128))
            step(NB, NB % XRING, NB // XRING, TP)

        with ph, nc.Block() as block:
            @block.sync
            def _(sp):
                def load(b, s, u, P):
                    if not isinstance(b, int) or b >= XRING:
                        sp.wait_ge(n_v, b - XRING + 1)
                        for to, of in ((un, uv), (xn, xv)):
                            sp.dma_start(to[s][0:P].rearrange("p g d -> p (g d)"), block_of(of, b, P)).then_inc(n_loaded[s], 16)
                    after(sp, n_v, b - NRING + 1)
                    sp.dma_start(an[s % NRING][0:P].rearrange("p g d -> p (g d)"), block_of(agg2v, b, P)).then_inc(an_loaded[s % NRING], 16)
                norm_blocks(sp, load)

            @block.gpsimd
            def _(pool):
                sc = scale2[:, :].unsqueeze(1).to_broadcast([128, G, D])
                bi = bias2[:, :].unsqueeze(1).to_broadcast([128, G, D])

                def bn(b, s, u, P):
                    pool.wait_ge(n_loaded[s], (u + 1) * 32)
                    nc.gpsimd.tensor_tensor(un[s][0:P], un[s][0:P], sc[0:P], ALU.mult).then_inc(n_scaled, 1)
                    pool.wait_ge(n_scaled, b + 1)
                    nc.gpsimd.tensor_tensor(un[s][0:P], un[s][0:P], bi[0:P], ALU.add).then_inc(n_shift, 1)
                norm_blocks(pool, bn)

            @block.tensor
            def _(pe):
                def v(b, s, u, P):
                    pe.wait_ge(n_x1, b + 1)
                    pe.wait_ge(an_loaded[s % NRING], (u * (XRING // NRING) + (s // NRING + 1)) * 16)
                    after(pe, n_out, b - 2)
                    for g in range(G):
                        o = pv2[s % 3][0:P, g * D:(g + 1) * D]
                        nc.tensor.matmul(o, ident[0:P, 0:P], an[s % NRING][0:P, g, :], start=True, stop=False)
                        last = nc.tensor.matmul(o, ident[0:P, 0:P], xn[s][0:P, g, :], start=False, stop=True)
                    last.then_inc(n_v, 1)
                norm_blocks(pe, v)

            @block.vector
            def _(dve):
                def inverse(b, j, P):
                    r, m, t = (nrs[0:P, j, i, :] for i in range(3))

                    def first():
                        dve.wait_ge(n_sd[j], b + 1)
                        after(dve, n_x1 if j == 0 else n_out, b)
                        nc.vector.reciprocal(r, nsd[0:P, j, :]).then_inc(n_small[j], 1)

                    def second():
                        dve.wait_ge(n_small[j], b * 4 + 1)
                        nc.vector.scalar_tensor_tensor(out=t, in0=nmv[0:P, j, :, 1], scalar=EPS, in1=r,
                                                       op0=ALU.add, op1=ALU.mult).then_inc(n_small[j], 1)

                    def third():
                        dve.wait_ge(n_small[j], b * 4 + 2)
                        nc.vector.scalar_tensor_tensor(out=t, in0=t, scalar=-0.5, in1=r,
                                                       op0=ALU.mult, op1=ALU.mult).then_inc(n_small[j], 1)

                    def fourth():
                        dve.wait_ge(n_small[j], b * 4 + 3)
                        nc.vector.scalar_tensor_tensor(out=r, in0=t, scalar=1.5, in1=r,
                                                       op0=ALU.add, op1=ALU.mult).then_inc(n_small[j], 1)

                    def fifth():
                        dve.wait_ge(n_small[j], b * 4 + 4)
                        nc.vector.scalar_tensor_tensor(out=m, in0=nmv[0:P, j, :, 0], scalar=-1.0, in1=r,
                                                       op0=ALU.mult, op1=ALU.mult).then_inc(n_rstd[j], 1)
                    return [first, second, third, fourth, fifth]

                def add_x(b, s, P):
                    dve.wait_ge(n_shift, b + 1)
                    nc.vector.scalar_tensor_tensor(out=xn[s][0:P], in0=un[s][0:P], scalar=0.0, in1=xn[s][0:P],
                                                   op0=ALU.max, op1=ALU.add).then_inc(n_y, 1)

                def stats(b, j, tile, P, between):
                    for g in range(G):
                        last = nc.vector.bn_stats(nst[0:P, j, g, :], tile(g))
                        if between:
                            between.pop(0)()
                    last.then_inc(n_s[j], 1)

                def gather_stats(b, j, P):
                    dve.wait_ge(n_s[j], b + 1)
                    dve.sem_inc(dve_passed, 1)
                    for g in range(G):
                        last = nc.vector.bn_aggr(nmv[0:P, j, g, :], nst[0:P, j, g, :])
                    last.then_inc(n_mv[j], 1)

                def y_stats(b, s, P, between):
                    dve.wait_ge(n_y, b + 1)
                    stats(b, 0, lambda g: xn[s][0:P, g, :], P, between)

                def v_stats(b, s, P, between):
                    dve.wait_ge(n_v, b + 1)
                    stats(b, 1, lambda g: pv2[s % 3][0:P, g * D:(g + 1) * D], P, between)

                def step(b, s, P):
                    small = inverse(b - 3, 1, 128)
                    add_x(b, s, P)
                    small.pop(0)()
                    y_stats(b, s, P, small)
                    gather_stats(b, 0, P)
                    small = inverse(b, 0, P)
                    v_stats(b - 2, (s - 2) % XRING, 128, small)
                    small.pop(0)()
                    gather_stats(b - 2, 1, 128)

                def all_of(steps):
                    for small in steps:
                        small()

                for b in range(3):
                    add_x(b, b, 128)
                    y_stats(b, b, 128, [])
                    gather_stats(b, 0, 128)
                    all_of(inverse(b, 0, 128))
                    if b == 2:
                        v_stats(0, 0, 128, [])
                        gather_stats(0, 1, 128)
                over(dve, 3, NB, XRING, lambda b, s, u: step(b, s, 128))
                step(NB, NB % XRING, TP)
                all_of(inverse(NB - 2, 1, 128))
                for b, P in ((NB - 1, 128), (NB, TP)):
                    v_stats(b, b % XRING, P, [])
                    gather_stats(b, 1, P)
                    all_of(inverse(b, 1, P))

            @block.scalar
            def _(act):
                def norm(to, tile, j, P, done):
                    for g in range(G):
                        last = nc.scalar.activation(to[0:P, g, :], tile(g), ACT.Identity,
                                                    bias=nrs[0:P, j, 1, g:g + 1], scale=nrs[0:P, j, 0, g:g + 1])
                    last.then_inc(done, 1)

                def deviation(b, j, P):
                    act.wait_ge(n_mv[j], b + 1)
                    nc.scalar.activation(nsd[0:P, j, :], nmv[0:P, j, :, 1], ACT.Sqrt, bias=epsc[0:P, :]).then_inc(n_sd[j], 1)

                def x1(b, s, P):
                    act.wait_ge(n_rstd[0], b + 1)
                    norm(xn[s], lambda g: xn[s][0:P, g, :], 0, P, n_x1)

                def result(b, s, u, P):
                    act.wait_ge(n_rstd[1], b + 1)
                    after(act, n_stored[s % 2], u * (XRING // 2 * 16) + (s // 2 * 16))
                    norm(on[s % 2], lambda g: pv2[s % 3][0:P, g * D:(g + 1) * D], 1, P, n_out)
                    act.wait_ge(n_out, b + 1)
                    act.dma_start(block_of(outv, b, P), on[s % 2][0:P].rearrange("p g d -> p (g d)")).then_inc(n_stored[s % 2], 16)

                def step(b, s, u, P):
                    x1(b - 1, (s - 1) % XRING, 128)
                    deviation(b, 0, P)
                    result(b - 3, (s - 3) % XRING, u + (s - 3) // XRING, 128)
                    deviation(b - 2, 1, 128)
                deviation(0, 0, 128)
                x1(0, 0, 128)
                deviation(1, 0, 128)
                x1(1, 1, 128)
                deviation(2, 0, 128)
                deviation(0, 1, 128)
                over(act, 3, NB, XRING, lambda b, s, u: step(b, s, u, 128))
                step(NB, NB % XRING, NB // XRING, TP)
                x1(NB, NB % XRING, TP)
                result(NB - 2, (NB - 2) % XRING, (NB - 2) // XRING, 128)
                for b, P in ((NB - 1, 128), (NB, TP)):
                    deviation(b, 1, P)
                    result(b, b % XRING, b // XRING, P)
                for s in range(2):
                    act.wait_ge(n_stored[s], ((NB - s) // 2 + 1) * 16)


_INS = ['x', 'src', 'dst', 'edge_weight', 'L0_gnn_W1', 'L0_gnn_b1', 'L0_gnn_g1', 'L0_gnn_bt1', 'L0_gnn_W2', 'L0_gnn_b2',
        'L0_gnn_g2', 'L0_gnn_bt2', 'L0_gnn_eps_gin', 'L1_gnn_W']


def kernel(**inputs):
    import numpy as _np
    import concourse.bacc as _bacc
    from concourse import mybir as _mybir
    from concourse.bass_utils import run_bass_kernel_spmd as _run

    nc = _bacc.Bacc("TRN2", target_bir_lowering=False, num_devices=1)
    arrays, args = {}, []
    for name in _INS:
        a = _np.ascontiguousarray(inputs[name])
        a = a.reshape(a.shape or (1,))
        arrays[f"in_{name}"] = a
        args.append(nc.dram_tensor(f"in_{name}", a.shape, _mybir.dt.from_np(a.dtype), kind="ExternalInput").ap())
    shape = _np.shape(inputs['x'])
    o = nc.dram_tensor("out_dram", shape, _mybir.dt.float32, kind="ExternalOutput").ap()
    gnn(nc, *args, o)
    r = _run(nc, [arrays], core_ids=[0])
    return r.results[0]["out_dram"]
```
